# Optimizing a Trainium2 kernel written in Bass

```python
import numpy as np
import jax
import jax.numpy as jnp

def _softmax(x, axis=-1):
    return jax.nn.softmax(x, axis=axis)

def _gelu(x):
    return jax.nn.gelu(x, approximate=True)

def _silu(x):
    return jax.nn.silu(x)

def _sigmoid(x):
    return jax.nn.sigmoid(x)

def _layernorm(x, axis=-1, eps=1e-05):
    m = jnp.mean(x, axis=axis, keepdims=True)
    v = jnp.var(x, axis=axis, keepdims=True)
    return (x - m) / jnp.sqrt(v + eps)

def _scatter_add(tgt, idx, src, axis=0):
    return tgt.at[idx].add(src)

def _segment_sum(src, seg, n):
    return jax.ops.segment_sum(src, seg, n)
kernel_name = 'mk_sandwich_d1_jaxref_r8_130701'

def setup_inputs(seed: int=0):
    np.random.seed(seed)
    _w = jnp.asarray

    def _L0_attn_setup():
        import jax, jax.numpy as jnp
        import numpy as np
        H, D, CR, SEL_K = (8, 64, 32, 16)
        ROPE_DIM, THETA, WINDOW, GROUPS = (32, 10000.0, 64, 2)
        INTER, HID, QC = (64, 128, 32)
        NEG = -1e+30

        def _rope_cache(t):
            half = ROPE_DIM // 2
            inv = 1.0 / THETA ** (jnp.arange(half, dtype=jnp.float32) * 2.0 / ROPE_DIM)
            ang = jnp.arange(t, dtype=jnp.float32)[:, None] * inv[None, :]
            return (jnp.cos(ang), jnp.sin(ang))

        def _apply_partial_rope(x, cos, sin):
            half = ROPE_DIM // 2
            x1, x2, rest = (x[..., :half], x[..., half:ROPE_DIM], x[..., ROPE_DIM:])
            return jnp.concatenate([x1 * cos - x2 * sin, x1 * sin + x2 * cos, rest], -1)

        def _rmsnorm(x, g, eps=1e-06):
            return x * jax.lax.rsqrt(jnp.mean(x * x, -1, keepdims=True) + eps) * g
        key = jax.random.key(seed)
        ks = jax.random.split(key, 9)
        f = lambda k, shp, s: jax.random.normal(k, shp, jnp.float32) * s
        return {'h': f(ks[0], (1, 256, HID), 1.0), 'w_qc': f(ks[1], (HID, QC), QC ** (-0.5)), 'w_qup': f(ks[2], (QC, H * D), (H * D) ** (-0.5)), 'w_k': f(ks[3], (HID, D), HID ** (-0.5)), 'w_v': f(ks[4], (HID, D), HID ** (-0.5)), 'g_qnorm': jnp.ones((D,), jnp.float32), 'g_knorm': jnp.ones((D,), jnp.float32), 'w_gate': f(ks[5], (D, 3), 0.05), 'b_gate': jnp.zeros((3,), jnp.float32), 'sink_logit': f(ks[6], (H,), 0.1), 'w_out_group': f(ks[7], (GROUPS, H // GROUPS * D, INTER), 0.05), 'w_out': f(ks[8], (GROUPS * INTER, HID), 0.03)}
    _L0_attn_in = _L0_attn_setup()

    def _L0_ffn_setup():
        import jax, jax.numpy as jnp
        import numpy as np
        B, S, D = (2, 128, 128)
        L, H = (64, 16)
        HD = L // H
        F, E, K = (256, 8, 2)
        THETA = 10000.0
        EPS = 1e-05

        def _rmsnorm(x, g):
            return x * g * jax.lax.rsqrt(jnp.mean(x * x, axis=-1, keepdims=True) + EPS)

        def _rope(t, pos):
            inv_freq = 1.0 / THETA ** (jnp.arange(0, HD, 2, dtype=jnp.float32) / HD)
            ang = pos[:, None].astype(jnp.float32) * inv_freq[None, :]
            cos, sin = (jnp.cos(ang), jnp.sin(ang))
            t1, t2 = (t[..., 0::2], t[..., 1::2])
            r1 = t1 * cos - t2 * sin
            r2 = t1 * sin + t2 * cos
            return jnp.stack([r1, r2], axis=-1).reshape(t.shape)

        def _forward(x, g1, g2, w_down, wq, wk, wv, w_up, router_w, w1, w2, w3):
            b, s, _ = x.shape
            pos = jnp.arange(s)
            h = _rmsnorm(x, g1)
            c = h @ w_down
            split = lambda t: t.reshape(b, s, H, HD).transpose(0, 2, 1, 3)
            q = _rope(split(c @ wq), pos)
            k = _rope(split(c @ wk), pos)
            v = split(c @ wv)
            scores = jnp.einsum('bhqd,bhkd->bhqk', q, k) / jnp.sqrt(jnp.float32(HD))
            causal = jnp.tril(jnp.ones((s, s), bool))
            scores = jnp.where(causal, scores, -jnp.inf)
            attn = jax.nn.softmax(scores, axis=-1)
            o = jnp.einsum('bhqk,bhkd->bhqd', attn, v).transpose(0, 2, 1, 3).reshape(b, s, L)
            x = x + o @ w_up
            res = x
            t = _rmsnorm(x, g2).reshape(-1, D)
            probs = jax.nn.softmax(t @ router_w, axis=-1)
            vals, idx = jax.lax.top_k(probs, K)
            w = vals / jnp.sum(vals, axis=-1, keepdims=True)
            gate = jnp.sum(jax.nn.one_hot(idx, E, dtype=t.dtype) * w[..., None], axis=1)
            hid = jax.nn.silu(jnp.einsum('td,edf->tef', t, w1)) * jnp.einsum('td,edf->tef', t, w3)
            y_e = jnp.einsum('tef,efd->ted', hid, w2)
            y = jnp.einsum('ted,te->td', y_e, gate)
            return res + y.reshape(b, s, D)
        key = jax.random.key(seed)
        ks = jax.random.split(key, 12)
        g = lambda k, shape, scale: jax.random.normal(k, shape, dtype=jnp.float32) * scale
        return {'x': g(ks[0], (B, S, D), 1.0), 'g1': jnp.ones((D,), jnp.float32), 'g2': jnp.ones((D,), jnp.float32), 'w_down': g(ks[1], (D, L), 0.02), 'wq': g(ks[2], (L, L), 0.02), 'wk': g(ks[3], (L, L), 0.02), 'wv': g(ks[4], (L, L), 0.02), 'w_up': g(ks[5], (L, D), 0.02), 'router_w': g(ks[6], (D, E), 0.02), 'w1': g(ks[7], (E, D, F), 0.02), 'w3': g(ks[8], (E, D, F), 0.02), 'w2': g(ks[9], (E, F, D), 0.02)}
    _L0_ffn_in = _L0_ffn_setup()
    _d = {'L0_attn_h': _L0_attn_in['h'], 'L0_attn_w_qc': _L0_attn_in['w_qc'], 'L0_attn_w_qup': _L0_attn_in['w_qup'], 'L0_attn_w_k': _L0_attn_in['w_k'], 'L0_attn_w_v': _L0_attn_in['w_v'], 'L0_attn_g_qnorm': _L0_attn_in['g_qnorm'], 'L0_attn_g_knorm': _L0_attn_in['g_knorm'], 'L0_attn_w_gate': _L0_attn_in['w_gate'], 'L0_attn_b_gate': _L0_attn_in['b_gate'], 'L0_attn_sink_logit': _L0_attn_in['sink_logit'], 'L0_attn_w_out_group': _L0_attn_in['w_out_group'], 'L0_attn_w_out': _L0_attn_in['w_out'], 'L0_ffn_g1': _L0_ffn_in['g1'], 'L0_ffn_g2': _L0_ffn_in['g2'], 'L0_ffn_w_down': _L0_ffn_in['w_down'], 'L0_ffn_wq': _L0_ffn_in['wq'], 'L0_ffn_wk': _L0_ffn_in['wk'], 'L0_ffn_wv': _L0_ffn_in['wv'], 'L0_ffn_w_up': _L0_ffn_in['w_up'], 'L0_ffn_router_w': _L0_ffn_in['router_w'], 'L0_ffn_w1': _L0_ffn_in['w1'], 'L0_ffn_w2': _L0_ffn_in['w2'], 'L0_ffn_w3': _L0_ffn_in['w3']}
    _x0 = _d['L0_attn_h']
    _d['L0_attn_h'] = jax.random.normal(jax.random.fold_in(jax.random.key(seed), 1), (8, 512, 128), dtype=_x0.dtype)
    del _x0
    return _d

def reference(L0_attn_h, L0_attn_w_qc, L0_attn_w_qup, L0_attn_w_k, L0_attn_w_v, L0_attn_g_qnorm, L0_attn_g_knorm, L0_attn_w_gate, L0_attn_b_gate, L0_attn_sink_logit, L0_attn_w_out_group, L0_attn_w_out, L0_ffn_g1, L0_ffn_g2, L0_ffn_w_down, L0_ffn_wq, L0_ffn_wk, L0_ffn_wv, L0_ffn_w_up, L0_ffn_router_w, L0_ffn_w1, L0_ffn_w2, L0_ffn_w3):

    def _L0_attn_ref(h, w_qc, w_qup, w_k, w_v, g_qnorm, g_knorm, w_gate, b_gate, sink_logit, w_out_group, w_out):
        import jax, jax.numpy as jnp
        import numpy as np
        H, D, CR, SEL_K = (8, 64, 32, 16)
        ROPE_DIM, THETA, WINDOW, GROUPS = (32, 10000.0, 64, 2)
        INTER, HID, QC = (64, 128, 32)
        NEG = -1e+30

        def _rope_cache(t):
            half = ROPE_DIM // 2
            inv = 1.0 / THETA ** (jnp.arange(half, dtype=jnp.float32) * 2.0 / ROPE_DIM)
            ang = jnp.arange(t, dtype=jnp.float32)[:, None] * inv[None, :]
            return (jnp.cos(ang), jnp.sin(ang))

        def _apply_partial_rope(x, cos, sin):
            half = ROPE_DIM // 2
            x1, x2, rest = (x[..., :half], x[..., half:ROPE_DIM], x[..., ROPE_DIM:])
            return jnp.concatenate([x1 * cos - x2 * sin, x1 * sin + x2 * cos, rest], -1)

        def _rmsnorm(x, g, eps=1e-06):
            return x * jax.lax.rsqrt(jnp.mean(x * x, -1, keepdims=True) + eps) * g
        b, t, _ = h.shape
        cos, sin = _rope_cache(t)
        q = (h @ w_qc @ w_qup).reshape(b, t, H, D).transpose(0, 2, 1, 3)
        q = _rmsnorm(_apply_partial_rope(q, cos, sin), g_qnorm)
        k = _rmsnorm(_apply_partial_rope(h @ w_k, cos, sin), g_knorm)
        v = h @ w_v
        scale = 1.0 / np.sqrt(D).astype(np.float32)
        qpos = jnp.arange(t)
        sink = jnp.broadcast_to(sink_logit[None, :, None, None], (b, H, t, 1))
        nb = t // CR
        kc = k[:, :nb * CR].reshape(b, nb, CR, D).mean(2)
        vc = v[:, :nb * CR].reshape(b, nb, CR, D).mean(2)
        comp_valid = ((jnp.arange(nb) + 1) * CR - 1)[None, :] <= qpos[:, None]
        any_blk = comp_valid.any(-1, keepdims=True)
        safe = jnp.where(any_blk, comp_valid, True)
        sc_raw = jnp.einsum('bhqd,bnd->bhqn', q, kc) * scale
        pc = jax.nn.softmax(jnp.concatenate([jnp.where(safe, sc_raw, NEG), sink], -1), -1)
        comp_out = jnp.einsum('bhqn,bnd->bhqd', pc[..., :nb], vc)
        comp_out = jnp.where(any_blk[None, None], comp_out, 0.0)
        sel_sc = jnp.where(comp_valid, sc_raw, -jnp.inf)
        top_idx = jax.lax.top_k(sel_sc, min(SEL_K, nb))[1]
        sel_blocks = (top_idx[..., :, None] == jnp.arange(nb)).any(-2)
        block_of = jnp.minimum(qpos // CR, nb - 1)
        causal = qpos[:, None] >= qpos[None, :]
        in_range = qpos < nb * CR
        tok_sel = sel_blocks[..., block_of] & (causal & in_range[None, :])[None, None]
        scores_full = jnp.einsum('bhqd,bkd->bhqk', q, k) * scale
        ps = jax.nn.softmax(jnp.where(tok_sel, scores_full, NEG), -1)
        sel_out = jnp.einsum('bhqk,bkd->bhqd', ps, v)
        sw = causal & (qpos[:, None] - qpos[None, :] < WINDOW)
        pw = jax.nn.softmax(jnp.concatenate([jnp.where(sw[None, None], scores_full, NEG), sink], -1), -1)
        sw_out = jnp.einsum('bhqk,bkd->bhqd', pw[..., :t], v)
        g = jax.nn.sigmoid(q @ w_gate + b_gate)
        g = g / jnp.clip(g.sum(-1, keepdims=True), 1e-06)
        mixed = g[..., 0:1] * comp_out + g[..., 1:2] * sel_out + g[..., 2:3] * sw_out
        x = mixed.transpose(0, 2, 1, 3).reshape(b, t, GROUPS, H // GROUPS * D)
        y = jnp.einsum('btgf,gfi->btgi', x, w_out_group).reshape(b, t, GROUPS * INTER)
        return y @ w_out

    def _L0_ffn_ref(x, g1, g2, w_down, wq, wk, wv, w_up, router_w, w1, w2, w3):
        import jax, jax.numpy as jnp
        import numpy as np
        B, S, D = (2, 128, 128)
        L, H = (64, 16)
        HD = L // H
        F, E, K = (256, 8, 2)
        THETA = 10000.0
        EPS = 1e-05

        def _rmsnorm(x, g):
            return x * g * jax.lax.rsqrt(jnp.mean(x * x, axis=-1, keepdims=True) + EPS)

        def _rope(t, pos):
            inv_freq = 1.0 / THETA ** (jnp.arange(0, HD, 2, dtype=jnp.float32) / HD)
            ang = pos[:, None].astype(jnp.float32) * inv_freq[None, :]
            cos, sin = (jnp.cos(ang), jnp.sin(ang))
            t1, t2 = (t[..., 0::2], t[..., 1::2])
            r1 = t1 * cos - t2 * sin
            r2 = t1 * sin + t2 * cos
            return jnp.stack([r1, r2], axis=-1).reshape(t.shape)

        def _forward(x, g1, g2, w_down, wq, wk, wv, w_up, router_w, w1, w2, w3):
            b, s, _ = x.shape
            pos = jnp.arange(s)
            h = _rmsnorm(x, g1)
            c = h @ w_down
            split = lambda t: t.reshape(b, s, H, HD).transpose(0, 2, 1, 3)
            q = _rope(split(c @ wq), pos)
            k = _rope(split(c @ wk), pos)
            v = split(c @ wv)
            scores = jnp.einsum('bhqd,bhkd->bhqk', q, k) / jnp.sqrt(jnp.float32(HD))
            causal = jnp.tril(jnp.ones((s, s), bool))
            scores = jnp.where(causal, scores, -jnp.inf)
            attn = jax.nn.softmax(scores, axis=-1)
            o = jnp.einsum('bhqk,bhkd->bhqd', attn, v).transpose(0, 2, 1, 3).reshape(b, s, L)
            x = x + o @ w_up
            res = x
            t = _rmsnorm(x, g2).reshape(-1, D)
            probs = jax.nn.softmax(t @ router_w, axis=-1)
            vals, idx = jax.lax.top_k(probs, K)
            w = vals / jnp.sum(vals, axis=-1, keepdims=True)
            gate = jnp.sum(jax.nn.one_hot(idx, E, dtype=t.dtype) * w[..., None], axis=1)
            hid = jax.nn.silu(jnp.einsum('td,edf->tef', t, w1)) * jnp.einsum('td,edf->tef', t, w3)
            y_e = jnp.einsum('tef,efd->ted', hid, w2)
            y = jnp.einsum('ted,te->td', y_e, gate)
            return res + y.reshape(b, s, D)
        return _forward(x, g1, g2, w_down, wq, wk, wv, w_up, router_w, w1, w2, w3)
    x = L0_attn_h
    x = x + _layernorm(_L0_attn_ref(_layernorm(x, axis=-1), L0_attn_w_qc, L0_attn_w_qup, L0_attn_w_k, L0_attn_w_v, L0_attn_g_qnorm, L0_attn_g_knorm, L0_attn_w_gate, L0_attn_b_gate, L0_attn_sink_logit, L0_attn_w_out_group, L0_attn_w_out), axis=-1)
    x = x + _layernorm(_L0_ffn_ref(_layernorm(x, axis=-1), L0_ffn_g1, L0_ffn_g2, L0_ffn_w_down, L0_ffn_wq, L0_ffn_wk, L0_ffn_wv, L0_ffn_w_up, L0_ffn_router_w, L0_ffn_w1, L0_ffn_w2, L0_ffn_w3), axis=-1)
    return x

_drawn_inputs = setup_inputs


def setup_inputs(seed=0):
    import zlib

    import numpy as np

    out = dict(_drawn_inputs(seed))
    spreads = {'L0_attn_g_qnorm': (1.0, 0.2),
     'L0_attn_g_knorm': (1.0, 0.2),
     'L0_attn_b_gate': (0.0, 0.8),
     'L0_ffn_g1': (1.0, 0.6),
     'L0_ffn_g2': (1.0, 0.6)}
    factors = {'L0_attn_sink_logit': 8.0,
     'L0_ffn_w_down': 8.0,
     'L0_ffn_wq': 8.0,
     'L0_ffn_wk': 8.0,
     'L0_ffn_wv': 8.0,
     'L0_ffn_w_up': 8.0,
     'L0_ffn_router_w': 8.0,
     'L0_ffn_w1': 8.0,
     'L0_ffn_w2': 8.0,
     'L0_ffn_w3': 8.0}
    for name, (base, spread) in spreads.items():
        noise = np.random.default_rng([zlib.crc32(name.encode()), seed]).standard_normal(out[name].shape)
        drawn = base * np.exp(spread * noise) if base else spread * noise
        out[name] = jnp.asarray(drawn.astype(out[name].dtype))
    for name, factor in factors.items():
        out[name] = (out[name] * factor).astype(out[name].dtype)
    return out
```

```python
import concourse.bass as bass
from concourse import mybir
from contextlib import ExitStack
import numpy as np

F32 = mybir.dt.float32
F32R = mybir.dt.float32r
BF16 = mybir.dt.bfloat16
ALU = mybir.AluOpType
ACT = mybir.ActivationFunctionType
AX = mybir.AxisListType

B, T, HID = 8, 512, 128
P = 128
NT = T // P
H, D, ROPE = 8, 64, 32
CR, WINDOW = 32, 64
NBLK = T // CR
H2, D2, L2 = 16, 4, 64
E, F = 8, 256
FC = F // P
BANK = 512
NEG = -1.0e30
SHIFT_CAP = 1.0e20
EPS5, EPS6 = 1e-5, 1e-6
SPLIT2 = 8
OW = D + 1
RW = 32

CONST_COLS = {}


def shape_constants():
    p = np.arange(P)
    cols, at = [], 0

    def add(name, a):
        nonlocal at
        a = np.asarray(a, np.float32).reshape(P, -1)
        CONST_COLS[name] = (at, a.shape[1])
        cols.append(a)
        at += a.shape[1]

    def rope(width, theta=10000.0):
        half = width // 2
        inv = (np.float32(1.0) / np.power(np.float32(theta), np.arange(half, dtype=np.float32) * np.float32(2.0) / np.float32(width))).astype(np.float32)
        ang = (np.arange(T, dtype=np.float32)[:, None] * inv[None, :]).astype(np.float32)
        ang = ang.reshape(NT, P, half).transpose(1, 0, 2)
        return np.cos(ang.astype(np.float64)), np.sin(ang.astype(np.float64))

    c, s = rope(ROPE)
    add("cos1", np.repeat(c[:, :, None, :], 2, axis=2))
    add("sin1", np.repeat(s[:, :, None, :], 2, axis=2))
    c, s = rope(D2)
    add("cos2", c)
    add("sin2", s)
    add("ident", np.eye(P))
    q, k = p[:, None], p[None, :]
    neg = lambda ok: np.where(ok, 0.0, NEG)
    back = np.concatenate([q + P - k, q - k], 1)
    add("near_q", neg((back >= 0) & (back < WINDOW)))
    add("far_q", neg(back >= WINDOW))
    add("causal_q", neg(q - k >= 0))
    kk, qq = p[:, None], p[None, :]
    add("near_own_k", neg((qq - kk >= 0) & (qq - kk < WINDOW)))
    add("near_prev_k", neg(qq + P - kk < WINDOW)[:, :P // 2])
    add("far_own_k", neg(qq - kk >= WINDOW))
    add("far_prev_k", neg(qq + P - kk >= WINDOW))
    add("causal_k", neg(qq - kk >= 0))
    tok = np.arange(NT)[None, :, None] * P + p[:, None, None]
    add("block_valid", neg((np.arange(NBLK)[None, None, :] + 1) * CR - 1 <= tok))
    blk = (np.arange(NT)[None, :, None] * P + p[:, None, None]) // CR
    add("mean_rows", (blk == (np.arange(P) % NBLK)[None, None, :]) / CR)
    add("head_rows", (p[:, None] // NBLK) == np.arange(H)[None, :])
    row = p
    quad, tile, kind, head = row // 64, row // 16 % 4, row // 8 % 2, row // 2 % 4
    add("shift_head", head[:, None] == np.arange(4)[None, :])
    add("shift_pick", np.repeat(((quad * 4 + tile) * 2 + kind)[:, None, None] == np.arange(16)[None, :, None], P, axis=2))
    add("shift2_tile", (row // 2 % 4)[:, None] == np.arange(4)[None, :])
    add("shift2_pick", np.repeat((row // 8)[:, None, None] == np.arange(H2)[None, :, None], P, axis=2))
    add("iota8", np.tile(np.arange(E, dtype=np.float32), (P, 1)))
    narrow, wide = [], []
    for (name, (at, n)), a in zip(list(CONST_COLS.items()), cols):
        if name in BF_CONSTS:
            BF_COLS[name] = (sum(c.shape[1] for c in narrow), n)
            narrow.append(a)
        if name not in BF_CONSTS or name == "ident":
            CONST_COLS[name] = (sum(c.shape[1] for c in wide), n)
            wide.append(a)
    return np.concatenate(wide, 1), np.concatenate(narrow, 1).astype(mybir.dt.np(BF16))


BF_COLS = {}
BF_CONSTS = ["ident", "near_q", "far_q", "causal_q", "near_own_k", "near_prev_k", "far_own_k",
             "far_prev_k", "causal_k", "shift_pick", "shift2_pick"]
CONSTS, CONSTS_BF = shape_constants()


class Signal:

    def __init__(self, sem, per):
        self.sem, self.per, self.given = sem, per, 0

    def at(self, b, n):
        assert 0 <= n <= self.per
        return b * self.per + n


def sandwich(nc, x, w_qc, w_qup, w_k, w_v, g_q, g_k, w_gate, b_gate, sink, w_og, w_out,
             g1, g2, w_down, wq2, wk2, wv2, w_up, router_w, w1, w2, w3, consts, consts_bf, out, n_batch=B):
    ctx = ExitStack()
    with ctx:
        def sb(name, shape, dt=F32):
            return ctx.enter_context(nc.sbuf_tensor(name, shape, dt))

        def sem(name):
            return ctx.enter_context(nc.semaphore(name))

        def signal(name, per):
            return Signal(sem(name), per)

        ncols = CONSTS.shape[1]
        cst = sb("cst", [P, ncols])
        cst_bf = sb("cst_bf", [P, CONSTS_BF.shape[1]], BF16)

        def con(name):
            a, n = CONST_COLS[name]
            return cst[:, a:a + n]

        def con_bf(name):
            a, n = BF_COLS[name]
            return cst_bf[:, a:a + n]

        ident, ident_bf = con("ident"), con_bf("ident")
        w_qc_sb = sb("w_qc_sb", [HID, 32])
        w_out_sb = sb("w_out_sb", [64, 2, HID])
        w_down_sb = sb("w_down_sb", [HID, L2])
        w_proj = sb("w_proj", [HID, H * D + 2 * D])
        w_fold = sb("w_fold", [P, 4, HID])
        w_qkv2 = sb("w_qkv2", [HID, 3 * L2])
        w_up_sb = sb("w_up_sb", [P, HID])
        router_sb = sb("router_sb", [HID, E])
        w13_sb = sb("w13_sb", [HID, E, 2, F])
        w2_sb = sb("w2_sb", [P, E, FC, HID])
        gain1 = sb("gain1", [P, H + 1, D])
        gain_in = sb("gain_in", [P, 2, D])
        g1_sb = sb("g1_sb", [P, HID])
        g2_sb = sb("g2_sb", [P, HID])
        bgate_sb = sb("bgate_sb", [P, 3])
        sink_sb = sb("sink_sb", [P, H])
        minus_half = sb("minus_half", [P, NT * (H + 1)])

        xin = sb("xin", [P, NT, HID])
        hn = sb("hn", [P, NT, HID])
        hT = sb("hT", [HID, T])
        stats = sb("stats", [P, NT, 6])
        mv = sb("mv", [P, NT, 2])
        var_in = sb("var_in", [P, NT * (H + 1)])
        rstd = sb("rstd", [P, NT * (H + 1)])
        qkv = sb("qkv", [P, NT, H + 2, D])
        sq = sb("sq", [P, H + 1, D])
        sumsq = sb("sumsq", [P, NT, H + 1])
        ropeA = sb("ropeA", [P, H + 1, ROPE])
        ropeB = sb("ropeB", [P, H + 1, ROPE])
        qsplit = sb("qsplit", [P, NT, H, 2, D])
        kdup = sb("kdup", [P, NT, 2, D])
        qT = sb("qT", [P, H, NT, P], F32R)
        kT_hi = sb("kT_hi", [P, T], F32R)
        kT_lo = sb("kT_lo", [P, T], F32R)
        va = sb("va", [P, NT, OW])
        comp_gate = sb("comp_gate", [P, RW])
        kmean = sb("kmean", [P, NBLK])
        vmean = sb("vmean", [P, H, D])
        cgT = sb("cgT", [P, 2, T])
        cg = sb("cg", [P, NT, H, RW])
        cs = sb("cs", [P, NT, H, NBLK])
        cexp = sb("cexp", [P, NT, H, NBLK])
        cmax = sb("cmax", [P, NT, H])
        csum = sb("csum", [P, NT, H])
        csink = sb("csink", [P, NT, H])
        ccoef = sb("ccoef", [P, NT, H])
        gz = sb("gz", [P, NT * H, 3])
        gate = sb("gate", [P, NT * H, 3])
        gsum = sb("gsum", [P, NT * H])
        pcT = sb("pcT", [P, T])
        nmax = sb("nmax", [P, 2, NT, 2, 4])
        nmax_bf = sb("nmax_bf", [P, 64, 2], BF16)
        shiftT = sb("shiftT", [P, 4, P], BF16)
        probs = [sb(f"probs{i}", [P, 2, BANK]) for i in range(2)]
        oT = [sb(f"oT{i}", [P, 2, BANK]) for i in range(2)]
        left_t = probs[0][0:64, :, :].rearrange("p a n -> p (a n)")[:, 0:6 * P].rearrange("p (c n) -> p c n", c=6)
        w_qup_sb = probs[1][0:32, 0, 0:H * D]
        w_og_sb = probs[1][:, 1, 0:4 * 64].rearrange("p (c n) -> p c n", c=4)
        w_qkv2_in = probs[1][0:L2, 1, 4 * 64:4 * 64 + 3 * L2].rearrange("p (w n) -> p w n", w=3)
        on = sb("on", [P, 2, NT, H, OW])
        cargs = sb("cargs", [P, 4, NT, H])
        cexps = sb("cexps", [P, 4, NT, H])
        nfull = sb("nfull", [P, NT, H])
        nsink = sb("nsink", [P, NT, H])
        zfull = sb("zfull", [P, NT, H])
        zwin = sb("zwin", [P, NT, H])
        ztmp = sb("ztmp", [P, NT, H])
        coef = sb("coef", [P, 2, NT, H])
        spare_s = qsplit[:, :, :, :, :].rearrange("p i h s d -> p (i h s d)")
        mixa, mixb = ([spare_s[:, (2 * m + n) * H * D:(2 * m + n + 1) * H * D].rearrange("p (h d) -> p h d", h=H)
                       for n in range(2)] for m in range(2))
        mixT = [spare_s[:, (4 + n) * H * D:(5 + n) * H * D].rearrange("p (c n) -> p c n", c=4) for n in range(2)]
        x1 = sb("x1", [P, NT, HID])
        ffn_in = sb("ffn_in", [P, NT, HID])
        ms = sb("ms", [P, NT])
        scrap = sb("scrap", [P, 1])
        qkv2 = sb("qkv2", [P, NT, 3 * L2])
        n_parts = NT * H2 * SPLIT2 * D2
        parts2 = spare_s[:, 0:n_parts].bitcast(BF16).rearrange("p (w n s d) -> p w n s d", w=2, s=SPLIT2, d=D2)
        n_rot = NT * 2 * H2 * 2
        rot = [spare_s[:, n_parts + n * n_rot:n_parts + (n + 1) * n_rot].rearrange("p (i h r) -> p i h r", i=NT, r=2) for n in range(4)]
        at = n_parts + 4 * n_rot
        n_qk = 2 * NT * L2
        qk2 = spare_s[:, at:at + n_qk].rearrange("p (w n d) -> p w n d", w=2, d=D2)
        rem = spare_s[:, at + n_qk:at + 2 * n_qk].rearrange("p (w n d) -> p w n d", w=2, d=D2)
        q2T = sb("q2T", [P, 4, T], BF16)
        k2Z = sb("k2Z", [P, 4, 4, T], BF16)
        va2 = sb("va2", [P, NT, H2, RW])
        nmax2 = sb("nmax2", [P, H2, NT])
        nmax2_bf = sb("nmax2_bf", [P, 64, 2], BF16)
        shift2T = sb("shift2T", [P, 4, P], BF16)
        o2T = [oT[n][:, 0, :] for n in range(2)]
        rz2 = sb("rz2", [P, NT, 4])
        o2n = sb("o2n", [P, NT, 2 * H2, D2])
        o2nT = cgT[:, 0, :]
        res = sb("res", [P, NT, HID])
        tT = sb("tT", [HID, T])
        logit = sb("logit", [P, NT, E])
        top1 = sb("top1", [P, NT])
        top2 = sb("top2", [P, NT])
        pick = sb("pick", [P, NT, E])
        hot1 = sb("hot1", [P, NT, E])
        hot2 = sb("hot2", [P, NT, E])
        wtop = sb("wtop", [P, 2, NT])
        egate = sb("egate", [P, NT, E])
        spare = on[:, :, :, :, :].rearrange("p k i h d -> p (k i h d)")
        hid = [spare[:, n * FC * T:(n + 1) * FC * T].rearrange("p (c t) -> p c t", c=FC) for n in range(2)]
        th = [spare[:, (2 * FC + n) * T:(2 * FC + n + 1) * T] for n in range(2)]
        spare_q = qkv[:, :, :, :].rearrange("p i h d -> p (i h d)")
        yg = [spare_q[:, n * T:(n + 1) * T].rearrange("p (i c) -> p i c", i=NT) for n in range(2)]
        acc = spare_q[:, 2 * T:3 * T].rearrange("p (i c) -> p i c", i=NT)
        yout = spare_q[:, 3 * T:4 * T].rearrange("p (i c) -> p i c", i=NT)

        ps = ctx.enter_context(nc.psum_tensor("ps", [P, 8, BANK], F32))

        def bank(n, k=1):
            return ps[:, n:n + k, :] if k > 1 else ps[:, n, :]

        loaded = sem("loaded")
        cast_done = sem("cast_done")
        folded = sem("folded")
        fold_psum = sem("fold_psum")
        padded = sem("padded")
        batch_done = signal("batch_done", 5)
        x_loaded = signal("x_loaded", 16)
        var_ready = signal("var_ready", 7)
        rstd_ready = signal("rstd_ready", 7)
        h_ready = signal("h_ready", 1)
        hT_psum = signal("hT_psum", 1)
        hT_ready = signal("hT_ready", 1)
        qkv_psum = signal("qkv_psum", NT)
        qkv_ready = signal("qkv_ready", NT)
        sq_ready = signal("sq_ready", NT)
        sq_used = signal("sq_used", NT)
        rope_done = signal("rope_done", NT)
        gained = signal("gained", NT)
        v_ready = signal("v_ready", 1)
        split_ready = signal("split_ready", NT)
        qT_psum = signal("qT_psum", NT)
        qT_ready = signal("qT_ready", NT)
        kT_psum = signal("kT_psum", 1)
        k_ready = signal("k_ready", 1)
        vmean_psum = signal("vmean_psum", 1)
        vmean_ready = signal("vmean_ready", 1)
        cgT_psum = signal("cgT_psum", 2)
        cgT_ready = signal("cgT_ready", 2)
        cg_psum = signal("cg_psum", 2)
        cg_ready = signal("cg_ready", 2)
        cexp_arg = signal("cexp_arg", 1)
        cexp_ready = signal("cexp_ready", 1)
        pc_ready = signal("pc_ready", 1)
        pcT_psum = signal("pcT_psum", 1)
        pcT_ready = signal("pcT_ready", 1)
        s_psum = signal("s_psum", 16)
        max_done = signal("max_done", 16)
        nmax_split = signal("nmax_split", 1)
        shift_psum = signal("shift_psum", 1)
        shift_ready = signal("shift_ready", 1)
        coef_arg = signal("coef_arg", 1)
        coef_exp = signal("coef_exp", 1)
        coef_done = signal("coef_done", 1)
        NU1 = 16
        st_psum = signal("st_psum", NU1)
        exp_done = signal("exp_done", NU1)
        pv_done = signal("pv_done", NU1)
        oT_ready = signal("oT_ready", 8)
        on_psum = signal("on_psum", 8)
        on_ready = signal("on_ready", 8)
        comp_psum = signal("comp_psum", NT)
        near_scaled = signal("near_scaled", NT)
        mix_ready = signal("mix_ready", NT)
        mixT_psum = signal("mixT_psum", NT)
        mixT_ready = signal("mixT_ready", NT)
        attn_psum = signal("attn_psum", 1)
        h2_ready = signal("h2_ready", 1)
        h2T_psum = signal("h2T_psum", 1)
        h2T_ready = signal("h2T_ready", 1)
        qkv2_psum = signal("qkv2_psum", 1)
        qkv2_ready = signal("qkv2_ready", 1)
        va2_ready = signal("va2_ready", 1)
        parts2_ready = signal("parts2_ready", 1)
        q2T_psum = signal("q2T_psum", 1)
        k2T_psum = signal("k2T_psum", 1)
        q2T_ready = signal("q2T_ready", 1)
        k2Z_ready = signal("k2Z_ready", 1)
        s2_psum = signal("s2_psum", 16)
        max2_done = signal("max2_done", 16)
        nmax2_split = signal("nmax2_split", 1)
        shift2_psum = signal("shift2_psum", 1)
        shift2_ready = signal("shift2_ready", 1)
        NU2 = 32
        st2_psum = signal("st2_psum", NU2)
        exp2_done = signal("exp2_done", NU2)
        pv2_done = signal("pv2_done", NU2)
        o2T_ready = signal("o2T_ready", 4)
        o2n_psum = signal("o2n_psum", 4)
        o2n_ready = signal("o2n_ready", 4)
        o2nT_psum = signal("o2nT_psum", 1)
        o2nT_ready = signal("o2nT_ready", 1)
        up_psum = signal("up_psum", 1)
        res_ready = signal("res_ready", 1)
        res_sq = signal("res_sq", 1)
        t_ready = signal("t_ready", 1)
        tT_psum = signal("tT_psum", 1)
        tT_ready = signal("tT_ready", 1)
        router_psum = signal("router_psum", 1)
        wtop_arg = signal("wtop_arg", 1)
        wtop_exp = signal("wtop_exp", 1)
        NX = E * FC
        hid_psum = signal("hid_psum", NX)
        th_ready = signal("th_ready", NX)
        hid_ready = signal("hid_ready", NX)
        y_psum = signal("y_psum", E)
        yg_ready = signal("yg_ready", E)
        acc_done = signal("acc_done", E)
        out_ready = signal("out_ready", 1)
        out_stored = signal("out_stored", 16)
        vector_chain = signal("vector_chain", VECTOR_STEPS)

        def units1(i):
            near, far = 0, 1
            if i == 0:
                return [[(near, 0, 0, P, "near_own_k"), (far, 0, 0, P, "far_own_k")]]
            first = [(near, i, 0, P, "near_own_k"), (near, i - 1, 0, P // 2, "near_prev_k"),
                     (far, i, P // 2, P // 2, "far_own_k")]
            rest = [(far, i - 1, 0, P, "far_prev_k")] + [(far, j, 0, P, None) for j in range(i - 1)]
            return [first] + [rest[n:n + 2] for n in range(0, len(rest), 2)]

        UNITS1 = [(quad, i, u, n == 0, n == len(units1(i)) - 1)
                  for quad in range(2) for i in range(NT) for n, u in enumerate(units1(i))]
        assert len(UNITS1) == NU1
        LAST_UNIT1 = [u + 1 for u, unit in enumerate(UNITS1) if unit[4]]
        UNITS2 = [(g, j, half) for g in range(4) for j in range(NT) for half in range(2)]
        assert len(UNITS2) == NU2

        block = ctx.enter_context(nc.Block())

        LOADS = []

        def row_bcast(v, n):
            return v.rearrange("(a n) -> a n", a=1).partition_broadcast(P)

        @block.sync
        def _(sync):
            loads = [
                (cst[:, :], consts), (cst_bf[:, :], consts_bf), (w_qc_sb[:, :], w_qc), (w_qup_sb[:, :], w_qup),
                (w_og_sb[:, 0:2, :], w_og[0, :, :].rearrange("(c p) n -> p c n", p=P)),
                (w_og_sb[:, 2:4, :], w_og[1, :, :].rearrange("(c p) n -> p c n", p=P)),
                (w_out_sb[:, :, :], w_out.rearrange("(g p) n -> p g n", p=64)),
                (w_down_sb[:, :], w_down),
                (w_qkv2_in[:, 0, :], wq2), (w_qkv2_in[:, 1, :], wk2), (w_qkv2_in[:, 2, :], wv2),
                (w_proj[:, H * D:H * D + D], w_k), (w_proj[:, H * D + D:], w_v),
                (w_up_sb[0:L2, :], w_up), (router_sb[:, :], router_w),
                (gain_in[:, 0, :], row_bcast(g_q, D)), (gain_in[:, 1, :], row_bcast(g_k, D)),
                (g1_sb[:, :], row_bcast(g1, HID)), (g2_sb[:, :], row_bcast(g2, HID)),
                (bgate_sb[:, :], row_bcast(b_gate, 3)), (sink_sb[:, :], row_bcast(sink, H)),
                (comp_gate[0:D, NBLK:NBLK + 3], w_gate), (comp_gate[D:P, NBLK:NBLK + 3], w_gate),
                (w13_sb[:, :, 0, :], w1.rearrange("e d f -> d e f")),
                (w13_sb[:, :, 1, :], w3.rearrange("e d f -> d e f")),
                (w2_sb[:, :, :, :].rearrange("p e c n -> p (e c) n"), w2.rearrange("e (c p) n -> p (e c) n", p=P)),
            ]
            sync.wait_ge(padded, 1)
            for dst, src in loads:
                sync.dma_start(dst, src).then_inc(loaded, 16)
            assert len(loads) == N_LOADS
            sync.sem_inc(batch_done.sem, 1)
            with sync.Fori(0, n_batch) as b:
                sync.wait_ge(batch_done.sem, batch_done.at(b, 1))
                sync.dma_start(xin[:, :, :], x[bass.ds(b, 1), :, :].rearrange("b (i p) c -> p (b i) c", p=P)).then_inc(x_loaded.sem, 16)
                sync.wait_ge(out_ready.sem, out_ready.at(b, 1))
                sync.dma_start(out[bass.ds(b, 1), :, :].rearrange("b (i p) c -> p (b i) c", p=P), yout[:, :, :]).then_inc(out_stored.sem, 16)
                sync.wait_ge(out_stored.sem, out_stored.at(b, 16))
                sync.sem_inc(batch_done.sem, 1)

        @block.gpsimd
        def _(pool):
            pool.memset(w_up_sb[:, :], 0.0)
            pool.memset(comp_gate[:, :], 0.0).then_inc(padded, 1)
            pool.memset(minus_half[:, :], -0.5)
            pool.memset(va[:, :, D:OW], 1.0)
            pool.memset(k2Z[:, :, :, :], 0.0)
            pool.memset(o2n[:, :, H2:, :], 0.0)
            pool.memset(va2[:, :, :, :], 0.0).then_inc(padded, 1)
            pool.wait_ge(padded, 2)
            pool.memset(va2[:, :, :, D2:D2 + 1], 1.0).then_inc(padded, 1)
            pool.wait_ge(cast_done, 1)

            with pool.Fori(0, n_batch) as b:

                def inverse_root(use, cols):
                    pool.wait_ge(var_ready.sem, var_ready.at(b, use))
                    pool.tensor_tensor(rstd[:, 0:cols], var_in[:, 0:cols], minus_half[:, 0:cols],
                                       ALU.pow).then_inc(rstd_ready.sem, 1)

                pool.wait_ge(batch_done.sem, batch_done.at(b, 1))
                inverse_root(1, NT)
                for i in range(NT):
                    pool.wait_ge(rope_done.sem, rope_done.at(b, i + 1))
                    pool.tensor_tensor(qkv[:, i, 0:H + 1, :], qkv[:, i, 0:H + 1, :], gain1[:, :, :],
                                       ALU.mult).then_inc(gained.sem, 1)
                pool.tensor_copy(va[:, :, 0:D], qkv[:, :, H + 1, :]).then_inc(v_ready.sem, 1)
                inverse_root(2, NT * (H + 1))
                pool.wait_ge(coef_done.sem, coef_done.at(b, 1))
                for i in range(NT):
                    if i >= 2:
                        pool.wait_ge(mix_ready.sem, mix_ready.at(b, i - 1))
                    pool.tensor_tensor(mixb[i % 2][:, :, :], on[:, 0, i, :, 0:D],
                                       coef[:, 0, i, :].unsqueeze(2).to_broadcast([P, H, D]),
                                       ALU.mult).then_inc(near_scaled.sem, 1)
                inverse_root(3, NT)
                inverse_root(4, NT)
                inverse_root(5, NT)
                inverse_root(6, NT)
                for e in range(E):
                    pool.wait_ge(yg_ready.sem, yg_ready.at(b, e + 1))
                    if e >= 1:
                        pool.wait_ge(acc_done.sem, acc_done.at(b, e))
                    so_far = acc if e >= 1 else res
                    pool.tensor_tensor(acc[:, :, :], so_far[:, :, :], yg[e % 2][:, :, :], ALU.add).then_inc(acc_done.sem, 1)
                inverse_root(7, NT)
                pool.wait_ge(rstd_ready.sem, rstd_ready.at(b, 7))
                pool.sem_inc(batch_done.sem, 1)

        @block.scalar
        def _(act):
            act.wait_ge(fold_psum, 1)
            flat = ps[:, 0:2, :].rearrange("p a n -> p (a n)")
            nc.scalar.activation(left_t[:, 0:5, :].rearrange("p c n -> p (c n)"), flat[0:64, 0:5 * P], ACT.Copy)
            nc.scalar.activation(left_t[0:32, 5, :], flat[0:32, 5 * P:6 * P], ACT.Copy).then_inc(folded, 1)
            act.wait_ge(fold_psum, 2)
            nc.scalar.activation(w_proj[:, 0:H * D], bank(2), ACT.Copy).then_inc(folded, 1)
            nc.scalar.activation(w_fold[:, :, :], bank(3).rearrange("p (c n) -> p c n", c=4), ACT.Copy).then_inc(folded, 1)
            nc.scalar.activation(w_qkv2[:, :], ps[:, 4, 0:3 * L2], ACT.Copy).then_inc(folded, 1)

            with act.Fori(0, n_batch) as b:

                def copy(dst, src, sig):
                    nc.scalar.activation(dst, src, ACT.Copy).then_inc(sig.sem, 1)

                act.wait_ge(batch_done.sem, batch_done.at(b, 1))
                act.wait_ge(hT_psum.sem, hT_psum.at(b, 1))
                copy(hT[:, :], bank(0), hT_ready)
                for i in range(NT):
                    act.wait_ge(qkv_psum.sem, qkv_psum.at(b, i + 1))
                    src = ps[:, 1 + 2 * (i % 2):3 + 2 * (i % 2), :].rearrange("p a n -> p (a n)")[:, 0:(H + 2) * D]
                    copy(qkv[:, i, :, :].rearrange("p h d -> p (h d)"), src, qkv_ready)
                    if i >= 1:
                        act.wait_ge(sq_used.sem, sq_used.at(b, i))
                    act.wait_ge(qkv_ready.sem, qkv_ready.at(b, i + 1))
                    nc.scalar.activation(sq[:, :, :], qkv[:, i, 0:H + 1, :], ACT.Square).then_inc(sq_ready.sem, 1)
                for i in range(NT):
                    act.wait_ge(qT_psum.sem, qT_psum.at(b, i + 1))
                    b0 = 6 if i % 2 == 0 else 4
                    copy(qT[:, :, i, :], ps[:, b0:b0 + 2, :].rearrange("p a (h n) -> p (a h) n", n=P), qT_ready)
                for quad in range(2):
                    act.wait_ge(cgT_psum.sem, cgT_psum.at(b, quad + 1))
                    copy(cgT[:, quad, :], bank(2 + quad), cgT_ready)
                for quad in range(2):
                    act.wait_ge(cg_psum.sem, cg_psum.at(b, quad + 1))
                    copy(cg[:, :, 4 * quad:4 * quad + 4, :].rearrange("p i h r -> p i (h r)"), bank(4 + quad).rearrange("p (i r) -> p i r", i=NT), cg_ready)
                act.wait_ge(cexp_arg.sem, cexp_arg.at(b, 1))
                nc.scalar.activation(cexp[:, :, :, :], cs[:, :, :, :], ACT.Exp)
                nc.scalar.activation(csink[:, :, :], csink[:, :, :], ACT.Exp)
                nc.scalar.activation(gz[:, :, :], gz[:, :, :], ACT.Exp, scale=-1.0).then_inc(cexp_ready.sem, 1)
                act.wait_ge(pcT_psum.sem, pcT_psum.at(b, 1))
                copy(pcT[:, :], bank(6), pcT_ready)
                act.wait_ge(coef_arg.sem, coef_arg.at(b, 1))
                nc.scalar.activation(cexps[:, :, :, :], cargs[:, :, :, :], ACT.Exp).then_inc(coef_exp.sem, 1)
                for u, (quad, i, blocks, first, last) in enumerate(UNITS1):
                    act.wait_ge(st_psum.sem, st_psum.at(b, u + 1))
                    if u >= 2:
                        act.wait_ge(pv_done.sem, pv_done.at(b, u - 1))
                    n = 1 if blocks[0][3] == P and len(blocks) == 1 else 2
                    nc.scalar.activation(probs[u % 2][:, 0:n, :], ps[:, 2 * (u % 2):2 * (u % 2) + n, :],
                                         ACT.Exp).then_inc(exp_done.sem, 1)
                for i in range(NT):
                    act.wait_ge(mixT_psum.sem, mixT_psum.at(b, i + 1))
                    if i >= 2:
                        act.wait_ge(mixT_psum.sem, mixT_psum.at(b, i + 1))
                    copy(mixT[i % 2][:, :, :], ps[:, 2 + i % 2, :].rearrange("p (c n) -> p c n", c=4), mixT_ready)
                act.wait_ge(h2T_psum.sem, h2T_psum.at(b, 1))
                copy(hT[:, :], bank(5), h2T_ready)
                act.wait_ge(qkv2_psum.sem, qkv2_psum.at(b, 1))
                copy(qkv2[:, :, :].rearrange("p (a i) n -> p a (i n)", a=2), ps[:, 6:8, 0:2 * 3 * L2], qkv2_ready)
                act.wait_ge(qkv2_ready.sem, qkv2_ready.at(b, 1))
                copy(va2[:, :, :, 0:D2], qkv2[:, :, 2 * L2:].rearrange("p i (h d) -> p i h d", d=D2), va2_ready)
                act.wait_ge(q2T_psum.sem, q2T_psum.at(b, 1))
                copy(q2T[:, :, :].rearrange("p g n -> p (g n)"), ps[:, 0:2, :].rearrange("p a n -> p (a n)").bitcast(BF16), q2T_ready)
                for u, (g, j, half) in enumerate(UNITS2):
                    act.wait_ge(st2_psum.sem, st2_psum.at(b, u + 1))
                    if u >= 2:
                        act.wait_ge(pv2_done.sem, pv2_done.at(b, u - 1))
                    n = T - j * P
                    nc.scalar.activation(probs[u % 2][:, :, 0:n], ps[:, 2 * (u % 2):2 * (u % 2) + 2, 0:n],
                                         ACT.Exp, scale=0.5).then_inc(exp2_done.sem, 1)
                act.wait_ge(o2nT_psum.sem, o2nT_psum.at(b, 1))
                copy(o2nT, bank(4), o2nT_ready)
                act.wait_ge(res_ready.sem, res_ready.at(b, 1))
                for i in range(NT):
                    ins = nc.scalar.activation(hn[:, i, :], res[:, i, :], ACT.Square, accum_out=ms[:, i:i + 1])
                ins.then_inc(res_sq.sem, 1)
                act.wait_ge(tT_psum.sem, tT_psum.at(b, 1))
                copy(tT[:, :], bank(1), tT_ready)
                act.wait_ge(wtop_arg.sem, wtop_arg.at(b, 1))
                nc.scalar.activation(wtop[:, 1, :], wtop[:, 0, :], ACT.Exp).then_inc(wtop_exp.sem, 1)
                for n in range(NX):
                    act.wait_ge(hid_psum.sem, hid_psum.at(b, n + 1))
                    if n >= 2:
                        act.wait_ge(hid_ready.sem, hid_ready.at(b, n - 1))
                    nc.scalar.activation(th[n % 2][:, :], bank(4 + 2 * (n % FC)), ACT.Tanh, scale=0.5).then_inc(th_ready.sem, 1)
                act.wait_ge(th_ready.sem, th_ready.at(b, NX))
                act.sem_inc(batch_done.sem, 1)

        @block.vector
        def _(dve):
            v = nc.vector
            dve.wait_ge(loaded, 16 * N_LOADS)
            v.tensor_scalar(gain1[:, 0:H, :], gain_in[:, 0, :].unsqueeze(1).to_broadcast([P, H, D]), D ** -0.5, None, ALU.mult)
            v.tensor_copy(gain1[:, H, :], gain_in[:, 1, :]).then_inc(cast_done, 1)
            dve.wait_ge(padded, 3)

            with dve.Fori(0, n_batch) as b:
                n_chain = [0]

                def link(ins):
                    n_chain[0] += 1
                    ins.then_inc(vector_chain.sem, 1)
                    dve.wait_ge(vector_chain.sem, vector_chain.at(b, n_chain[0]))


                def over(a, shape, axis):
                    return a.unsqueeze(axis).to_broadcast(shape)

                def mean_var(src, use):
                    for i in range(NT):
                        ins = v.bn_stats(stats[:, i, :], src(i))
                    link(ins)
                    v.memset(scrap[:, :], 0.0)
                    for i in range(NT):
                        ins = v.bn_aggr(mv[:, i, :], stats[:, i, :])
                    link(ins)
                    v.tensor_scalar(var_in[:, 0:NT], mv[:, :, 1], EPS5, None, ALU.add).then_inc(var_ready.sem, 1)
                    dve.wait_ge(rstd_ready.sem, rstd_ready.at(b, use))

                def centred(dst, src):
                    for i in range(NT):
                        ins = v.tensor_scalar(dst[:, i, :], src(i), mv[:, i, 0:1], rstd[:, i:i + 1], ALU.subtract, ALU.mult)
                    return ins

                dve.wait_ge(batch_done.sem, batch_done.at(b, 1))
                dve.wait_ge(x_loaded.sem, x_loaded.at(b, 16))
                mean_var(lambda i: xin[:, i, :], 1)
                centred(hn, lambda i: xin[:, i, :]).then_inc(h_ready.sem, 1)
                cos1 = con("cos1").rearrange("p (i r) -> p i r", i=NT)
                sin1 = con("sin1").rearrange("p (i r) -> p i r", i=NT)
                for i in range(NT):
                    dve.wait_ge(sq_ready.sem, sq_ready.at(b, i + 1))
                    v.tensor_reduce(sumsq[:, i, :], sq[:, :, :], AX.X, ALU.add).then_inc(sq_used.sem, 1)
                    if i >= 1:
                        dve.wait_ge(rope_done.sem, rope_done.at(b, i))
                    part = qkv[:, i, 0:H + 1, 0:ROPE]
                    v.tensor_tensor(ropeA[:, :, :], part, over(cos1[:, i, :], [P, H + 1, ROPE], 1), ALU.mult)
                    link(v.tensor_tensor(ropeB[:, :, :], part, over(sin1[:, i, :], [P, H + 1, ROPE], 1), ALU.mult))
                    half = ROPE // 2
                    v.tensor_tensor(qkv[:, i, 0:H + 1, 0:half], ropeA[:, :, 0:half], ropeB[:, :, half:], ALU.subtract)
                    v.tensor_tensor(qkv[:, i, 0:H + 1, half:ROPE], ropeB[:, :, 0:half], ropeA[:, :, half:], ALU.add).then_inc(rope_done.sem, 1)
                v.tensor_scalar(var_in[:, :], sumsq[:, :, :].rearrange("p i h -> p (i h)"), 1.0 / D, EPS6, ALU.mult, ALU.add).then_inc(var_ready.sem, 1)
                dve.wait_ge(rstd_ready.sem, rstd_ready.at(b, 2))
                for i in range(NT):
                    dve.wait_ge(gained.sem, gained.at(b, i + 1))
                    r = rstd[:, i * (H + 1):(i + 1) * (H + 1)]
                    qk = qkv[:, i, 0:H + 1, :]
                    link(v.tensor_tensor(qk, qk, over(r, [P, H + 1, D], 2), ALU.mult))
                    v.tensor_copy(kdup[:, i, :, :], over(qkv[:, i, H, :], [P, 2, D], 1))
                    link(v.tensor_copy(qsplit[:, i, :, 0, :].bitcast(F32R), qkv[:, i, 0:H, :]))
                    v.tensor_tensor(qsplit[:, i, :, 1, :], qkv[:, i, 0:H, :], qsplit[:, i, :, 0, :], ALU.subtract).then_inc(split_ready.sem, 1)
                dve.wait_ge(kT_psum.sem, kT_psum.at(b, 1))
                v.tensor_reduce(kmean[:, :], bank(0).rearrange("p (n r) -> p n r", r=CR), AX.X, ALU.add)
                link(v.tensor_copy(kT_hi[:, :], bank(0)))
                v.tensor_scalar(comp_gate[:, 0:NBLK], kmean[:, :], 1.0 / CR, None, ALU.mult)
                v.tensor_tensor(kT_lo[:, :], bank(0), kT_hi[:, :], ALU.subtract).then_inc(k_ready.sem, 1)
                dve.wait_ge(vmean_psum.sem, vmean_psum.at(b, 1))
                v.tensor_tensor(vmean[:, :, :], over(ps[:, 1, 0:D], [P, H, D], 1), over(con("head_rows"), [P, H, D], 2), ALU.mult).then_inc(vmean_ready.sem, 1)
                dve.wait_ge(cg_ready.sem, cg_ready.at(b, 2))
                full = [P, NT, H, NBLK]
                sink_b = over(sink_sb[:, :], [P, NT, H], 1)
                valid = con("block_valid").rearrange("p (i n) -> p i n", i=NT)
                for i in range(NT):
                    ins = v.tensor_tensor(cs[:, i, :, :], cg[:, i, :, 0:NBLK], over(valid[:, i, :], [P, H, NBLK], 1), ALU.add)
                gf = cg[:, :, :, NBLK:NBLK + 3].rearrange("p i h c -> p (i h) c")
                v.scalar_tensor_tensor(gz[:, :, :], gf, D ** 0.5, over(bgate_sb[:, :], [P, NT * H, 3], 1), ALU.mult, ALU.add)
                link(ins)
                link(v.tensor_reduce(cmax[:, :, :], cs[:, :, :, :], AX.X, ALU.max))
                link(v.tensor_tensor(cmax[:, :, :], cmax[:, :, :], sink_b, ALU.max))
                csf = cs[:, :, :, :].rearrange("p i h n -> p (i h) n")
                cmf = cmax[:, :, :].rearrange("p i h -> p (i h)")
                v.tensor_tensor(csf, csf, over(cmf, [P, NT * H, NBLK], 2), ALU.subtract)
                v.tensor_tensor(csink[:, :, :], sink_b, cmax[:, :, :], ALU.subtract).then_inc(cexp_arg.sem, 1)
                dve.wait_ge(cexp_ready.sem, cexp_ready.at(b, 1))
                link(v.tensor_scalar(gz[:, :, :], gz[:, :, :], 1.0, None, ALU.add))
                link(v.reciprocal(gate[:, :, :], gz[:, :, :]))
                link(v.tensor_reduce(gsum[:, :], gate[:, :, :], AX.X, ALU.add))
                link(v.tensor_scalar(gsum[:, :], gsum[:, :], 1e-6, None, ALU.max))
                v.tensor_reduce(csum[:, :, :], cexp[:, :, :, :], AX.X, ALU.add)
                link(v.reciprocal(gsum[:, :], gsum[:, :]))
                link(v.tensor_tensor(gate[:, :, :], gate[:, :, :], over(gsum[:, :], [P, NT * H, 3], 2), ALU.mult))
                link(v.tensor_tensor(csum[:, :, :], csum[:, :, :], csink[:, :, :], ALU.add))
                link(v.reciprocal(ccoef[:, :, :], csum[:, :, :]))
                gates = gate[:, :, :].rearrange("p (i h) c -> p i h c", i=NT)
                link(v.tensor_tensor(ccoef[:, :, :], ccoef[:, :, :], gates[:, :, :, 0], ALU.mult))
                cef = cexp[:, :, :, :].rearrange("p i h n -> p (i h) n")
                v.tensor_tensor(cef, cef, over(ccoef[:, :, :].rearrange("p i h -> p (i h)"), [P, NT * H, NBLK], 2), ALU.mult).then_inc(pc_ready.sem, 1)
                n = 0
                for pair in range(4):
                    for i in range(NT):
                        dve.wait_ge(s_psum.sem, s_psum.at(b, n + 1))
                        b0 = 3 * (n % 2)
                        quad, h0 = pair // 2, 2 * (pair % 2)
                        w = (i + 1) * P
                        lo, hi = (P, 2 * P) if i == 0 else (P // 2, 2 * P)
                        near = ps[:, b0 + 2, :].rearrange("p (h k) -> p h k", h=2)[:, :, lo:hi]
                        v.tensor_reduce(nmax[:, quad, i, 0, h0:h0 + 2], near, AX.X, ALU.max, negate=True)
                        v.tensor_reduce(nmax[:, quad, i, 1, h0:h0 + 2], ps[:, b0:b0 + 2, 0:w], AX.X, ALU.max, negate=True).then_inc(max_done.sem, 1)
                        n += 1
                dve.wait_ge(max_done.sem, max_done.at(b, 16))
                nm = nmax[:, :, :, :, :].rearrange("p a i k h -> p (a i k h)")
                link(v.tensor_scalar(nm, nm, SHIFT_CAP, None, ALU.min))
                link(v.tensor_copy(nmax_bf[:, :, 0], nm))
                link(v.tensor_tensor(nmax_bf[:, :, 1], nm, nmax_bf[:, :, 0], ALU.subtract))
                v.tensor_tensor(nm, nmax_bf[:, :, 0], nmax_bf[:, :, 1], ALU.add).then_inc(nmax_split.sem, 1)
                dve.wait_ge(shift_psum.sem, shift_psum.at(b, 1))
                v.tensor_tensor(shiftT[:, :, :], over(ps[:, 7, 0:P // 2].bitcast(BF16), [P, 4, P], 1),
                                over(con("shift_head"), [P, 4, P], 2), ALU.mult).then_inc(shift_ready.sem, 1)
                def nk(kind, quad):
                    return nmax[:, quad, :, kind, :]
                for quad in range(2):
                    hs = slice(4 * quad, 4 * quad + 4)
                    v.tensor_tensor(nfull[:, :, hs], nk(0, quad), nk(1, quad), ALU.min)
                    ins = v.scalar_tensor_tensor(nsink[:, :, hs], over(sink_sb[:, hs], [P, NT, 4], 1), -1.0, nk(0, quad), ALU.mult, ALU.min)
                link(ins)
                for quad in range(2):
                    hs = slice(4 * quad, 4 * quad + 4)
                    v.tensor_tensor(cargs[:, 0, :, hs], nfull[:, :, hs], nk(0, quad), ALU.subtract)
                    v.tensor_tensor(cargs[:, 1, :, hs], nfull[:, :, hs], nk(1, quad), ALU.subtract)
                    v.tensor_tensor(cargs[:, 2, :, hs], nsink[:, :, hs], nk(0, quad), ALU.subtract)
                v.tensor_tensor(cargs[:, 3, :, :], nsink[:, :, :], sink_b, ALU.add).then_inc(coef_arg.sem, 1)
                for g in range(8):
                    dve.wait_ge(pv_done.sem, pv_done.at(b, LAST_UNIT1[g]))
                    if g >= 2:
                        dve.wait_ge(on_psum.sem, on_psum.at(b, g - 1))
                    v.tensor_copy(oT[g % 2][0:OW, :, :], ps[0:OW, 4:6, :]).then_inc(oT_ready.sem, 1)
                    dve.wait_ge(on_psum.sem, on_psum.at(b, g + 1))
                    quad, i = g // NT, g % NT
                    v.tensor_copy(on[:, :, i, 4 * quad:4 * quad + 4, :].rearrange("p k h d -> p k (h d)"),
                                  ps[:, 6:8, 0:4 * OW]).then_inc(on_ready.sem, 1)
                dve.wait_ge(on_ready.sem, on_ready.at(b, 8))
                zn, zf = on[:, 0, :, :, D], on[:, 1, :, :, D]
                dve.wait_ge(coef_exp.sem, coef_exp.at(b, 1))
                v.tensor_tensor(zfull[:, :, :], cexps[:, 0, :, :], zn, ALU.mult)
                v.tensor_tensor(ztmp[:, :, :], cexps[:, 1, :, :], zf, ALU.mult)
                link(v.tensor_tensor(zwin[:, :, :], cexps[:, 2, :, :], zn, ALU.mult))
                v.tensor_tensor(zfull[:, :, :], zfull[:, :, :], ztmp[:, :, :], ALU.add)
                link(v.tensor_tensor(zwin[:, :, :], zwin[:, :, :], cexps[:, 3, :, :], ALU.add))
                v.reciprocal(zfull[:, :, :], zfull[:, :, :])
                link(v.reciprocal(zwin[:, :, :], zwin[:, :, :]))
                v.tensor_tensor(zfull[:, :, :], zfull[:, :, :], gates[:, :, :, 1], ALU.mult)
                link(v.tensor_tensor(zwin[:, :, :], zwin[:, :, :], gates[:, :, :, 2], ALU.mult))
                v.tensor_tensor(coef[:, 0, :, :], cexps[:, 0, :, :], zfull[:, :, :], ALU.mult)
                v.tensor_tensor(coef[:, 1, :, :], cexps[:, 1, :, :], zfull[:, :, :], ALU.mult)
                link(v.tensor_tensor(zwin[:, :, :], cexps[:, 2, :, :], zwin[:, :, :], ALU.mult))
                v.tensor_tensor(coef[:, 0, :, :], coef[:, 0, :, :], zwin[:, :, :], ALU.add).then_inc(coef_done.sem, 1)
                dve.wait_ge(coef_done.sem, coef_done.at(b, 1))
                for i in range(NT):
                    if i >= 2:
                        dve.wait_ge(mixT_psum.sem, mixT_psum.at(b, i - 1))
                    m = mixa[i % 2]
                    link(v.tensor_tensor(m[:, :, :], on[:, 1, i, :, 0:D], over(coef[:, 1, i, :], [P, H, D], 2), ALU.mult))
                    dve.wait_ge(comp_psum.sem, comp_psum.at(b, i + 1))
                    link(v.tensor_tensor(m[:, :, :], m[:, :, :], bank(i % 2).rearrange("p (h d) -> p h d", h=H), ALU.add))
                    dve.wait_ge(near_scaled.sem, near_scaled.at(b, i + 1))
                    v.tensor_tensor(m[:, :, :], m[:, :, :], mixb[i % 2][:, :, :], ALU.add).then_inc(mix_ready.sem, 1)
                dve.wait_ge(attn_psum.sem, attn_psum.at(b, 1))
                ao = lambda i: ps[:, 4, i * P:(i + 1) * P]
                mean_var(ao, 3)
                link(centred(x1, ao))
                link(v.tensor_tensor(x1[:, :, :], x1[:, :, :], xin[:, :, :], ALU.add))
                mean_var(lambda i: x1[:, i, :], 4)
                link(centred(ffn_in, lambda i: x1[:, i, :]))
                link(v.tensor_tensor(ms[:, :], rstd[:, 0:NT], rstd[:, 0:NT], ALU.mult))
                link(v.tensor_tensor(ms[:, :], ms[:, :], mv[:, :, 1], ALU.mult))
                v.tensor_scalar(var_in[:, 0:NT], ms[:, :], EPS5, None, ALU.add).then_inc(var_ready.sem, 1)
                dve.wait_ge(rstd_ready.sem, rstd_ready.at(b, 5))
                for i in range(NT):
                    ins = v.scalar_tensor_tensor(hn[:, i, :], ffn_in[:, i, :], rstd[:, i:i + 1], g1_sb[:, :], ALU.mult, ALU.mult)
                ins.then_inc(h2_ready.sem, 1)
                dve.wait_ge(qkv2_ready.sem, qkv2_ready.at(b, 1))
                cos2 = con("cos2").rearrange("p (i r) -> p i r", i=NT)
                sin2 = con("sin2").rearrange("p (i r) -> p i r", i=NT)
                pairs = qkv2[:, :, 0:2 * L2].rearrange("p i (h r c) -> p i h r c", r=2, c=2)
                for i in range(NT):
                    even, odd = pairs[:, i, :, :, 0], pairs[:, i, :, :, 1]
                    cb, sbb = over(cos2[:, i, :], [P, 2 * H2, 2], 1), over(sin2[:, i, :], [P, 2 * H2, 2], 1)
                    v.tensor_tensor(rot[0][:, i, :, :], even, cb, ALU.mult)
                    v.tensor_tensor(rot[1][:, i, :, :], odd, sbb, ALU.mult)
                    v.tensor_tensor(rot[2][:, i, :, :], even, sbb, ALU.mult)
                    ins = v.tensor_tensor(rot[3][:, i, :, :], odd, cb, ALU.mult)
                link(ins)
                for w in range(2):
                    hs = slice(w * H2, (w + 1) * H2)
                    dst = qk2[:, w, :, :].rearrange("p (i h) (r c) -> p i h r c", i=NT, r=2)
                    for i in range(NT):
                        v.tensor_tensor(dst[:, i, :, :, 0], rot[0][:, i, hs, :], rot[1][:, i, hs, :], ALU.subtract)
                        ins = v.tensor_tensor(dst[:, i, :, :, 1], rot[2][:, i, hs, :], rot[3][:, i, hs, :], ALU.add)
                link(ins)
                sl = ((0, 3, 6), (0, 1, 2))
                for lvl in range(3):
                    for w in range(2):
                        src = (qk2 if lvl == 0 else rem)[:, w, :, :]
                        ins = v.tensor_copy(parts2[:, w, :, sl[w][lvl], :], src)
                    link(ins)
                    if lvl < 2:
                        for w in range(2):
                            src = (qk2 if lvl == 0 else rem)[:, w, :, :]
                            ins = v.tensor_tensor(rem[:, w, :, :], src, parts2[:, w, :, sl[w][lvl], :], ALU.subtract)
                        link(ins)
                pq, pk = parts2[:, 0, :, :, :], parts2[:, 1, :, :, :]
                v.tensor_copy(pq[:, :, 1:3, :], over(pq[:, :, 0, :], [P, NT * H2, 2, D2], 2))
                v.tensor_copy(pq[:, :, 4:6, :], over(pq[:, :, 3, :], [P, NT * H2, 2, D2], 2))
                v.tensor_copy(pq[:, :, 7, :], pq[:, :, 6, :])
                v.tensor_copy(pk[:, :, 3:6, :], pk[:, :, 0:3, :])
                v.tensor_copy(pk[:, :, 6:8, :], pk[:, :, 0:2, :]).then_inc(parts2_ready.sem, 1)
                dve.wait_ge(k2T_psum.sem, k2T_psum.at(b, 1))
                kp = ps[:, 2:4, :].rearrange("p a n -> p (a n)").bitcast(BF16).rearrange("p (g n) -> p g n", g=4)
                for hh in range(4):
                    rows = slice(RW * hh, RW * (hh + 1))
                    ins = v.tensor_copy(k2Z[rows, :, hh, :], kp[rows, :, :])
                ins.then_inc(k2Z_ready.sem, 1)
                n = 0
                for g in range(4):
                    for i in range(NT):
                        dve.wait_ge(s2_psum.sem, s2_psum.at(b, n + 1))
                        b0 = 4 * (n % 2)
                        v.tensor_reduce(nmax2[:, 4 * g:4 * g + 4, i], ps[:, b0:b0 + 4, 0:(i + 1) * P], AX.X, ALU.max, negate=True).then_inc(max2_done.sem, 1)
                        n += 1
                dve.wait_ge(max2_done.sem, max2_done.at(b, 16))
                nm2 = nmax2[:, :, :].rearrange("p h i -> p (h i)")
                link(v.tensor_copy(nmax2_bf[:, :, 0], nm2))
                v.tensor_tensor(nmax2_bf[:, :, 1], nm2, nmax2_bf[:, :, 0], ALU.subtract).then_inc(nmax2_split.sem, 1)
                dve.wait_ge(shift2_psum.sem, shift2_psum.at(b, 1))
                v.tensor_tensor(shift2T[:, :, :], over(ps[:, 0, 0:P // 2].bitcast(BF16), [P, 4, P], 1),
                                over(con("shift2_tile"), [P, 4, P], 2), ALU.mult).then_inc(shift2_ready.sem, 1)
                for g in range(4):
                    dve.wait_ge(pv2_done.sem, pv2_done.at(b, 8 * (g + 1)))
                    v.tensor_copy(o2T[g % 2][:, :], bank(4 + g % 2)).then_inc(o2T_ready.sem, 1)
                    dve.wait_ge(o2n_psum.sem, o2n_psum.at(b, g + 1))
                    nat = bank(6 + g % 2).rearrange("p (i h r) -> p i h r", i=NT, h=4)
                    link(v.reciprocal(rz2[:, :, :], nat[:, :, :, D2]))
                    for i in range(NT):
                        ins = v.tensor_tensor(o2n[:, i, 4 * g:4 * g + 4, :], nat[:, i, :, 0:D2], over(rz2[:, i, :], [P, 4, D2], 2), ALU.mult)
                    ins.then_inc(o2n_ready.sem, 1)
                    dve.wait_ge(o2n_ready.sem, o2n_ready.at(b, g + 1))
                dve.wait_ge(up_psum.sem, up_psum.at(b, 1))
                v.tensor_tensor(res[:, :, :], ffn_in[:, :, :], bank(6).rearrange("p (i c) -> p i c", i=NT), ALU.add).then_inc(res_ready.sem, 1)
                dve.wait_ge(res_sq.sem, res_sq.at(b, 1))
                v.tensor_scalar(var_in[:, 0:NT], ms[:, :], 1.0 / HID, EPS5, ALU.mult, ALU.add).then_inc(var_ready.sem, 1)
                dve.wait_ge(rstd_ready.sem, rstd_ready.at(b, 6))
                for i in range(NT):
                    ins = v.scalar_tensor_tensor(hn[:, i, :], res[:, i, :], rstd[:, i:i + 1], g2_sb[:, :], ALU.mult, ALU.mult)
                ins.then_inc(t_ready.sem, 1)
                dve.wait_ge(router_psum.sem, router_psum.at(b, 1))
                link(v.tensor_copy(logit[:, :, :], ps[:, 2, 0:NT * E].rearrange("p (i e) -> p i e", i=NT)))
                shape = [P, NT, E]
                iota = over(con("iota8"), shape, 1)
                for top, hot in ((top1, hot1), (top2, hot2)):
                    link(v.tensor_reduce(top[:, :], logit[:, :, :], AX.X, ALU.max))
                    link(v.tensor_tensor(pick[:, :, :], logit[:, :, :], over(top[:, :], shape, 2), ALU.is_lt))
                    link(v.scalar_tensor_tensor(pick[:, :, :], pick[:, :, :], float(E), iota, ALU.mult, ALU.add))
                    link(v.tensor_reduce(ms[:, :], pick[:, :, :], AX.X, ALU.min))
                    link(v.tensor_tensor(hot[:, :, :], iota, over(ms[:, :], shape, 2), ALU.is_equal))
                    if hot is hot1:
                        link(v.scalar_tensor_tensor(logit[:, :, :], hot[:, :, :], -3.0e38, logit[:, :, :], ALU.mult, ALU.add))
                v.tensor_tensor(wtop[:, 0, :], top2[:, :], top1[:, :], ALU.subtract).then_inc(wtop_arg.sem, 1)
                dve.wait_ge(wtop_exp.sem, wtop_exp.at(b, 1))
                link(v.tensor_scalar(top1[:, :], wtop[:, 1, :], 1.0, 2.0, ALU.add, ALU.mult))
                link(v.reciprocal(top1[:, :], top1[:, :]))
                link(v.tensor_tensor(top2[:, :], top1[:, :], wtop[:, 1, :], ALU.mult))
                v.tensor_tensor(hot1[:, :, :], hot1[:, :, :], over(top1[:, :], shape, 2), ALU.mult)
                link(v.tensor_tensor(hot2[:, :, :], hot2[:, :, :], over(top2[:, :], shape, 2), ALU.mult))
                link(v.tensor_tensor(egate[:, :, :], hot1[:, :, :], hot2[:, :, :], ALU.add))

                def weigh(e):
                    dve.wait_ge(y_psum.sem, y_psum.at(b, e + 1))
                    if e >= 2:
                        dve.wait_ge(acc_done.sem, acc_done.at(b, e - 1))
                    v.tensor_tensor(yg[e % 2][:, :, :], bank(e % 2).rearrange("p (i c) -> p i c", i=NT),
                                    over(egate[:, :, e], [P, NT, HID], 2), ALU.mult).then_inc(yg_ready.sem, 1)

                for n in range(NX):
                    e, c = n // FC, n % FC
                    dve.wait_ge(th_ready.sem, th_ready.at(b, n + 1))
                    if c == 0 and e >= 2:
                        dve.wait_ge(y_psum.sem, y_psum.at(b, e - 1))
                    link(v.scalar_tensor_tensor(th[n % 2], th[n % 2], 1.0, bank(4 + 2 * c), ALU.add, ALU.mult))
                    v.tensor_tensor(hid[e % 2][:, c, :], th[n % 2][:, :], bank(5 + 2 * c), ALU.mult).then_inc(hid_ready.sem, 1)
                    if c == FC - 1 and e >= 1:
                        weigh(e - 1)
                weigh(E - 1)
                dve.wait_ge(acc_done.sem, acc_done.at(b, E))
                mean_var(lambda i: acc[:, i, :], 7)
                link(centred(acc, lambda i: acc[:, i, :]))
                v.tensor_tensor(yout[:, :, :], acc[:, :, :], x1[:, :, :], ALU.add).then_inc(out_ready.sem, 1)
                dve.wait_ge(out_ready.sem, out_ready.at(b, 1))
                dve.sem_inc(batch_done.sem, 1)
                assert n_chain[0] == VECTOR_STEPS

        @block.tensor
        def _(pe):
            mm, tr = nc.tensor.matmul, nc.tensor.transpose
            pe.wait_ge(loaded, 16 * N_LOADS)
            flat = ps[:, 0:2, :].rearrange("p a n -> p (a n)")
            for c in range(4):
                tr(flat[0:64, c * P:(c + 1) * P], w_og_sb[:, c, :], ident)
            tr(flat[0:L2, 4 * P:5 * P], w_down_sb[:, :], ident)
            tr(flat[0:32, 5 * P:6 * P], w_qc_sb[:, :], ident).then_inc(fold_psum, 1)
            pe.wait_ge(folded, 1)
            mm(bank(2), left_t[0:32, 5, :], w_qup_sb[:, :], start=True, stop=True)
            for c in range(4):
                mm(ps[:, 3, c * P:(c + 1) * P], left_t[:, c, :], w_out_sb[:, c // 2, :], start=True, stop=True)
            mm(ps[:, 4, 0:3 * L2], left_t[:, 4, :], w_qkv2_in[:, :, :].rearrange("p w n -> p (w n)"), start=True, stop=True).then_inc(fold_psum, 1)
            pe.wait_ge(folded, 4)
            pe.wait_ge(cast_done, 1)
            pe.wait_ge(padded, 3)

            with pe.Fori(0, n_batch) as b:

                pe.wait_ge(batch_done.sem, batch_done.at(b, 1))
                pe.wait_ge(h_ready.sem, h_ready.at(b, 1))
                for i in range(NT):
                    ins = tr(ps[:, 0, i * P:(i + 1) * P], hn[:, i, :], ident)
                ins.then_inc(hT_psum.sem, 1)
                pe.wait_ge(hT_ready.sem, hT_ready.at(b, 1))
                for i in range(NT):
                    if i >= 2:
                        pe.wait_ge(qkv_ready.sem, qkv_ready.at(b, i - 1))
                    b0 = 1 + 2 * (i % 2)
                    mm(bank(b0), hT[:, i * P:(i + 1) * P], w_proj[:, 0:H * D], start=True, stop=True)
                    mm(ps[:, b0 + 1, 0:2 * D], hT[:, i * P:(i + 1) * P], w_proj[:, H * D:], start=True, stop=True).then_inc(qkv_psum.sem, 1)
                for i in range(NT):
                    pe.wait_ge(split_ready.sem, split_ready.at(b, i + 1))
                    if i >= 2:
                        pe.wait_ge(qT_ready.sem, qT_ready.at(b, i - 1))
                    b0 = 6 if i % 2 == 0 else 4
                    for h in range(H):
                        ins = tr(ps[:, b0 + h // 4, (h % 4) * P:(h % 4 + 1) * P],
                                 qsplit[:, i, h, :, :].rearrange("p s d -> p (s d)"), ident)
                    ins.then_inc(qT_psum.sem, 1)
                    ins = tr(ps[:, 0, i * P:(i + 1) * P], kdup[:, i, :, :].rearrange("p s d -> p (s d)"), ident)
                ins.then_inc(kT_psum.sem, 1)
                pe.wait_ge(v_ready.sem, v_ready.at(b, 1))
                rows = con("mean_rows").rearrange("p (i r) -> p i r", i=NT)
                for i in range(NT):
                    ins = mm(ps[:, 1, 0:D], rows[:, i, :], va[:, i, 0:D], start=i == 0, stop=i == NT - 1)
                ins.then_inc(vmean_psum.sem, 1)
                pe.wait_ge(k_ready.sem, k_ready.at(b, 1))
                pe.wait_ge(qT_ready.sem, qT_ready.at(b, NT))
                for h in range(H):
                    r0 = RW * (h % 4)
                    ins = mm(ps[r0:r0 + RW, 2 + h // 4, :], comp_gate[:, :], qT[:, h, :, :].rearrange("p i n -> p (i n)").bitcast(F32), start=True, stop=True)
                    if h % 4 == 3:
                        ins.then_inc(cgT_psum.sem, 1)
                for quad in range(2):
                    pe.wait_ge(cgT_ready.sem, cgT_ready.at(b, quad + 1))
                    for i in range(NT):
                        ins = tr(ps[:, 4 + quad, i * P:(i + 1) * P], cgT[:, quad, i * P:(i + 1) * P], ident)
                    ins.then_inc(cg_psum.sem, 1)
                pe.wait_ge(vmean_ready.sem, vmean_ready.at(b, 1))
                pe.wait_ge(cg_ready.sem, cg_ready.at(b, 2))
                n = 0
                for pair in range(4):
                    for i in range(NT):
                        b0 = 3 * (n % 2)
                        if n >= 2:
                            pe.wait_ge(max_done.sem, max_done.at(b, n - 1))
                        w = (i + 1) * P
                        last = min(2 * P, w)
                        for hh in range(2):
                            q = qT[:, 2 * pair + hh, i, :]
                            mm(ps[:, b0 + hh, 0:w], q, kT_hi[:, 0:w], start=True, stop=False)
                            mm(ps[:, b0 + hh, w - last:w], ident_bf, con_bf("far_q")[:, 2 * P - last:], start=False, stop=True)
                            o = 2 * P * hh + 2 * P - last
                            mm(ps[:, b0 + 2, o:o + last], q, kT_hi[:, w - last:w], start=True, stop=False)
                            ins = mm(ps[:, b0 + 2, o:o + last], ident_bf, con_bf("near_q")[:, 2 * P - last:], start=False, stop=True)
                        ins.then_inc(s_psum.sem, 1)
                        n += 1
                pe.wait_ge(pc_ready.sem, pc_ready.at(b, 1))
                for i in range(NT):
                    ins = tr(ps[:, 6, i * P:(i + 1) * P], cexp[:, i, :, :].rearrange("p h n -> p (h n)"), ident)
                ins.then_inc(pcT_psum.sem, 1)
                pe.wait_ge(nmax_split.sem, nmax_split.at(b, 1))
                tr(ps[:, 7, 0:P // 2].bitcast(BF16), nmax_bf[:, :, :].rearrange("p n s -> p (n s)"), ident_bf).then_inc(shift_psum.sem, 1)
                pe.wait_ge(shift_ready.sem, shift_ready.at(b, 1))
                pe.wait_ge(pcT_ready.sem, pcT_ready.at(b, 1))
                pick1 = con_bf("shift_pick").rearrange("p (n r) -> p n r", n=16)

                def scores(u):
                    quad, i, blocks, _, _ = UNITS1[u]
                    if u >= 2:
                        pe.wait_ge(exp_done.sem, exp_done.at(b, u - 1))
                    at = 2 * (u % 2) * BANK
                    for kind, j, q0, nq, mask in blocks:
                        a, c = divmod(at, BANK)
                        dst = ps[:, a, c:c + 4 * nq].rearrange("p (h n) -> p h n", h=4)
                        q = qT[:, 4 * quad:4 * quad + 4, i, q0:q0 + nq]
                        keys = slice(j * P, (j + 1) * P)
                        mm(dst, kT_hi[:, keys], q, start=True, stop=False)
                        mm(dst, kT_lo[:, keys], q, start=False, stop=False)
                        if mask:
                            m = con_bf(mask)
                            if m.shape[1] > nq:
                                m = m[:, q0:q0 + nq]
                            mm(dst, ident_bf, m.unsqueeze(1).to_broadcast([P, 4, nq]), start=False, stop=False)
                        ins = mm(dst, pick1[:, (quad * 4 + i) * 2 + kind, :], shiftT[:, :, q0:q0 + nq], start=False, stop=True)
                        at += 4 * nq
                    ins.then_inc(st_psum.sem, 1)

                def natural(g):
                    pe.wait_ge(oT_ready.sem, oT_ready.at(b, g + 1))
                    if g >= 1:
                        pe.wait_ge(on_ready.sem, on_ready.at(b, g))
                    for kind in range(2):
                        for hh in range(4):
                            ins = tr(ps[:, 6 + kind, hh * OW:(hh + 1) * OW], oT[g % 2][0:OW, kind, hh * P:(hh + 1) * P], ident[0:OW, 0:OW])
                    ins.then_inc(on_psum.sem, 1)

                scores(0)
                for u in range(NU1):
                    if u + 1 < NU1:
                        scores(u + 1)
                    quad, i, blocks, first, last = UNITS1[u]
                    g = quad * NT + i
                    pe.wait_ge(exp_done.sem, exp_done.at(b, u + 1))
                    if first and g >= 1:
                        pe.wait_ge(oT_ready.sem, oT_ready.at(b, g))
                    at = 0
                    for kind, j, q0, nq, mask in blocks:
                        a, c = divmod(at, BANK)
                        at += 4 * nq
                        pr = probs[u % 2][:, a, c:c + 4 * nq].rearrange("p (h n) -> p h n", h=4)
                        dst = ps[0:OW, 4 + kind, :].rearrange("p (h n) -> p h n", h=4)[:, :, q0:q0 + nq]
                        starts = (kind, j) in ((0, i), (1, i))
                        ins = mm(dst, va[:, j, :], pr, start=starts, stop=True, skip_group_check=True)
                    ins.then_inc(pv_done.sem, 1)
                    if first and g >= 1:
                        natural(g - 1)
                natural(7)
                pe.wait_ge(on_ready.sem, on_ready.at(b, 8))

                def comp(i):
                    mm(bank(i % 2), pcT[:, i * P:(i + 1) * P], vmean[:, :, :].rearrange("p h d -> p (h d)"), start=True, stop=True).then_inc(comp_psum.sem, 1)

                comp(0)
                comp(1)
                for i in range(NT):
                    pe.wait_ge(mix_ready.sem, mix_ready.at(b, i + 1))
                    for c in range(4):
                        ins = tr(ps[:, 2 + i % 2, c * P:(c + 1) * P], mixa[i % 2][:, 2 * c:2 * c + 2, :].rearrange("p h d -> p (h d)"), ident)
                    ins.then_inc(mixT_psum.sem, 1)
                    if i + 2 < NT:
                        comp(i + 2)
                    pe.wait_ge(mixT_ready.sem, mixT_ready.at(b, i + 1))
                    for c in range(4):
                        ins = mm(ps[:, 4, i * P:(i + 1) * P], mixT[i % 2][:, c, :], w_fold[:, c, :], start=c == 0, stop=c == 3)
                ins.then_inc(attn_psum.sem, 1)
                pe.wait_ge(h2_ready.sem, h2_ready.at(b, 1))
                for i in range(NT):
                    ins = tr(ps[:, 5, i * P:(i + 1) * P], hn[:, i, :], ident)
                ins.then_inc(h2T_psum.sem, 1)
                pe.wait_ge(h2T_ready.sem, h2T_ready.at(b, 1))
                for i in range(NT):
                    o = (i % 2) * 3 * L2
                    ins = mm(ps[:, 6 + i // 2, o:o + 3 * L2], hT[:, i * P:(i + 1) * P], w_qkv2[:, :], start=True, stop=True)
                ins.then_inc(qkv2_psum.sem, 1)
                pe.wait_ge(parts2_ready.sem, parts2_ready.at(b, 1))
                for w in range(2):
                    for g in range(4):
                        for i in range(NT):
                            src = parts2[:, w, i * H2 + 4 * g:i * H2 + 4 * g + 4, :, :].rearrange("p h s d -> p (h s d)")
                            o = ((g % 2) * NT + i) * P // 2
                            ins = tr(ps[:, 2 * w + g // 2, o:o + P // 2].bitcast(BF16), src, ident_bf)
                    ins.then_inc((k2T_psum if w else q2T_psum).sem, 1)
                pe.wait_ge(q2T_ready.sem, q2T_ready.at(b, 1))
                pe.wait_ge(k2Z_ready.sem, k2Z_ready.at(b, 1))
                n = 0
                for g in range(4):
                    for i in range(NT):
                        if n >= 2:
                            pe.wait_ge(max2_done.sem, max2_done.at(b, n - 1))
                        w = (i + 1) * P
                        for hh in range(4):
                            dst = ps[:, 4 * (n % 2) + hh, :]
                            mm(dst[:, 0:w], q2T[:, g, i * P:w], k2Z[:, g, hh, 0:w], start=True, stop=False)
                            ins = mm(dst[:, w - P:w], ident_bf, con_bf("causal_q"), start=False, stop=True)
                        ins.then_inc(s2_psum.sem, 1)
                        n += 1
                pe.wait_ge(nmax2_split.sem, nmax2_split.at(b, 1))
                tr(ps[:, 0, 0:P // 2].bitcast(BF16), nmax2_bf[:, :, :].rearrange("p n s -> p (n s)"), ident_bf).then_inc(shift2_psum.sem, 1)
                pe.wait_ge(shift2_ready.sem, shift2_ready.at(b, 1))
                pe.wait_ge(va2_ready.sem, va2_ready.at(b, 1))
                pick2 = con_bf("shift2_pick").rearrange("p (n r) -> p n r", n=H2)

                def scores2(u):
                    g, j, half = UNITS2[u]
                    if u >= 2:
                        pe.wait_ge(exp2_done.sem, exp2_done.at(b, u - 1))
                    for s in range(2):
                        hh = 2 * half + s
                        dst = ps[:, 2 * (u % 2) + s, 0:T - j * P]
                        mm(dst, k2Z[:, g, hh, j * P:(j + 1) * P], q2T[:, g, j * P:], start=True, stop=False)
                        mm(dst, pick2[:, 4 * g + hh, :], shift2T[:, j:, :].rearrange("p i n -> p (i n)"), start=False, stop=False)
                        ins = mm(dst[:, 0:P], ident_bf, con_bf("causal_k"), start=False, stop=True)
                    ins.then_inc(st2_psum.sem, 1)

                def natural2(g):
                    pe.wait_ge(o2T_ready.sem, o2T_ready.at(b, g + 1))
                    for i in range(NT):
                        ins = tr(ps[:, 6 + g % 2, i * P:(i + 1) * P], o2T[g % 2][:, i * P:(i + 1) * P], ident)
                    ins.then_inc(o2n_psum.sem, 1)

                scores2(0)
                for u in range(NU2):
                    if u + 1 < NU2:
                        scores2(u + 1)
                    g, j, half = UNITS2[u]
                    pe.wait_ge(exp2_done.sem, exp2_done.at(b, u + 1))
                    if j == 0 and half == 0 and g >= 2:
                        pe.wait_ge(o2T_ready.sem, o2T_ready.at(b, g - 1))
                    for s in range(2):
                        hh = 2 * half + s
                        ins = mm(ps[RW * hh:RW * (hh + 1), 4 + g % 2, j * P:], va2[:, j, 4 * g + hh, :], probs[u % 2][:, s, 0:T - j * P],
                                 start=j == 0, stop=True, skip_group_check=True)
                    ins.then_inc(pv2_done.sem, 1)
                    if j == 0 and half == 1 and g >= 1:
                        natural2(g - 1)
                natural2(3)
                pe.wait_ge(o2n_ready.sem, o2n_ready.at(b, 4))
                for i in range(NT):
                    ins = tr(ps[:, 4, i * P:(i + 1) * P], o2n[:, i, :, :].rearrange("p h d -> p (h d)"), ident)
                ins.then_inc(o2nT_psum.sem, 1)
                pe.wait_ge(o2nT_ready.sem, o2nT_ready.at(b, 1))
                for i in range(NT):
                    ins = mm(ps[:, 6, i * P:(i + 1) * P], o2nT[:, i * P:(i + 1) * P], w_up_sb[:, :], start=True, stop=True)
                ins.then_inc(up_psum.sem, 1)
                pe.wait_ge(t_ready.sem, t_ready.at(b, 1))
                for i in range(NT):
                    ins = tr(ps[:, 1, i * P:(i + 1) * P], hn[:, i, :], ident)
                ins.then_inc(tT_psum.sem, 1)
                pe.wait_ge(tT_ready.sem, tT_ready.at(b, 1))
                for i in range(NT):
                    ins = mm(ps[:, 2, i * E:(i + 1) * E], tT[:, i * P:(i + 1) * P], router_sb[:, :], start=True, stop=True)
                ins.then_inc(router_psum.sem, 1)

                def hidden(n):
                    e, c = n // FC, n % FC
                    if n >= FC:
                        pe.wait_ge(hid_ready.sem, hid_ready.at(b, n - FC + 1))
                    for k in range(2):
                        ins = mm(bank(4 + 2 * c + k), w13_sb[:, e, k, c * P:(c + 1) * P], tT[:, :], start=True, stop=True)
                    ins.then_inc(hid_psum.sem, 1)

                hidden(0)
                hidden(1)
                for e in range(E):
                    if e + 1 < E:
                        hidden(FC * (e + 1))
                    pe.wait_ge(hid_ready.sem, hid_ready.at(b, FC * (e + 1)))
                    if e + 1 < E:
                        hidden(FC * (e + 1) + 1)
                    if e >= 2:
                        pe.wait_ge(yg_ready.sem, yg_ready.at(b, e - 1))
                    for i in range(NT):
                        for c in range(FC):
                            ins = mm(ps[:, e % 2, i * P:(i + 1) * P], hid[e % 2][:, c, i * P:(i + 1) * P], w2_sb[:, e, c, :], start=c == 0, stop=c == FC - 1)
                    ins.then_inc(y_psum.sem, 1)
                pe.wait_ge(y_psum.sem, y_psum.at(b, E))
                pe.sem_inc(batch_done.sem, 1)


N_LOADS = 26
VECTOR_STEPS = 101

_INS = ['L0_attn_h', 'L0_attn_w_qc', 'L0_attn_w_qup', 'L0_attn_w_k', 'L0_attn_w_v', 'L0_attn_g_qnorm', 'L0_attn_g_knorm',
        'L0_attn_w_gate', 'L0_attn_b_gate', 'L0_attn_sink_logit', 'L0_attn_w_out_group', 'L0_attn_w_out',
        'L0_ffn_g1', 'L0_ffn_g2', 'L0_ffn_w_down', 'L0_ffn_wq', 'L0_ffn_wk', 'L0_ffn_wv', 'L0_ffn_w_up',
        'L0_ffn_router_w', 'L0_ffn_w1', 'L0_ffn_w2', 'L0_ffn_w3']


def kernel(**inputs):
    import concourse.bacc as bacc
    from concourse.bass_utils import run_bass_kernel_spmd

    nc = bacc.Bacc("TRN2", target_bir_lowering=False, num_devices=1)
    arrays, args = {}, []
    for name in _INS:
        a = np.ascontiguousarray(inputs[name])
        arrays[f"in_{name}"] = a
        args.append(nc.dram_tensor(f"in_{name}", a.shape, mybir.dt.from_np(a.dtype), kind="ExternalInput").ap())
    arrays["shape_constants"] = CONSTS
    arrays["shape_constants_bf16"] = CONSTS_BF
    args.append(nc.dram_tensor("shape_constants", CONSTS.shape, F32, kind="ExternalInput").ap())
    args.append(nc.dram_tensor("shape_constants_bf16", CONSTS_BF.shape, BF16, kind="ExternalInput").ap())
    args.append(nc.dram_tensor("out", (B, T, HID), F32, kind="ExternalOutput").ap())
    sandwich(nc, *args)
    r = run_bass_kernel_spmd(nc, [arrays], core_ids=[0])
    return r.results[0]["out"]
```

```python
import concourse.bass as bass
from concourse import mybir
from contextlib import ExitStack
import numpy as np

F32 = mybir.dt.float32
F32R = mybir.dt.float32r
BF16 = mybir.dt.bfloat16
ALU = mybir.AluOpType
ACT = mybir.ActivationFunctionType
AX = mybir.AxisListType

B, T, HID = 8, 512, 128
P = 128
NT = T // P
H, D, ROPE = 8, 64, 32
CR, WINDOW = 32, 64
NBLK = T // CR
H2, D2, L2 = 16, 4, 64
E, F = 8, 256
FC = F // P
BANK = 512
NEG = -1.0e30
SHIFT_CAP = 1.0e20
EPS5, EPS6 = 1e-5, 1e-6
SPLIT2 = 8
OW = D + 1
RW = 32

CONST_COLS = {}


def shape_constants():
    p = np.arange(P)
    cols, at = [], 0

    def add(name, a):
        nonlocal at
        a = np.asarray(a, np.float32).reshape(P, -1)
        CONST_COLS[name] = (at, a.shape[1])
        cols.append(a)
        at += a.shape[1]

    def rope(width, theta=10000.0):
        half = width // 2
        inv = (np.float32(1.0) / np.power(np.float32(theta), np.arange(half, dtype=np.float32) * np.float32(2.0) / np.float32(width))).astype(np.float32)
        ang = (np.arange(T, dtype=np.float32)[:, None] * inv[None, :]).astype(np.float32)
        ang = ang.reshape(NT, P, half).transpose(1, 0, 2)
        return np.cos(ang.astype(np.float64)), np.sin(ang.astype(np.float64))

    c, s = rope(ROPE)
    add("cos1", np.repeat(c[:, :, None, :], 2, axis=2))
    add("sin1", np.repeat(s[:, :, None, :], 2, axis=2))
    c, s = rope(D2)
    add("cos2", c)
    add("sin2", s)
    add("ident", np.eye(P))
    q, k = p[:, None], p[None, :]
    neg = lambda ok: np.where(ok, 0.0, NEG)
    back = np.concatenate([q + P - k, q - k], 1)
    add("near_q", neg((back >= 0) & (back < WINDOW)))
    add("far_q", neg(back >= WINDOW))
    add("causal_q", neg(q - k >= 0))
    kk, qq = p[:, None], p[None, :]
    add("near_own_k", neg((qq - kk >= 0) & (qq - kk < WINDOW)))
    add("near_prev_k", neg(qq + P - kk < WINDOW)[:, :P // 2])
    add("far_own_k", neg(qq - kk >= WINDOW))
    add("far_prev_k", neg(qq + P - kk >= WINDOW))
    add("causal_k", neg(qq - kk >= 0))
    tok = np.arange(NT)[None, :, None] * P + p[:, None, None]
    add("block_valid", neg((np.arange(NBLK)[None, None, :] + 1) * CR - 1 <= tok))
    blk = (np.arange(NT)[None, :, None] * P + p[:, None, None]) // CR
    add("mean_rows", (blk == (np.arange(P) % NBLK)[None, None, :]) / CR)
    add("head_rows", (p[:, None] // NBLK) == np.arange(H)[None, :])
    row = p
    quad, tile, kind, head = row // 64, row // 16 % 4, row // 8 % 2, row // 2 % 4
    add("shift_head", head[:, None] == np.arange(4)[None, :])
    add("shift_pick", np.repeat(((quad * 4 + tile) * 2 + kind)[:, None, None] == np.arange(16)[None, :, None], P, axis=2))
    add("shift2_tile", (row // 2 % 4)[:, None] == np.arange(4)[None, :])
    add("shift2_pick", np.repeat((row // 8)[:, None, None] == np.arange(H2)[None, :, None], P, axis=2))
    add("iota8", np.tile(np.arange(E, dtype=np.float32), (P, 1)))
    narrow, wide = [], []
    for (name, (at, n)), a in zip(list(CONST_COLS.items()), cols):
        if name in BF_CONSTS:
            BF_COLS[name] = (sum(c.shape[1] for c in narrow), n)
            narrow.append(a)
        if name not in BF_CONSTS or name == "ident":
            CONST_COLS[name] = (sum(c.shape[1] for c in wide), n)
            wide.append(a)
    return np.concatenate(wide, 1), np.concatenate(narrow, 1).astype(mybir.dt.np(BF16))


BF_COLS = {}
BF_CONSTS = ["ident", "near_q", "far_q", "causal_q", "near_own_k", "near_prev_k", "far_own_k",
             "far_prev_k", "causal_k", "shift_pick", "shift2_pick"]
CONSTS, CONSTS_BF = shape_constants()


class Signal:

    def __init__(self, sem, per):
        self.sem, self.per, self.given = sem, per, 0

    def at(self, b, n):
        assert 0 <= n <= self.per
        return b * self.per + n


def sandwich(nc, x, w_qc, w_qup, w_k, w_v, g_q, g_k, w_gate, b_gate, sink, w_og, w_out,
             g1, g2, w_down, wq2, wk2, wv2, w_up, router_w, w1, w2, w3, consts, consts_bf, out, n_batch=B):
    ctx = ExitStack()
    with ctx:
        def sb(name, shape, dt=F32):
            return ctx.enter_context(nc.sbuf_tensor(name, shape, dt))

        def sem(name):
            return ctx.enter_context(nc.semaphore(name))

        def signal(name, per):
            return Signal(sem(name), per)

        ncols = CONSTS.shape[1]
        cst = sb("cst", [P, ncols])
        cst_bf = sb("cst_bf", [P, CONSTS_BF.shape[1]], BF16)

        def con(name):
            a, n = CONST_COLS[name]
            return cst[:, a:a + n]

        def con_bf(name):
            a, n = BF_COLS[name]
            return cst_bf[:, a:a + n]

        ident, ident_bf = con("ident"), con_bf("ident")
        w_qc_sb = sb("w_qc_sb", [HID, 32])
        w_out_sb = sb("w_out_sb", [64, 2, HID])
        w_down_sb = sb("w_down_sb", [HID, L2])
        w_proj = sb("w_proj", [HID, H * D + 2 * D])
        w_fold = sb("w_fold", [P, 4, HID])
        w_qkv2 = sb("w_qkv2", [HID, 3 * L2])
        w_up_sb = sb("w_up_sb", [P, HID])
        router_sb = sb("router_sb", [HID, E])
        w13_sb = sb("w13_sb", [HID, E, 2, F])
        w2_sb = sb("w2_sb", [P, E, FC, HID])
        gain1 = sb("gain1", [P, H + 1, D])
        gain_in = sb("gain_in", [P, 2, D])
        g1_sb = sb("g1_sb", [P, HID])
        g2_sb = sb("g2_sb", [P, HID])
        bgate_sb = sb("bgate_sb", [P, 3])
        sink_sb = sb("sink_sb", [P, H])
        minus_half = sb("minus_half", [P, NT * (H + 1)])

        xin = sb("xin", [P, NT, HID])
        hn = sb("hn", [P, NT, HID])
        hT = sb("hT", [HID, T])
        stats = sb("stats", [P, NT, 6])
        mv = sb("mv", [P, NT, 2])
        var_in = sb("var_in", [P, NT * (H + 1)])
        rstd = sb("rstd", [P, NT * (H + 1)])
        qkv = sb("qkv", [P, NT, H + 2, D])
        sq = sb("sq", [P, H + 1, D])
        sumsq = sb("sumsq", [P, NT, H + 1])
        ropeA = sb("ropeA", [P, H + 1, ROPE])
        ropeB = sb("ropeB", [P, H + 1, ROPE])
        qsplit = sb("qsplit", [P, NT, H, 2, D])
        kdup = sb("kdup", [P, NT, 2, D])
        qT = sb("qT", [P, H, NT, P], F32R)
        kT_hi = sb("kT_hi", [P, T], F32R)
        kT_lo = sb("kT_lo", [P, T], F32R)
        va = sb("va", [P, NT, OW])
        comp_gate = sb("comp_gate", [P, RW])
        kmean = sb("kmean", [P, NBLK])
        vmean = sb("vmean", [P, H, D])
        cgT = sb("cgT", [P, 2, T])
        cg = sb("cg", [P, NT, H, RW])
        cs = sb("cs", [P, NT, H, NBLK])
        cexp = cs
        cmax = sb("cmax", [P, NT, H])
        csum = sb("csum", [P, NT, H])
        csink = sb("csink", [P, NT, H])
        ccoef = sb("ccoef", [P, NT, H])
        gz = sb("gz", [P, NT * H, 3])
        gate = sb("gate", [P, NT * H, 3])
        gsum = sb("gsum", [P, NT * H])
        pcT = sb("pcT", [P, T])
        nmax = sb("nmax", [P, 2, NT, 2, 4])
        nmax_bf = sb("nmax_bf", [P, 64, 2], BF16)
        shiftT = sb("shiftT", [P, 4, P], BF16)
        prob_pairs = [sb(f"prob_pair{i}", [P, 2, BANK]) for i in range(2)]
        oT = [sb(f"oT{i}", [P, 2, BANK]) for i in range(2)]
        probs = [prob_pairs[n // 2][:, n % 2, :] for n in range(4)]
        left_t = prob_pairs[0][0:64, :, :].rearrange("p a n -> p (a n)")[:, 0:6 * P].rearrange("p (c n) -> p c n", c=6)
        w_qup_sb = prob_pairs[1][0:32, 0, 0:H * D]
        w_og_sb = prob_pairs[1][:, 1, 0:4 * 64].rearrange("p (c n) -> p c n", c=4)
        w_qkv2_in = prob_pairs[1][0:L2, 1, 4 * 64:4 * 64 + 3 * L2].rearrange("p (w n) -> p w n", w=3)
        on = sb("on", [P, 2, NT, H, OW])
        cargs = sb("cargs", [P, 4, NT, H])
        cexps = sb("cexps", [P, 4, NT, H])
        nfull = sb("nfull", [P, NT, H])
        nsink = sb("nsink", [P, NT, H])
        zfull = sb("zfull", [P, NT, H])
        zwin = sb("zwin", [P, NT, H])
        ztmp = sb("ztmp", [P, NT, H])
        coef = sb("coef", [P, 2, NT, H])
        spare_s = qsplit[:, :, :, :, :].rearrange("p i h s d -> p (i h s d)")
        mixa, mixb = ([spare_s[:, (2 * m + n) * H * D:(2 * m + n + 1) * H * D].rearrange("p (h d) -> p h d", h=H)
                       for n in range(2)] for m in range(2))
        mixT = [spare_s[:, (4 + n) * H * D:(5 + n) * H * D].rearrange("p (c n) -> p c n", c=4) for n in range(2)]
        x1 = sb("x1", [P, NT, HID])
        ffn_in = sb("ffn_in", [P, NT, HID])
        ms = sb("ms", [P, NT])
        scrap = sb("scrap", [P, 1])
        qkv2 = sb("qkv2", [P, NT, 3 * L2])
        n_parts = NT * H2 * SPLIT2 * D2
        parts2 = spare_s[:, 0:n_parts].bitcast(BF16).rearrange("p (w n s d) -> p w n s d", w=2, s=SPLIT2, d=D2)
        n_rot = NT * 2 * H2 * 2
        rot = [spare_s[:, n_parts + n * n_rot:n_parts + (n + 1) * n_rot].rearrange("p (i h r) -> p i h r", i=NT, r=2) for n in range(4)]
        at = n_parts + 4 * n_rot
        n_qk = 2 * NT * L2
        qk2 = spare_s[:, at:at + n_qk].rearrange("p (w n d) -> p w n d", w=2, d=D2)
        rem = spare_s[:, at + n_qk:at + 2 * n_qk].rearrange("p (w n d) -> p w n d", w=2, d=D2)
        q2T = sb("q2T", [P, 4, T], BF16)
        k2Z = sb("k2Z", [P, 4, 4, T], BF16)
        va2 = sb("va2", [P, NT, H2, RW])
        nmax2 = sb("nmax2", [P, H2, NT])
        nmax2_bf = sb("nmax2_bf", [P, 64, 2], BF16)
        shift2T = sb("shift2T", [P, 4, P], BF16)
        probs2 = probs + [oT[n][:, 1, :] for n in range(2)]
        o2T = [oT[n][:, 0, :] for n in range(2)]
        rz2 = sb("rz2", [P, NT, 4])
        o2n = sb("o2n", [P, NT, 2 * H2, D2])
        o2nT = spare_s[:, 0:T]
        t_sb = spare_s[:, T:2 * T].rearrange("p (i c) -> p i c", i=NT)
        res = sb("res", [P, NT, HID])
        tT = sb("tT", [HID, T])
        logit = sb("logit", [P, NT, E])
        top1 = sb("top1", [P, NT])
        top2 = sb("top2", [P, NT])
        pick = sb("pick", [P, NT, E])
        hot1 = sb("hot1", [P, NT, E])
        hot2 = sb("hot2", [P, NT, E])
        wtop = sb("wtop", [P, 2, NT])
        egate = sb("egate", [P, NT, E])
        spare = on[:, :, :, :, :].rearrange("p k i h d -> p (k i h d)")
        hid = [spare[:, n * FC * T:(n + 1) * FC * T].rearrange("p (c t) -> p c t", c=FC) for n in range(2)]
        th = [spare[:, (2 * FC + n) * T:(2 * FC + n + 1) * T] for n in range(2)]
        spare_q = qkv[:, :, :, :].rearrange("p i h d -> p (i h d)")
        yg = [spare_q[:, n * T:(n + 1) * T].rearrange("p (i c) -> p i c", i=NT) for n in range(2)]
        acc = spare_q[:, 2 * T:3 * T].rearrange("p (i c) -> p i c", i=NT)
        yout = spare_q[:, 3 * T:4 * T].rearrange("p (i c) -> p i c", i=NT)

        ps = ctx.enter_context(nc.psum_tensor("ps", [P, 8, BANK], F32))

        def bank(n, k=1):
            return ps[:, n:n + k, :] if k > 1 else ps[:, n, :]

        loaded = sem("loaded")
        cast_done = sem("cast_done")
        folded = sem("folded")
        fold_psum = sem("fold_psum")
        padded = sem("padded")
        slot_done = sem("slot_done")
        x_loaded = signal("x_loaded", 16)
        x_again = signal("x_again", 16)
        var1_ready = signal("var1_ready", 2)
        rstd1_ready = signal("rstd1_ready", 2)
        var2_ready = signal("var2_ready", 3)
        rstd2_ready = signal("rstd2_ready", 3)
        var3_ready = signal("var3_ready", 2)
        rstd3_ready = signal("rstd3_ready", 2)
        h_ready = signal("h_ready", 1)
        hT_psum = signal("hT_psum", 1)
        hT_ready = signal("hT_ready", 1)
        kv_psum = signal("kv_psum", 1)
        kv_ready = signal("kv_ready", 1)
        qkv_psum = signal("qkv_psum", NT)
        qkv_ready = signal("qkv_ready", NT)
        sq_ready = signal("sq_ready", NT)
        sq_used = signal("sq_used", NT)
        rope_done = signal("rope_done", NT)
        gained = signal("gained", NT)
        v_ready = signal("v_ready", 1)
        split_ready = signal("split_ready", NT)
        qT_psum = signal("qT_psum", 2 * NT)
        qT_ready = signal("qT_ready", 2 * NT)
        kT_psum = signal("kT_psum", 1)
        k_ready = signal("k_ready", 1)
        vmean_psum = signal("vmean_psum", 1)
        vmean_ready = signal("vmean_ready", 1)
        cgT_psum = signal("cgT_psum", 2)
        cgT_ready = signal("cgT_ready", 2)
        cg_psum = signal("cg_psum", 2)
        cg_ready = signal("cg_ready", 2)
        cexp_arg = signal("cexp_arg", 1)
        cexp_ready = signal("cexp_ready", 1)
        pc_ready = signal("pc_ready", 1)
        pcT_psum = signal("pcT_psum", 1)
        pcT_ready = signal("pcT_ready", 1)
        s_psum = signal("s_psum", NT * H)
        near_max = signal("near_max", NT * H)
        max_done = signal("max_done", NT * H)
        nmax_split = signal("nmax_split", 1)
        shift_psum = signal("shift_psum", 1)
        shift_ready = signal("shift_ready", 1)
        coef_arg = signal("coef_arg", 1)
        coef_exp = signal("coef_exp", 1)
        coef_done = signal("coef_done", 1)
        NU1 = 28
        st_psum = signal("st_psum", NU1)
        exp_done = signal("exp_done", NU1)
        pv_done = signal("pv_done", NU1)
        oT_ready = signal("oT_ready", 8)
        on_psum = signal("on_psum", 16)
        on_ready = signal("on_ready", 16)
        comp_psum = signal("comp_psum", NT)
        near_scaled = signal("near_scaled", NT)
        mix_ready = signal("mix_ready", NT)
        mixT_psum = signal("mixT_psum", NT)
        mixT_ready = signal("mixT_ready", NT)
        mixT_used = signal("mixT_used", NT)
        attn_ready = signal("attn_ready", 1)
        x1_ready = signal("x1_ready", 1)
        h2_ready = signal("h2_ready", 1)
        h2T_psum = signal("h2T_psum", 1)
        h2T_ready = signal("h2T_ready", 1)
        qkv2_psum = signal("qkv2_psum", 1)
        qkv2_ready = signal("qkv2_ready", 1)
        va2_ready = signal("va2_ready", 1)
        parts2_ready = signal("parts2_ready", 1)
        q2T_psum = signal("q2T_psum", 2)
        q2T_ready = signal("q2T_ready", 2)
        k2T_psum = signal("k2T_psum", 2)
        k2Z_low = signal("k2Z_low", 2)
        k2Z_high = signal("k2Z_high", 2)
        UNITS_MAX2 = [(g, i, hh, n) for g in range(4) for i in range(NT)
                      for n in [{0: 4, 1: 2}.get(i, 1)] for hh in range(0, 4, n)]
        s2_psum = signal("s2_psum", len(UNITS_MAX2))
        max2_done = signal("max2_done", len(UNITS_MAX2))
        nmax2_split = signal("nmax2_split", 1)
        shift2_psum = signal("shift2_psum", 1)
        shift2_ready = signal("shift2_ready", 1)
        NU2 = 4 * NT * 4
        st2_psum = signal("st2_psum", NU2)
        exp2_done = signal("exp2_done", NU2)
        pv2_done = signal("pv2_done", NU2 // 4)
        o2T_ready = signal("o2T_ready", 4)
        o2n_psum = signal("o2n_psum", 4)
        o2n_ready = signal("o2n_ready", 4)
        o2nT_psum = signal("o2nT_psum", 1)
        o2nT_ready = signal("o2nT_ready", 1)
        up_psum = signal("up_psum", 1)
        res_ready = signal("res_ready", 1)
        res_sq = signal("res_sq", 1)
        t_ready = signal("t_ready", 1)
        tT_psum = signal("tT_psum", 1)
        tT_ready = signal("tT_ready", 1)
        router_psum = signal("router_psum", 1)
        wtop_arg = signal("wtop_arg", 1)
        wtop_exp = signal("wtop_exp", 1)
        NX = E * FC
        hid_psum = signal("hid_psum", NX)
        th_ready = signal("th_ready", NX)
        hid_ready = signal("hid_ready", NX)
        y_psum = signal("y_psum", E)
        yg_ready = signal("yg_ready", E)
        acc_done = signal("acc_done", E)
        out_ready = signal("out_ready", 1)
        out_stored = signal("out_stored", 16)
        vector_chain = sem("vector_chain")

        def units1(i):
            near, far = 0, 1
            own = (near, i, 0, P, "near_own_k")
            if i == 0:
                return [[own], [(far, 0, 0, P, "far_own_k")]]
            return [[own],
                    [(near, i - 1, 0, P // 2, "near_prev_k"), (far, i, P // 2, P // 2, "far_own_k")],
                    [(far, i - 1, 0, P, "far_prev_k")]] + [[(far, j, 0, P, None)] for j in range(i - 1)]

        UNITS1 = [(quad, i, u, n) for quad in range(2) for i in range(NT) for n, u in enumerate(units1(i))]
        assert len(UNITS1) == NU1
        FIRST1 = [u for u in range(NU1) if UNITS1[u][3] == 0] + [NU1]

        def spread(*stages):
            marks = [(lo + (hi - lo) * (k + 0.5) / n, name) for name, n, lo, hi in stages for k in range(n)]
            return [name for _, name in sorted(marks, key=lambda m: m[0])]

        STEPS = {"attention": NU1 + 4, "prepare2": 15, "maxima2": len(UNITS_MAX2) + 3,
                 "mix": 8, "prepare1": 19, "attention2": NU2 + 4,
                 "maxima1": NT * H + 4, "after2": 10, "experts": 4 * E + 8}
        SLOTS = [
            spread(("attention", STEPS["attention"], 0, 1), ("prepare2", STEPS["prepare2"], 0, 0.45),
                   ("maxima2", STEPS["maxima2"], 0.45, 1)),
            spread(("prepare1", 2, 0, 0.04), ("mix", STEPS["mix"], 0.03, 0.38),
                   ("prepare1", STEPS["prepare1"] - 2, 0.38, 1), ("attention2", STEPS["attention2"], 0.01, 1)),
            spread(("maxima1", STEPS["maxima1"], 0, 0.97), ("after2", STEPS["after2"], 0, 0.25),
                   ("experts", STEPS["experts"], 0.15, 1)),
        ]
        SLOTS_ENGINES = 4

        def take(slot, **stages):
            for name in SLOTS[slot]:
                if name in stages:
                    next(stages[name])
            for name, stage in stages.items():
                assert next(stage, "end") == "end", name

        def slots_before(b, slot):
            return 3 * (b + 1) + slot - 1

        def in_range(b):
            return not isinstance(b, int) or 0 <= b < n_batch

        def is_first(b):
            return isinstance(b, int) and b == 0

        block = ctx.enter_context(nc.Block())

        def row_bcast(v, n):
            return v.rearrange("(a n) -> a n", a=1).partition_broadcast(P)

        @block.sync
        def _(sync):
            loads = [
                (cst[:, :], consts), (cst_bf[:, :], consts_bf), (w_qc_sb[:, :], w_qc), (w_qup_sb[:, :], w_qup),
                (w_og_sb[:, 0:2, :], w_og[0, :, :].rearrange("(c p) n -> p c n", p=P)),
                (w_og_sb[:, 2:4, :], w_og[1, :, :].rearrange("(c p) n -> p c n", p=P)),
                (w_out_sb[:, :, :], w_out.rearrange("(g p) n -> p g n", p=64)),
                (w_down_sb[:, :], w_down),
                (w_qkv2_in[:, 0, :], wq2), (w_qkv2_in[:, 1, :], wk2), (w_qkv2_in[:, 2, :], wv2),
                (w_proj[:, H * D:H * D + D], w_k), (w_proj[:, H * D + D:], w_v),
                (w_up_sb[0:L2, :], w_up), (router_sb[:, :], router_w),
                (gain_in[:, 0, :], row_bcast(g_q, D)), (gain_in[:, 1, :], row_bcast(g_k, D)),
                (g1_sb[:, :], row_bcast(g1, HID)), (g2_sb[:, :], row_bcast(g2, HID)),
                (bgate_sb[:, :], row_bcast(b_gate, 3)), (sink_sb[:, :], row_bcast(sink, H)),
                (comp_gate[0:D, NBLK:NBLK + 3], w_gate), (comp_gate[D:P, NBLK:NBLK + 3], w_gate),
                (w13_sb[:, :, 0, :], w1.rearrange("e d f -> d e f")),
                (w13_sb[:, :, 1, :], w3.rearrange("e d f -> d e f")),
                (w2_sb[:, :, :, :].rearrange("p e c n -> p (e c) n"), w2.rearrange("e (c p) n -> p (e c) n", p=P)),
            ]
            sync.dma_start(xin[:, :, :], x[0:1, :, :].rearrange("b (i p) c -> p (b i) c", p=P)).then_inc(x_loaded.sem, 16)
            sync.sem_inc(out_stored.sem, 1)
            sync.wait_ge(padded, 1)
            for dst, src in loads:
                sync.dma_start(dst, src).then_inc(loaded, 16)
            assert len(loads) == N_LOADS

            def rows(b):
                return bass.ds(b, 1) if not isinstance(b, int) else slice(b, b + 1)

            def load(b, sig):
                sync.dma_start(xin[:, :, :], x[rows(b), :, :].rearrange("b (i p) c -> p (b i) c", p=P)).then_inc(sig.sem, 16)

            def turn(b):
                if in_range(b + 1) and not is_first(b + 1):
                    if is_first(b):
                        sync.wait_ge(h_ready.sem, h_ready.at(b, 1))
                    else:
                        sync.wait_ge(x1_ready.sem, x1_ready.at(b - 1, 1))
                    load(b + 1, x_loaded)
                if in_range(b):
                    if in_range(b + 1):
                        sync.wait_ge(h_ready.sem, h_ready.at(b + 1, 1))
                    elif is_first(b):
                        sync.wait_ge(h_ready.sem, h_ready.at(b, 1))
                    else:
                        sync.wait_ge(x1_ready.sem, x1_ready.at(b - 1, 1))
                    load(b, x_again)
                if in_range(b - 1):
                    sync.wait_ge(out_ready.sem, out_ready.at(b - 1, 1))
                    sync.dma_start(out[rows(b - 1), :, :].rearrange("b (i p) c -> p (b i) c", p=P), yout[:, :, :]).then_inc(out_stored.sem, 16)

            turn(0)
            if n_batch > 2:
                with sync.Fori(1, n_batch - 1) as b:
                    turn(b)
            if n_batch > 1:
                turn(n_batch - 1)
            turn(n_batch)
            sync.wait_ge(out_stored.sem, out_stored.at(n_batch - 1, 16) + 1)

        @block.gpsimd
        def _(pool):
            pool.memset(w_up_sb[:, :], 0.0)
            pool.memset(comp_gate[:, :], 0.0).then_inc(padded, 1)
            pool.memset(minus_half[:, :], -0.5)
            pool.memset(va[:, :, D:OW], 1.0)
            pool.memset(k2Z[:, :, :, :], 0.0)
            pool.memset(o2n[:, :, H2:, :], 0.0)
            pool.memset(va2[:, :, :, :], 0.0).then_inc(padded, 1)
            pool.wait_ge(padded, 2)
            pool.memset(va2[:, :, :, D2:D2 + 1], 1.0).then_inc(padded, 1)
            pool.wait_ge(cast_done, 1)

            def inverse_root(cols):
                return pool.tensor_tensor(rstd[:, 0:cols], var_in[:, 0:cols], minus_half[:, 0:cols], ALU.pow)

            def prepare1(b):
                for step in range(STEPS["prepare1"]):
                    if step == 0:
                        pool.wait_ge(var1_ready.sem, var1_ready.at(b, 1))
                        inverse_root(NT).then_inc(rstd1_ready.sem, 1)
                    if 4 <= step < 4 + NT:
                        i = step - 4
                        pool.wait_ge(rope_done.sem, rope_done.at(b, i + 1))
                        pool.tensor_tensor(qkv[:, i, 0:H + 1, :], qkv[:, i, 0:H + 1, :], gain1[:, :, :],
                                           ALU.mult).then_inc(gained.sem, 1)
                    if step == 7:
                        pool.wait_ge(var1_ready.sem, var1_ready.at(b, 2))
                        inverse_root(NT * (H + 1)).then_inc(rstd1_ready.sem, 1)
                        pool.tensor_copy(va[:, :, 0:D], qkv[:, :, H + 1, :]).then_inc(v_ready.sem, 1)
                    yield
                pool.wait_ge(v_ready.sem, v_ready.at(b, 1))

            def mix(b):
                for step in range(STEPS["mix"]):
                    if 1 <= step < 1 + NT:
                        i = step - 1
                        pool.wait_ge(coef_done.sem, coef_done.at(b, 1))
                        if i >= 2:
                            pool.wait_ge(mix_ready.sem, mix_ready.at(b, i - 1))
                        pool.tensor_tensor(mixb[i % 2][:, :, :], on[:, 0, i, :, 0:D],
                                           coef[:, 0, i, :].unsqueeze(2).to_broadcast([P, H, D]),
                                           ALU.mult).then_inc(near_scaled.sem, 1)
                    yield
                pool.wait_ge(near_scaled.sem, near_scaled.at(b, NT))

            def prepare2(b):
                for step in range(STEPS["prepare2"]):
                    if step in (0, 2, 4):
                        use = step // 2 + 1
                        pool.wait_ge(var2_ready.sem, var2_ready.at(b, use))
                        inverse_root(NT).then_inc(rstd2_ready.sem, 1)
                    yield
                pool.wait_ge(rstd2_ready.sem, rstd2_ready.at(b, 3))

            def after2(b):
                for step in range(STEPS["after2"]):
                    if step == 3:
                        pool.wait_ge(var3_ready.sem, var3_ready.at(b, 1))
                        inverse_root(NT).then_inc(rstd3_ready.sem, 1)
                    yield

            def experts(b):
                for step in range(STEPS["experts"]):
                    if step >= 9 and (step - 9) % 4 == 0 and (step - 9) // 4 < E:
                        e = (step - 9) // 4
                        pool.wait_ge(yg_ready.sem, yg_ready.at(b, e + 1))
                        if e >= 1:
                            pool.wait_ge(acc_done.sem, acc_done.at(b, e))
                        so_far = acc if e >= 1 else res
                        pool.tensor_tensor(acc[:, :, :], so_far[:, :, :], yg[e % 2][:, :, :], ALU.add).then_inc(acc_done.sem, 1)
                    if step == STEPS["experts"] - 1:
                        pool.wait_ge(var3_ready.sem, var3_ready.at(b, 2))
                        inverse_root(NT).then_inc(rstd3_ready.sem, 1)
                    yield
                pool.wait_ge(rstd3_ready.sem, rstd3_ready.at(b, 2))

            def turn(b):
                if in_range(b) or in_range(b - 1):
                    pool.wait_ge(slot_done, SLOTS_ENGINES * slots_before(b, 0))
                    take(0, **({"prepare2": prepare2(b - 1)} if in_range(b - 1) else {}))
                    pool.sem_inc(slot_done, 1)
                stages = {}
                if in_range(b):
                    stages["mix"] = mix(b)
                if in_range(b + 1):
                    stages["prepare1"] = prepare1(b + 1)
                if not is_first(b + 1):
                    pool.wait_ge(slot_done, SLOTS_ENGINES * slots_before(b, 1))
                take(1, **stages)
                pool.sem_inc(slot_done, 1)
                stages = {}
                if in_range(b - 1):
                    stages["after2"] = after2(b - 1)
                    stages["experts"] = experts(b - 1)
                pool.wait_ge(slot_done, SLOTS_ENGINES * slots_before(b, 2))
                take(2, **stages)
                pool.sem_inc(slot_done, 1)

            turn(-1)
            turn(0)
            if n_batch > 2:
                with pool.Fori(1, n_batch - 1) as b:
                    turn(b)
            if n_batch > 1:
                turn(n_batch - 1)
            turn(n_batch)

        @block.scalar
        def _(act):
            act.wait_ge(fold_psum, 1)
            flat = ps[:, 0:2, :].rearrange("p a n -> p (a n)")
            nc.scalar.activation(left_t[:, 0:5, :].rearrange("p c n -> p (c n)"), flat[0:64, 0:5 * P], ACT.Copy)
            nc.scalar.activation(left_t[0:32, 5, :], flat[0:32, 5 * P:6 * P], ACT.Copy).then_inc(folded, 1)
            act.wait_ge(fold_psum, 2)
            nc.scalar.activation(w_proj[:, 0:H * D], bank(2), ACT.Copy).then_inc(folded, 1)
            nc.scalar.activation(w_fold[:, :, :], bank(3).rearrange("p (c n) -> p c n", c=4), ACT.Copy).then_inc(folded, 1)
            nc.scalar.activation(w_qkv2[:, :], ps[:, 4, 0:3 * L2], ACT.Copy).then_inc(folded, 1)

            def copy(dst, src):
                return nc.scalar.activation(dst, src, ACT.Copy)

            def prepare1(b):
                for step in range(STEPS["prepare1"]):
                    if step == 1:
                        act.wait_ge(hT_psum.sem, hT_psum.at(b, 1))
                        copy(hT[:, :], bank(4)).then_inc(hT_ready.sem, 1)
                    if step == 2:
                        if not (isinstance(b, int) and b < 3):
                            act.wait_ge(out_stored.sem, out_stored.at(b - 3, 16) + 1)
                        act.wait_ge(kv_psum.sem, kv_psum.at(b, 1))
                        copy(qkv[:, :, H:, :].rearrange("p i h d -> p i (h d)"), bank(7).rearrange("p (i n) -> p i n", i=NT)).then_inc(kv_ready.sem, 1)
                        act.wait_ge(kv_ready.sem, kv_ready.at(b, 1))
                    if 2 <= step < 2 + NT:
                        i = step - 2
                        act.wait_ge(qkv_psum.sem, qkv_psum.at(b, i + 1))
                        copy(qkv[:, i, 0:H, :].rearrange("p h d -> p (h d)"), bank(5 + i % 2)).then_inc(qkv_ready.sem, 1)
                        if i >= 1:
                            act.wait_ge(sq_used.sem, sq_used.at(b, i))
                        act.wait_ge(qkv_ready.sem, qkv_ready.at(b, i + 1))
                        nc.scalar.activation(sq[:, :, :], qkv[:, i, 0:H + 1, :], ACT.Square).then_inc(sq_ready.sem, 1)
                    if 9 <= step < 9 + NT:
                        i = step - 9
                        for quad in range(2):
                            act.wait_ge(qT_psum.sem, qT_psum.at(b, 2 * i + quad + 1))
                            copy(qT[:, 4 * quad:4 * quad + 4, i, :], bank(5 + quad).rearrange("p (h n) -> p h n", n=P)).then_inc(qT_ready.sem, 1)
                    if step == 14:
                        for quad in range(2):
                            act.wait_ge(cgT_psum.sem, cgT_psum.at(b, quad + 1))
                            copy(cgT[:, quad, :], bank(6 - quad)).then_inc(cgT_ready.sem, 1)
                    if step == 15:
                        for quad in range(2):
                            act.wait_ge(cg_psum.sem, cg_psum.at(b, quad + 1))
                            copy(cg[:, :, 4 * quad:4 * quad + 4, :].rearrange("p i h r -> p i (h r)"),
                                 bank(7 - quad).rearrange("p (i r) -> p i r", i=NT)).then_inc(cg_ready.sem, 1)
                    if step == 17:
                        act.wait_ge(cexp_arg.sem, cexp_arg.at(b, 1))
                        nc.scalar.activation(cexp[:, :, :, :], cs[:, :, :, :], ACT.Exp)
                        nc.scalar.activation(csink[:, :, :], csink[:, :, :], ACT.Exp)
                        nc.scalar.activation(gz[:, :, :], gz[:, :, :], ACT.Exp, scale=-1.0).then_inc(cexp_ready.sem, 1)
                    yield
                act.wait_ge(cexp_ready.sem, cexp_ready.at(b, 1))

            def maxima1(b):
                act.wait_ge(pcT_psum.sem, pcT_psum.at(b, 1))
                copy(pcT[:, :], bank(5)).then_inc(pcT_ready.sem, 1)
                yield
                for _ in range(NT * H + 2):
                    yield
                act.wait_ge(coef_arg.sem, coef_arg.at(b, 1))
                nc.scalar.activation(cexps[:, :, :, :], cargs[:, :, :, :], ACT.Exp).then_inc(coef_exp.sem, 1)
                yield
                act.wait_ge(coef_exp.sem, coef_exp.at(b, 1))

            def attention(b):
                for step in range(STEPS["attention"]):
                    for g in range(8):
                        if step == FIRST1[g + 1] + 1:
                            act.wait_ge(pv_done.sem, pv_done.at(b, FIRST1[g + 1]))
                            if g >= 2:
                                act.wait_ge(on_psum.sem, on_psum.at(b, 2 * (g - 1)))
                            copy(oT[g % 2][0:OW, :, :], ps[0:OW, 2:4, :]).then_inc(oT_ready.sem, 1)
                    if step < NU1:
                        u = step
                        act.wait_ge(st_psum.sem, st_psum.at(b, u + 1))
                        if u >= 4:
                            act.wait_ge(pv_done.sem, pv_done.at(b, u - 3))
                        nc.scalar.activation(probs[u % 4], bank(u % 2), ACT.Exp).then_inc(exp_done.sem, 1)
                    for g in range(8):
                        for kind in range(2):
                            if step == FIRST1[g + 1] + 2 + kind:
                                act.wait_ge(on_psum.sem, on_psum.at(b, 2 * g + kind + 1))
                                quad, i = g // NT, g % NT
                                copy(on[:, kind, i, 4 * quad:4 * quad + 4, :].rearrange("p h d -> p (h d)"),
                                     ps[:, 4, 0:4 * OW]).then_inc(on_ready.sem, 1)
                    yield
                act.wait_ge(on_ready.sem, on_ready.at(b, 16))

            def mix(b):
                for step in range(STEPS["mix"]):
                    if 2 <= step < 2 + NT:
                        i = step - 2
                        act.wait_ge(mixT_psum.sem, mixT_psum.at(b, i + 1))
                        if i >= 2:
                            act.wait_ge(mixT_used.sem, mixT_used.at(b, i - 1))
                        copy(mixT[i % 2][:, :, :], bank(6).rearrange("p (c n) -> p c n", c=4)).then_inc(mixT_ready.sem, 1)
                    if step == 3 + NT:
                        act.wait_ge(mixT_used.sem, mixT_used.at(b, NT))
                        if in_range(b + 1):
                            act.wait_ge(hT_psum.sem, hT_psum.at(b + 1, 1))
                        copy(hn[:, :, :], bank(7).rearrange("p (i c) -> p i c", i=NT)).then_inc(attn_ready.sem, 1)
                    yield
                act.wait_ge(attn_ready.sem, attn_ready.at(b, 1))

            def prepare2(b):
                for step in range(STEPS["prepare2"]):
                    if step == 5:
                        act.wait_ge(h2T_psum.sem, h2T_psum.at(b, 1))
                        copy(hT[:, :], bank(5)).then_inc(h2T_ready.sem, 1)
                    if step == 6:
                        act.wait_ge(qkv2_psum.sem, qkv2_psum.at(b, 1))
                        copy(qkv2[:, :, :].rearrange("p (a i) n -> p a (i n)", a=2), ps[:, 6:8, 0:2 * 3 * L2]).then_inc(qkv2_ready.sem, 1)
                    if step == 7:
                        act.wait_ge(qkv2_ready.sem, qkv2_ready.at(b, 1))
                        copy(va2[:, :, :, 0:D2], qkv2[:, :, 2 * L2:].rearrange("p i (h d) -> p i h d", d=D2)).then_inc(va2_ready.sem, 1)
                    if step in (11, 12):
                        half = step - 11
                        act.wait_ge(q2T_psum.sem, q2T_psum.at(b, half + 1))
                        copy(q2T[:, 2 * half:2 * half + 2, :].rearrange("p g n -> p (g n)"), bank(5 + half).bitcast(BF16)).then_inc(q2T_ready.sem, 1)
                    if step in (13, 14):
                        half = step - 13
                        act.wait_ge(k2T_psum.sem, k2T_psum.at(b, half + 1))
                        act.wait_ge(k2Z_low.sem, k2Z_low.at(b, half + 1))
                        kp = bank(7 - 2 * half).bitcast(BF16).rearrange("p (g n) -> p g n", g=2)
                        for hh in range(2, 4):
                            rows = slice(RW * hh, RW * (hh + 1))
                            ins = copy(k2Z[rows, 2 * half:2 * half + 2, hh, :], kp[rows, :, :])
                        ins.then_inc(k2Z_high.sem, 1)
                    yield
                act.wait_ge(k2Z_high.sem, k2Z_high.at(b, 2))

            def attention2(b):
                for step in range(STEPS["attention2"]):
                    if step < NU2:
                        u = step
                        j = u // 4 % NT
                        act.wait_ge(st2_psum.sem, st2_psum.at(b, u + 1))
                        if u >= 6:
                            act.wait_ge(pv2_done.sem, pv2_done.at(b, (u - 6) // 4 + 1))
                        nc.scalar.activation(probs2[u % 6][:, 0:T - j * P], ps[:, u % 3, 0:T - j * P],
                                             ACT.Exp, scale=0.5).then_inc(exp2_done.sem, 1)
                    if step >= 4 * NT + 1 and (step - 1) % (4 * NT) == 0:
                        g = (step - 1) // (4 * NT) - 1
                        act.wait_ge(pv2_done.sem, pv2_done.at(b, NT * (g + 1)))
                        if g >= 2:
                            act.wait_ge(o2n_psum.sem, o2n_psum.at(b, g - 1))
                        copy(o2T[g % 2], bank(3)).then_inc(o2T_ready.sem, 1)
                    yield
                act.wait_ge(o2T_ready.sem, o2T_ready.at(b, 4))

            def after2(b):
                for step in range(STEPS["after2"]):
                    if step == 0:
                        act.wait_ge(o2nT_psum.sem, o2nT_psum.at(b, 1))
                        copy(o2nT, bank(0)).then_inc(o2nT_ready.sem, 1)
                    if step == 2:
                        act.wait_ge(res_ready.sem, res_ready.at(b, 1))
                        for i in range(NT):
                            ins = nc.scalar.activation(t_sb[:, i, :], res[:, i, :], ACT.Square, accum_out=ms[:, i:i + 1])
                        ins.then_inc(res_sq.sem, 1)
                    if step == 5:
                        act.wait_ge(tT_psum.sem, tT_psum.at(b, 1))
                        copy(tT[:, :], bank(2)).then_inc(tT_ready.sem, 1)
                    if step == 8:
                        act.wait_ge(wtop_arg.sem, wtop_arg.at(b, 1))
                        nc.scalar.activation(wtop[:, 1, :], wtop[:, 0, :], ACT.Exp).then_inc(wtop_exp.sem, 1)
                    yield

            def experts(b):
                for step in range(STEPS["experts"]):
                    if step < 2 * NX and step % 2 == 0:
                        n = step // 2
                        act.wait_ge(hid_psum.sem, hid_psum.at(b, n + 1))
                        if n >= 2:
                            act.wait_ge(hid_ready.sem, hid_ready.at(b, n - 1))
                        nc.scalar.activation(th[n % 2][:, :], bank(2 * (n % FC)), ACT.Tanh, scale=0.5).then_inc(th_ready.sem, 1)
                    yield
                act.wait_ge(th_ready.sem, th_ready.at(b, NX))

            def turn(b):
                if in_range(b) or in_range(b - 1):
                    stages = {}
                    if in_range(b):
                        stages["attention"] = attention(b)
                    if in_range(b - 1):
                        stages["prepare2"] = prepare2(b - 1)
                    act.wait_ge(slot_done, SLOTS_ENGINES * slots_before(b, 0))
                    take(0, **stages)
                    act.sem_inc(slot_done, 1)
                stages = {}
                if in_range(b):
                    stages["mix"] = mix(b)
                if in_range(b + 1):
                    stages["prepare1"] = prepare1(b + 1)
                if in_range(b - 1):
                    stages["attention2"] = attention2(b - 1)
                if not is_first(b + 1):
                    act.wait_ge(slot_done, SLOTS_ENGINES * slots_before(b, 1))
                take(1, **stages)
                act.sem_inc(slot_done, 1)
                stages = {}
                if in_range(b + 1):
                    stages["maxima1"] = maxima1(b + 1)
                if in_range(b - 1):
                    stages["after2"] = after2(b - 1)
                    stages["experts"] = experts(b - 1)
                act.wait_ge(slot_done, SLOTS_ENGINES * slots_before(b, 2))
                take(2, **stages)
                act.sem_inc(slot_done, 1)

            turn(-1)
            turn(0)
            if n_batch > 2:
                with act.Fori(1, n_batch - 1) as b:
                    turn(b)
            if n_batch > 1:
                turn(n_batch - 1)
            turn(n_batch)

        @block.vector
        def _(dve):
            v = nc.vector
            dve.wait_ge(loaded, 16 * N_LOADS)
            v.tensor_scalar(gain1[:, 0:H, :], gain_in[:, 0, :].unsqueeze(1).to_broadcast([P, H, D]), D ** -0.5, None, ALU.mult)
            v.tensor_copy(gain1[:, H, :], gain_in[:, 1, :]).then_inc(cast_done, 1)
            dve.wait_ge(padded, 3)

            chain = {"before": 0, "given": 0}

            def link(ins):
                chain["given"] += 1
                ins.then_inc(vector_chain, 1)
                dve.wait_ge(vector_chain, chain["before"] + chain["given"])

            def over(a, shape, axis):
                return a.unsqueeze(axis).to_broadcast(shape)

            def mean_var(src):
                for i in range(NT):
                    ins = v.bn_stats(stats[:, i, :], src(i))
                link(ins)
                v.memset(scrap[:, :], 0.0)
                for i in range(NT):
                    ins = v.bn_aggr(mv[:, i, :], stats[:, i, :])
                link(ins)
                return v.tensor_scalar(var_in[:, 0:NT], mv[:, :, 1], EPS5, None, ALU.add)

            def centred(dst, src):
                for i in range(NT):
                    ins = v.tensor_scalar(dst[:, i, :], src(i), mv[:, i, 0:1], rstd[:, i:i + 1], ALU.subtract, ALU.mult)
                return ins

            gates = gate[:, :, :].rearrange("p (i h) c -> p i h c", i=NT)
            sink_b = over(sink_sb[:, :], [P, NT, H], 1)

            def prepare1(b):
                dve.wait_ge(x_loaded.sem, x_loaded.at(b, 16))
                mean_var(lambda i: xin[:, i, :]).then_inc(var1_ready.sem, 1)
                dve.wait_ge(rstd1_ready.sem, rstd1_ready.at(b, 1))
                centred(hn, lambda i: xin[:, i, :]).then_inc(h_ready.sem, 1)
                for _ in range(3):
                    yield
                cos1 = con("cos1").rearrange("p (i r) -> p i r", i=NT)
                sin1 = con("sin1").rearrange("p (i r) -> p i r", i=NT)
                half = ROPE // 2
                for i in range(NT):
                    dve.wait_ge(sq_ready.sem, sq_ready.at(b, i + 1))
                    v.tensor_reduce(sumsq[:, i, :], sq[:, :, :], AX.X, ALU.add).then_inc(sq_used.sem, 1)
                    if i >= 1:
                        dve.wait_ge(rope_done.sem, rope_done.at(b, i))
                    part = qkv[:, i, 0:H + 1, 0:ROPE]
                    v.tensor_tensor(ropeA[:, :, :], part, over(cos1[:, i, :], [P, H + 1, ROPE], 1), ALU.mult)
                    link(v.tensor_tensor(ropeB[:, :, :], part, over(sin1[:, i, :], [P, H + 1, ROPE], 1), ALU.mult))
                    v.tensor_tensor(qkv[:, i, 0:H + 1, 0:half], ropeA[:, :, 0:half], ropeB[:, :, half:], ALU.subtract)
                    v.tensor_tensor(qkv[:, i, 0:H + 1, half:ROPE], ropeB[:, :, 0:half], ropeA[:, :, half:], ALU.add).then_inc(rope_done.sem, 1)
                    yield
                dve.wait_ge(sq_used.sem, sq_used.at(b, NT))
                v.tensor_scalar(var_in[:, :], sumsq[:, :, :].rearrange("p i h -> p (i h)"), 1.0 / D, EPS6, ALU.mult, ALU.add).then_inc(var1_ready.sem, 1)
                yield
                for i in range(NT):
                    dve.wait_ge(rstd1_ready.sem, rstd1_ready.at(b, 2))
                    dve.wait_ge(gained.sem, gained.at(b, i + 1))
                    if i == 0 and not is_first(b):
                        dve.wait_ge(mixT_used.sem, mixT_used.at(b - 1, NT))
                    r = rstd[:, i * (H + 1):(i + 1) * (H + 1)]
                    qk = qkv[:, i, 0:H + 1, :]
                    link(v.tensor_tensor(qk, qk, over(r, [P, H + 1, D], 2), ALU.mult))
                    v.tensor_copy(kdup[:, i, :, :], over(qkv[:, i, H, :], [P, 2, D], 1))
                    link(v.tensor_copy(qsplit[:, i, :, 0, :].bitcast(F32R), qkv[:, i, 0:H, :]))
                    v.tensor_tensor(qsplit[:, i, :, 1, :], qkv[:, i, 0:H, :], qsplit[:, i, :, 0, :], ALU.subtract).then_inc(split_ready.sem, 1)
                    yield
                yield
                dve.wait_ge(kT_psum.sem, kT_psum.at(b, 1))
                v.tensor_reduce(kmean[:, :], bank(7).rearrange("p (n r) -> p n r", r=CR), AX.X, ALU.add)
                link(v.tensor_copy(kT_hi[:, :], bank(7)))
                v.tensor_scalar(comp_gate[:, 0:NBLK], kmean[:, :], 1.0 / CR, None, ALU.mult)
                v.tensor_tensor(kT_lo[:, :], bank(7), kT_hi[:, :], ALU.subtract).then_inc(k_ready.sem, 1)
                yield
                dve.wait_ge(vmean_psum.sem, vmean_psum.at(b, 1))
                v.tensor_tensor(vmean[:, :, :], over(ps[:, 5, 0:D], [P, H, D], 1), over(con("head_rows"), [P, H, D], 2), ALU.mult).then_inc(vmean_ready.sem, 1)
                yield
                yield
                dve.wait_ge(cg_ready.sem, cg_ready.at(b, 2))
                valid = con("block_valid").rearrange("p (i n) -> p i n", i=NT)
                for i in range(NT):
                    ins = v.tensor_tensor(cs[:, i, :, :], cg[:, i, :, 0:NBLK], over(valid[:, i, :], [P, H, NBLK], 1), ALU.add)
                gf = cg[:, :, :, NBLK:NBLK + 3].rearrange("p i h c -> p (i h) c")
                v.scalar_tensor_tensor(gz[:, :, :], gf, D ** 0.5, over(bgate_sb[:, :], [P, NT * H, 3], 1), ALU.mult, ALU.add)
                link(ins)
                link(v.tensor_reduce(cmax[:, :, :], cs[:, :, :, :], AX.X, ALU.max))
                link(v.tensor_tensor(cmax[:, :, :], cmax[:, :, :], sink_b, ALU.max))
                csf = cs[:, :, :, :].rearrange("p i h n -> p (i h) n")
                cmf = cmax[:, :, :].rearrange("p i h -> p (i h)")
                v.tensor_tensor(csf, csf, over(cmf, [P, NT * H, NBLK], 2), ALU.subtract)
                v.tensor_tensor(csink[:, :, :], sink_b, cmax[:, :, :], ALU.subtract).then_inc(cexp_arg.sem, 1)
                yield
                yield
                dve.wait_ge(cexp_ready.sem, cexp_ready.at(b, 1))
                link(v.tensor_scalar(gz[:, :, :], gz[:, :, :], 1.0, None, ALU.add))
                link(v.reciprocal(gate[:, :, :], gz[:, :, :]))
                link(v.tensor_reduce(gsum[:, :], gate[:, :, :], AX.X, ALU.add))
                link(v.tensor_scalar(gsum[:, :], gsum[:, :], 1e-6, None, ALU.max))
                v.tensor_reduce(csum[:, :, :], cexp[:, :, :, :], AX.X, ALU.add)
                link(v.reciprocal(gsum[:, :], gsum[:, :]))
                link(v.tensor_tensor(gate[:, :, :], gate[:, :, :], over(gsum[:, :], [P, NT * H, 3], 2), ALU.mult))
                link(v.tensor_tensor(csum[:, :, :], csum[:, :, :], csink[:, :, :], ALU.add))
                link(v.reciprocal(ccoef[:, :, :], csum[:, :, :]))
                link(v.tensor_tensor(ccoef[:, :, :], ccoef[:, :, :], gates[:, :, :, 0], ALU.mult))
                cef = cexp[:, :, :, :].rearrange("p i h n -> p (i h) n")
                v.tensor_tensor(cef, cef, over(ccoef[:, :, :].rearrange("p i h -> p (i h)"), [P, NT * H, NBLK], 2), ALU.mult).then_inc(pc_ready.sem, 1)
                yield
                dve.wait_ge(pc_ready.sem, pc_ready.at(b, 1))

            def maxima1(b):
                yield
                for n in range(NT * H):
                    h, i = n // NT, n % NT
                    quad, hh = h // 4, h % 4
                    dve.wait_ge(s_psum.sem, s_psum.at(b, n + 1))
                    w = (i + 1) * P
                    lo = P if i == 0 else P // 2
                    v.tensor_reduce(nmax[:, quad, i, 0, hh:hh + 1], ps[:, 7, lo:2 * P], AX.X, ALU.max, negate=True).then_inc(near_max.sem, 1)
                    v.tensor_reduce(nmax[:, quad, i, 1, hh:hh + 1], ps[:, 5 + n % 2, 0:w], AX.X, ALU.max, negate=True).then_inc(max_done.sem, 1)
                    yield
                dve.wait_ge(max_done.sem, max_done.at(b, NT * H))
                nm = nmax[:, :, :, :, :].rearrange("p a i k h -> p (a i k h)")
                link(v.tensor_scalar(nm, nm, SHIFT_CAP, None, ALU.min))
                link(v.tensor_copy(nmax_bf[:, :, 0], nm))
                link(v.tensor_tensor(nmax_bf[:, :, 1], nm, nmax_bf[:, :, 0], ALU.subtract))
                v.tensor_tensor(nm, nmax_bf[:, :, 0], nmax_bf[:, :, 1], ALU.add).then_inc(nmax_split.sem, 1)
                yield
                dve.wait_ge(shift_psum.sem, shift_psum.at(b, 1))
                v.tensor_tensor(shiftT[:, :, :], over(ps[:, 5, 0:P // 2].bitcast(BF16), [P, 4, P], 1),
                                over(con("shift_head"), [P, 4, P], 2), ALU.mult).then_inc(shift_ready.sem, 1)
                yield
                dve.wait_ge(nmax_split.sem, nmax_split.at(b, 1))

                def nk(kind, quad):
                    return nmax[:, quad, :, kind, :]
                for quad in range(2):
                    hs = slice(4 * quad, 4 * quad + 4)
                    v.tensor_tensor(nfull[:, :, hs], nk(0, quad), nk(1, quad), ALU.min)
                    ins = v.scalar_tensor_tensor(nsink[:, :, hs], over(sink_sb[:, hs], [P, NT, 4], 1), -1.0, nk(0, quad), ALU.mult, ALU.min)
                link(ins)
                for quad in range(2):
                    hs = slice(4 * quad, 4 * quad + 4)
                    v.tensor_tensor(cargs[:, 0, :, hs], nfull[:, :, hs], nk(0, quad), ALU.subtract)
                    v.tensor_tensor(cargs[:, 1, :, hs], nfull[:, :, hs], nk(1, quad), ALU.subtract)
                    v.tensor_tensor(cargs[:, 2, :, hs], nsink[:, :, hs], nk(0, quad), ALU.subtract)
                v.tensor_tensor(cargs[:, 3, :, :], nsink[:, :, :], sink_b, ALU.add).then_inc(coef_arg.sem, 1)
                yield
                dve.wait_ge(coef_arg.sem, coef_arg.at(b, 1))

            def mix(b):
                dve.wait_ge(on_ready.sem, on_ready.at(b, 16))
                dve.wait_ge(coef_exp.sem, coef_exp.at(b, 1))
                zn, zf = on[:, 0, :, :, D], on[:, 1, :, :, D]
                v.tensor_tensor(zfull[:, :, :], cexps[:, 0, :, :], zn, ALU.mult)
                v.tensor_tensor(ztmp[:, :, :], cexps[:, 1, :, :], zf, ALU.mult)
                link(v.tensor_tensor(zwin[:, :, :], cexps[:, 2, :, :], zn, ALU.mult))
                v.tensor_tensor(zfull[:, :, :], zfull[:, :, :], ztmp[:, :, :], ALU.add)
                link(v.tensor_tensor(zwin[:, :, :], zwin[:, :, :], cexps[:, 3, :, :], ALU.add))
                v.reciprocal(zfull[:, :, :], zfull[:, :, :])
                link(v.reciprocal(zwin[:, :, :], zwin[:, :, :]))
                v.tensor_tensor(zfull[:, :, :], zfull[:, :, :], gates[:, :, :, 1], ALU.mult)
                link(v.tensor_tensor(zwin[:, :, :], zwin[:, :, :], gates[:, :, :, 2], ALU.mult))
                v.tensor_tensor(coef[:, 0, :, :], cexps[:, 0, :, :], zfull[:, :, :], ALU.mult)
                v.tensor_tensor(coef[:, 1, :, :], cexps[:, 1, :, :], zfull[:, :, :], ALU.mult)
                link(v.tensor_tensor(zwin[:, :, :], cexps[:, 2, :, :], zwin[:, :, :], ALU.mult))
                v.tensor_tensor(coef[:, 0, :, :], coef[:, 0, :, :], zwin[:, :, :], ALU.add).then_inc(coef_done.sem, 1)
                yield
                for i in range(NT):
                    dve.wait_ge(coef_done.sem, coef_done.at(b, 1))
                    if i >= 2:
                        dve.wait_ge(mixT_psum.sem, mixT_psum.at(b, i - 1))
                    m = mixa[i % 2]
                    link(v.tensor_tensor(m[:, :, :], on[:, 1, i, :, 0:D], over(coef[:, 1, i, :], [P, H, D], 2), ALU.mult))
                    dve.wait_ge(comp_psum.sem, comp_psum.at(b, i + 1))
                    link(v.tensor_tensor(m[:, :, :], m[:, :, :], bank(5).rearrange("p (h d) -> p h d", h=H), ALU.add))
                    dve.wait_ge(near_scaled.sem, near_scaled.at(b, i + 1))
                    v.tensor_tensor(m[:, :, :], m[:, :, :], mixb[i % 2][:, :, :], ALU.add).then_inc(mix_ready.sem, 1)
                    yield
                for _ in range(3):
                    yield
                dve.wait_ge(mix_ready.sem, mix_ready.at(b, NT))

            def prepare2(b):
                ao = lambda i: hn[:, i, :]
                dve.wait_ge(attn_ready.sem, attn_ready.at(b, 1))
                mean_var(ao).then_inc(var2_ready.sem, 1)
                yield
                dve.wait_ge(rstd2_ready.sem, rstd2_ready.at(b, 1))
                link(centred(x1, ao))
                dve.wait_ge(x_again.sem, x_again.at(b, 16))
                v.tensor_tensor(x1[:, :, :], x1[:, :, :], xin[:, :, :], ALU.add).then_inc(x1_ready.sem, 1)
                dve.wait_ge(x1_ready.sem, x1_ready.at(b, 1))
                yield
                mean_var(lambda i: x1[:, i, :]).then_inc(var2_ready.sem, 1)
                yield
                dve.wait_ge(rstd2_ready.sem, rstd2_ready.at(b, 2))
                link(centred(ffn_in, lambda i: x1[:, i, :]))
                link(v.tensor_tensor(ms[:, :], rstd[:, 0:NT], rstd[:, 0:NT], ALU.mult))
                link(v.tensor_tensor(ms[:, :], ms[:, :], mv[:, :, 1], ALU.mult))
                v.tensor_scalar(var_in[:, 0:NT], ms[:, :], EPS5, None, ALU.add).then_inc(var2_ready.sem, 1)
                yield
                dve.wait_ge(rstd2_ready.sem, rstd2_ready.at(b, 3))
                for i in range(NT):
                    ins = v.scalar_tensor_tensor(hn[:, i, :], ffn_in[:, i, :], rstd[:, i:i + 1], g1_sb[:, :], ALU.mult, ALU.mult)
                ins.then_inc(h2_ready.sem, 1)
                for _ in range(3):
                    yield
                dve.wait_ge(qkv2_ready.sem, qkv2_ready.at(b, 1))
                cos2 = con("cos2").rearrange("p (i r) -> p i r", i=NT)
                sin2 = con("sin2").rearrange("p (i r) -> p i r", i=NT)
                pairs = qkv2[:, :, 0:2 * L2].rearrange("p i (h r c) -> p i h r c", r=2, c=2)
                for i in range(NT):
                    even, odd = pairs[:, i, :, :, 0], pairs[:, i, :, :, 1]
                    cb, sbb = over(cos2[:, i, :], [P, 2 * H2, 2], 1), over(sin2[:, i, :], [P, 2 * H2, 2], 1)
                    v.tensor_tensor(rot[0][:, i, :, :], even, cb, ALU.mult)
                    v.tensor_tensor(rot[1][:, i, :, :], odd, sbb, ALU.mult)
                    v.tensor_tensor(rot[2][:, i, :, :], even, sbb, ALU.mult)
                    ins = v.tensor_tensor(rot[3][:, i, :, :], odd, cb, ALU.mult)
                link(ins)
                yield
                for w in range(2):
                    hs = slice(w * H2, (w + 1) * H2)
                    dst = qk2[:, w, :, :].rearrange("p (i h) (r c) -> p i h r c", i=NT, r=2)
                    for i in range(NT):
                        v.tensor_tensor(dst[:, i, :, :, 0], rot[0][:, i, hs, :], rot[1][:, i, hs, :], ALU.subtract)
                        ins = v.tensor_tensor(dst[:, i, :, :, 1], rot[2][:, i, hs, :], rot[3][:, i, hs, :], ALU.add)
                link(ins)
                yield
                sl = ((0, 3, 6), (0, 1, 2))
                for lvl in range(3):
                    for w in range(2):
                        src = (qk2 if lvl == 0 else rem)[:, w, :, :]
                        ins = v.tensor_copy(parts2[:, w, :, sl[w][lvl], :], src)
                    link(ins)
                    if lvl < 2:
                        for w in range(2):
                            src = (qk2 if lvl == 0 else rem)[:, w, :, :]
                            ins = v.tensor_tensor(rem[:, w, :, :], src, parts2[:, w, :, sl[w][lvl], :], ALU.subtract)
                        link(ins)
                yield
                pq, pk = parts2[:, 0, :, :, :], parts2[:, 1, :, :, :]
                v.tensor_copy(pq[:, :, 1:3, :], over(pq[:, :, 0, :], [P, NT * H2, 2, D2], 2))
                v.tensor_copy(pq[:, :, 4:6, :], over(pq[:, :, 3, :], [P, NT * H2, 2, D2], 2))
                v.tensor_copy(pq[:, :, 7, :], pq[:, :, 6, :])
                v.tensor_copy(pk[:, :, 3:6, :], pk[:, :, 0:3, :])
                v.tensor_copy(pk[:, :, 6:8, :], pk[:, :, 0:2, :]).then_inc(parts2_ready.sem, 1)
                for _ in range(3):
                    yield
                for half in range(2):
                    dve.wait_ge(k2T_psum.sem, k2T_psum.at(b, half + 1))
                    kp = bank(7 - 2 * half).bitcast(BF16).rearrange("p (g n) -> p g n", g=2)
                    for hh in range(2):
                        rows = slice(RW * hh, RW * (hh + 1))
                        ins = v.tensor_copy(k2Z[rows, 2 * half:2 * half + 2, hh, :], kp[rows, :, :])
                    ins.then_inc(k2Z_low.sem, 1)
                    yield
                dve.wait_ge(k2Z_low.sem, k2Z_low.at(b, 2))

            def maxima2(b):
                for n, (g, i, hh, nh) in enumerate(UNITS_MAX2):
                    dve.wait_ge(s2_psum.sem, s2_psum.at(b, n + 1))
                    w = (i + 1) * P
                    v.tensor_reduce(nmax2[:, 4 * g + hh:4 * g + hh + nh, i], ps[:, 5 + n % 3, 0:nh * w].rearrange("p (h k) -> p h k", h=nh),
                                    AX.X, ALU.max, negate=True).then_inc(max2_done.sem, 1)
                    yield
                dve.wait_ge(max2_done.sem, max2_done.at(b, len(UNITS_MAX2)))
                nm2 = nmax2[:, :, :].rearrange("p h i -> p (h i)")
                link(v.tensor_copy(nmax2_bf[:, :, 0], nm2))
                v.tensor_tensor(nmax2_bf[:, :, 1], nm2, nmax2_bf[:, :, 0], ALU.subtract).then_inc(nmax2_split.sem, 1)
                yield
                yield
                dve.wait_ge(shift2_psum.sem, shift2_psum.at(b, 1))
                v.tensor_tensor(shift2T[:, :, :], over(ps[:, 5, 0:P // 2].bitcast(BF16), [P, 4, P], 1),
                                over(con("shift2_tile"), [P, 4, P], 2), ALU.mult).then_inc(shift2_ready.sem, 1)
                yield
                dve.wait_ge(shift2_ready.sem, shift2_ready.at(b, 1))

            def attention2(b):
                for step in range(STEPS["attention2"]):
                    if step >= 4 * NT + 3 and (step - 3) % (4 * NT) == 0:
                        g = (step - 3) // (4 * NT) - 1
                        dve.wait_ge(o2n_psum.sem, o2n_psum.at(b, g + 1))
                        nat = bank(4).rearrange("p (i h r) -> p i h r", i=NT, h=4)
                        link(v.reciprocal(rz2[:, :, :], nat[:, :, :, D2]))
                        for i in range(NT):
                            ins = v.tensor_tensor(o2n[:, i, 4 * g:4 * g + 4, :], nat[:, i, :, 0:D2], over(rz2[:, i, :], [P, 4, D2], 2), ALU.mult)
                        ins.then_inc(o2n_ready.sem, 1)
                        dve.wait_ge(o2n_ready.sem, o2n_ready.at(b, g + 1))
                    yield

            def after2(b):
                yield
                yield
                dve.wait_ge(up_psum.sem, up_psum.at(b, 1))
                v.tensor_tensor(res[:, :, :], ffn_in[:, :, :], bank(1).rearrange("p (i c) -> p i c", i=NT), ALU.add).then_inc(res_ready.sem, 1)
                yield
                dve.wait_ge(res_sq.sem, res_sq.at(b, 1))
                v.tensor_scalar(var_in[:, 0:NT], ms[:, :], 1.0 / HID, EPS5, ALU.mult, ALU.add).then_inc(var3_ready.sem, 1)
                yield
                dve.wait_ge(rstd3_ready.sem, rstd3_ready.at(b, 1))
                for i in range(NT):
                    ins = v.scalar_tensor_tensor(t_sb[:, i, :], res[:, i, :], rstd[:, i:i + 1], g2_sb[:, :], ALU.mult, ALU.mult)
                ins.then_inc(t_ready.sem, 1)
                for _ in range(3):
                    yield
                dve.wait_ge(router_psum.sem, router_psum.at(b, 1))
                link(v.tensor_copy(logit[:, :, :], ps[:, 4, 0:NT * E].rearrange("p (i e) -> p i e", i=NT)))
                shape = [P, NT, E]
                iota = over(con("iota8"), shape, 1)
                for top, hot in ((top1, hot1), (top2, hot2)):
                    if hot is hot2:
                        yield
                    link(v.tensor_reduce(top[:, :], logit[:, :, :], AX.X, ALU.max))
                    link(v.tensor_tensor(pick[:, :, :], logit[:, :, :], over(top[:, :], shape, 2), ALU.is_lt))
                    link(v.scalar_tensor_tensor(pick[:, :, :], pick[:, :, :], float(E), iota, ALU.mult, ALU.add))
                    link(v.tensor_reduce(ms[:, :], pick[:, :, :], AX.X, ALU.min))
                    link(v.tensor_tensor(hot[:, :, :], iota, over(ms[:, :], shape, 2), ALU.is_equal))
                    if hot is hot1:
                        link(v.scalar_tensor_tensor(logit[:, :, :], hot[:, :, :], -3.0e38, logit[:, :, :], ALU.mult, ALU.add))
                v.tensor_tensor(wtop[:, 0, :], top2[:, :], top1[:, :], ALU.subtract).then_inc(wtop_arg.sem, 1)
                yield
                dve.wait_ge(wtop_exp.sem, wtop_exp.at(b, 1))
                link(v.tensor_scalar(top1[:, :], wtop[:, 1, :], 1.0, 2.0, ALU.add, ALU.mult))
                link(v.reciprocal(top1[:, :], top1[:, :]))
                link(v.tensor_tensor(top2[:, :], top1[:, :], wtop[:, 1, :], ALU.mult))
                v.tensor_tensor(hot1[:, :, :], hot1[:, :, :], over(top1[:, :], shape, 2), ALU.mult)
                link(v.tensor_tensor(hot2[:, :, :], hot2[:, :, :], over(top2[:, :], shape, 2), ALU.mult))
                link(v.tensor_tensor(egate[:, :, :], hot1[:, :, :], hot2[:, :, :], ALU.add))
                yield

            def experts(b):
                for step in range(STEPS["experts"]):
                    if step < 2 * NX and step % 2 == 1:
                        n = step // 2
                        e, c = n // FC, n % FC
                        dve.wait_ge(th_ready.sem, th_ready.at(b, n + 1))
                        if c == 0 and e >= 2:
                            dve.wait_ge(y_psum.sem, y_psum.at(b, e - 1))
                        link(v.scalar_tensor_tensor(th[n % 2], th[n % 2], 1.0, bank(2 * c), ALU.add, ALU.mult))
                        v.tensor_tensor(hid[e % 2][:, c, :], th[n % 2][:, :], bank(2 * c + 1), ALU.mult).then_inc(hid_ready.sem, 1)
                    if step >= 8 and step % 4 == 0 and step // 4 - 2 < E:
                        e = step // 4 - 2
                        dve.wait_ge(y_psum.sem, y_psum.at(b, e + 1))
                        if e == 0 and not is_first(b):
                            dve.wait_ge(out_stored.sem, out_stored.at(b - 1, 16) + 1)
                        if e >= 2:
                            dve.wait_ge(acc_done.sem, acc_done.at(b, e - 1))
                        v.tensor_tensor(yg[e % 2][:, :, :], bank(4).rearrange("p (i c) -> p i c", i=NT),
                                        over(egate[:, :, e], [P, NT, HID], 2), ALU.mult).then_inc(yg_ready.sem, 1)
                    if step == STEPS["experts"] - 1:
                        dve.wait_ge(acc_done.sem, acc_done.at(b, E))
                        mean_var(lambda i: acc[:, i, :]).then_inc(var3_ready.sem, 1)
                        dve.wait_ge(rstd3_ready.sem, rstd3_ready.at(b, 2))
                        link(centred(acc, lambda i: acc[:, i, :]))
                        v.tensor_tensor(yout[:, :, :], acc[:, :, :], x1[:, :, :], ALU.add).then_inc(out_ready.sem, 1)
                    yield
                dve.wait_ge(out_ready.sem, out_ready.at(b, 1))

            def turn(b):
                if in_range(b - 1):
                    dve.wait_ge(slot_done, SLOTS_ENGINES * slots_before(b, 0))
                    take(0, prepare2=prepare2(b - 1), maxima2=maxima2(b - 1))
                    dve.sem_inc(slot_done, 1)
                elif in_range(b):
                    dve.wait_ge(slot_done, SLOTS_ENGINES * slots_before(b, 0))
                    dve.sem_inc(slot_done, 1)
                stages = {}
                if in_range(b):
                    stages["mix"] = mix(b)
                if in_range(b + 1):
                    stages["prepare1"] = prepare1(b + 1)
                if in_range(b - 1):
                    stages["attention2"] = attention2(b - 1)
                if not is_first(b + 1):
                    dve.wait_ge(slot_done, SLOTS_ENGINES * slots_before(b, 1))
                take(1, **stages)
                dve.sem_inc(slot_done, 1)
                stages = {}
                if in_range(b + 1):
                    stages["maxima1"] = maxima1(b + 1)
                if in_range(b - 1):
                    stages["after2"] = after2(b - 1)
                    stages["experts"] = experts(b - 1)
                dve.wait_ge(slot_done, SLOTS_ENGINES * slots_before(b, 2))
                take(2, **stages)
                dve.sem_inc(slot_done, 1)

            turn(-1)
            turn(0)
            if n_batch > 2:
                before = chain["given"]
                with dve.Fori(1, n_batch - 1) as b:
                    chain["before"], chain["given"] = before + (b - 1) * VECTOR_LINKS, 0
                    turn(b)
                    assert chain["given"] == VECTOR_LINKS, chain["given"]
                chain["before"], chain["given"] = before + (n_batch - 2) * VECTOR_LINKS, 0
            if n_batch > 1:
                turn(n_batch - 1)
            turn(n_batch)

        @block.tensor
        def _(pe):
            mm, tr = nc.tensor.matmul, nc.tensor.transpose
            pe.wait_ge(loaded, 16 * N_LOADS)
            flat = ps[:, 0:2, :].rearrange("p a n -> p (a n)")
            for c in range(4):
                tr(flat[0:64, c * P:(c + 1) * P], w_og_sb[:, c, :], ident)
            tr(flat[0:L2, 4 * P:5 * P], w_down_sb[:, :], ident)
            tr(flat[0:32, 5 * P:6 * P], w_qc_sb[:, :], ident).then_inc(fold_psum, 1)
            pe.wait_ge(folded, 1)
            mm(bank(2), left_t[0:32, 5, :], w_qup_sb[:, :], start=True, stop=True)
            for c in range(4):
                mm(ps[:, 3, c * P:(c + 1) * P], left_t[:, c, :], w_out_sb[:, c // 2, :], start=True, stop=True)
            mm(ps[:, 4, 0:3 * L2], left_t[:, 4, :], w_qkv2_in[:, :, :].rearrange("p w n -> p (w n)"), start=True, stop=True).then_inc(fold_psum, 1)
            pe.wait_ge(folded, 4)
            pe.wait_ge(cast_done, 1)
            pe.wait_ge(padded, 3)

            def prepare1(b):
                for step in range(STEPS["prepare1"]):
                    if step == 1:
                        pe.wait_ge(h_ready.sem, h_ready.at(b, 1))
                        for i in range(NT):
                            ins = tr(ps[:, 4, i * P:(i + 1) * P], hn[:, i, :], ident)
                        ins.then_inc(hT_psum.sem, 1)
                    if step == 2:
                        pe.wait_ge(hT_ready.sem, hT_ready.at(b, 1))
                        if not is_first(b):
                            pe.wait_ge(attn_ready.sem, attn_ready.at(b - 1, 1))
                        for i in range(NT):
                            ins = mm(ps[:, 7, i * 2 * D:(i + 1) * 2 * D], hT[:, i * P:(i + 1) * P], w_proj[:, H * D:], start=True, stop=True)
                        ins.then_inc(kv_psum.sem, 1)
                    if 2 <= step < 2 + NT:
                        i = step - 2
                        if i >= 2:
                            pe.wait_ge(qkv_ready.sem, qkv_ready.at(b, i - 1))
                        mm(bank(5 + i % 2), hT[:, i * P:(i + 1) * P], w_proj[:, 0:H * D], start=True, stop=True).then_inc(qkv_psum.sem, 1)
                    if 9 <= step < 9 + NT:
                        i = step - 9
                        pe.wait_ge(split_ready.sem, split_ready.at(b, i + 1))
                        for quad in range(2):
                            if i >= 1:
                                pe.wait_ge(qT_ready.sem, qT_ready.at(b, 2 * (i - 1) + quad + 1))
                            else:
                                pe.wait_ge(qkv_ready.sem, qkv_ready.at(b, NT))
                            for h in range(4 * quad, 4 * quad + 4):
                                ins = tr(ps[:, 5 + quad, (h % 4) * P:(h % 4 + 1) * P],
                                         qsplit[:, i, h, :, :].rearrange("p s d -> p (s d)"), ident)
                            ins.then_inc(qT_psum.sem, 1)
                        if i == NT - 1:
                            for n in range(NT):
                                ins = tr(ps[:, 7, n * P:(n + 1) * P], kdup[:, n, :, :].rearrange("p s d -> p (s d)"), ident)
                            ins.then_inc(kT_psum.sem, 1)
                    if step == 13:
                        pe.wait_ge(v_ready.sem, v_ready.at(b, 1))
                        pe.wait_ge(qT_ready.sem, qT_ready.at(b, 2 * NT))
                        rows = con("mean_rows").rearrange("p (i r) -> p i r", i=NT)
                        for i in range(NT):
                            ins = mm(ps[:, 5, 0:D], rows[:, i, :], va[:, i, 0:D], start=i == 0, stop=i == NT - 1)
                        ins.then_inc(vmean_psum.sem, 1)
                    if step == 14:
                        pe.wait_ge(k_ready.sem, k_ready.at(b, 1))
                        for h in range(H):
                            if h == 4:
                                pe.wait_ge(vmean_ready.sem, vmean_ready.at(b, 1))
                            r0 = RW * (h % 4)
                            ins = mm(ps[r0:r0 + RW, 6 - h // 4, :], comp_gate[:, :], qT[:, h, :, :].rearrange("p i n -> p (i n)").bitcast(F32), start=True, stop=True)
                            if h % 4 == 3:
                                ins.then_inc(cgT_psum.sem, 1)
                    if step == 15:
                        for quad in range(2):
                            pe.wait_ge(cgT_ready.sem, cgT_ready.at(b, quad + 1))
                            for i in range(NT):
                                ins = tr(ps[:, 7 - quad, i * P:(i + 1) * P], cgT[:, quad, i * P:(i + 1) * P], ident)
                            ins.then_inc(cg_psum.sem, 1)
                    yield
                pe.wait_ge(cg_psum.sem, cg_psum.at(b, 2))

            def maxima1(b):
                pe.wait_ge(pc_ready.sem, pc_ready.at(b, 1))
                for i in range(NT):
                    ins = tr(ps[:, 5, i * P:(i + 1) * P], cexp[:, i, :, :].rearrange("p h n -> p (h n)"), ident)
                ins.then_inc(pcT_psum.sem, 1)
                yield
                for n in range(NT * H):
                    h, i = n // NT, n % NT
                    if n == 0:
                        pe.wait_ge(pcT_ready.sem, pcT_ready.at(b, 1))
                    if n >= 2:
                        pe.wait_ge(max_done.sem, max_done.at(b, n - 1))
                    w = (i + 1) * P
                    last = min(2 * P, w)
                    q = qT[:, h, i, :]
                    far = ps[:, 5 + n % 2, 0:w]
                    mm(far, q, kT_hi[:, 0:w], start=True, stop=False)
                    mm(far[:, w - last:], ident_bf, con_bf("far_q")[:, 2 * P - last:], start=False, stop=True)
                    if n >= 1:
                        pe.wait_ge(near_max.sem, near_max.at(b, n))
                    near = ps[:, 7, 2 * P - last:2 * P]
                    mm(near, q, kT_hi[:, w - last:w], start=True, stop=False)
                    mm(near, ident_bf, con_bf("near_q")[:, 2 * P - last:], start=False, stop=True).then_inc(s_psum.sem, 1)
                    yield
                yield
                pe.wait_ge(nmax_split.sem, nmax_split.at(b, 1))
                tr(ps[:, 5, 0:P // 2].bitcast(BF16), nmax_bf[:, :, :].rearrange("p n s -> p (n s)"), ident_bf).then_inc(shift_psum.sem, 1)
                yield
                yield
                pe.wait_ge(shift_psum.sem, shift_psum.at(b, 1))

            pick1 = con_bf("shift_pick").rearrange("p (n r) -> p n r", n=16)

            def scores(b, u):
                quad, i, blocks, _ = UNITS1[u]
                if u >= 2:
                    pe.wait_ge(exp_done.sem, exp_done.at(b, u - 1))
                at = 0
                for kind, j, q0, nq, mask in blocks:
                    dst = ps[:, u % 2, at:at + 4 * nq].rearrange("p (h n) -> p h n", h=4)
                    q = qT[:, 4 * quad:4 * quad + 4, i, q0:q0 + nq]
                    keys = slice(j * P, (j + 1) * P)
                    mm(dst, kT_hi[:, keys], q, start=True, stop=False)
                    mm(dst, kT_lo[:, keys], q, start=False, stop=False)
                    if mask:
                        m = con_bf(mask)
                        if m.shape[1] > nq:
                            m = m[:, q0:q0 + nq]
                        mm(dst, ident_bf, m.unsqueeze(1).to_broadcast([P, 4, nq]), start=False, stop=False)
                    ins = mm(dst, pick1[:, (quad * 4 + i) * 2 + kind, :], shiftT[:, :, q0:q0 + nq], start=False, stop=True)
                    at += 4 * nq
                ins.then_inc(st_psum.sem, 1)

            def natural(b, g, kind):
                pe.wait_ge(oT_ready.sem, oT_ready.at(b, g + 1))
                if g or kind:
                    pe.wait_ge(on_ready.sem, on_ready.at(b, 2 * g + kind))
                for hh in range(4):
                    ins = tr(ps[:, 4, hh * OW:(hh + 1) * OW], oT[g % 2][0:OW, kind, hh * P:(hh + 1) * P], ident[0:OW, 0:OW])
                ins.then_inc(on_psum.sem, 1)

            def attention(b):
                for step in range(STEPS["attention"]):
                    if step == 0:
                        scores(b, 0)
                    if step + 1 < NU1:
                        scores(b, step + 1)
                    if 1 <= step <= NU1:
                        u = step - 1
                        quad, i, blocks, place = UNITS1[u]
                        g = quad * NT + i
                        pe.wait_ge(exp_done.sem, exp_done.at(b, u + 1))
                        if place == 0 and g >= 1:
                            pe.wait_ge(oT_ready.sem, oT_ready.at(b, g))
                        at = 0
                        for kind, j, q0, nq, mask in blocks:
                            pr = probs[u % 4][:, at:at + 4 * nq].rearrange("p (h n) -> p h n", h=4)
                            at += 4 * nq
                            dst = ps[0:OW, 2 + kind, :].rearrange("p (h n) -> p h n", h=4)[:, :, q0:q0 + nq]
                            ins = mm(dst, va[:, j, :], pr, start=j == i, stop=True, skip_group_check=True)
                        ins.then_inc(pv_done.sem, 1)
                    for g in range(8):
                        for kind in range(2):
                            if step == FIRST1[g + 1] + 2 + kind:
                                natural(b, g, kind)
                    yield
                pe.wait_ge(on_psum.sem, on_psum.at(b, 16))

            def mix(b):
                for step in range(STEPS["mix"]):
                    i = step - 1
                    if 0 <= i < NT:
                        if i >= 1:
                            pe.wait_ge(mix_ready.sem, mix_ready.at(b, i))
                        mm(bank(5), pcT[:, i * P:(i + 1) * P], vmean[:, :, :].rearrange("p h d -> p (h d)"), start=True, stop=True).then_inc(comp_psum.sem, 1)
                    i = step - 2
                    if 0 <= i < NT:
                        pe.wait_ge(mix_ready.sem, mix_ready.at(b, i + 1))
                        if i >= 1:
                            pe.wait_ge(mixT_ready.sem, mixT_ready.at(b, i))
                        for c in range(4):
                            ins = tr(ps[:, 6, c * P:(c + 1) * P], mixa[i % 2][:, 2 * c:2 * c + 2, :].rearrange("p h d -> p (h d)"), ident)
                        ins.then_inc(mixT_psum.sem, 1)
                    i = step - 3
                    if 0 <= i < NT:
                        pe.wait_ge(mixT_ready.sem, mixT_ready.at(b, i + 1))
                        for c in range(4):
                            ins = mm(ps[:, 7, i * P:(i + 1) * P], mixT[i % 2][:, c, :], w_fold[:, c, :], start=c == 0, stop=c == 3)
                        ins.then_inc(mixT_used.sem, 1)
                    yield
                pe.wait_ge(mixT_used.sem, mixT_used.at(b, NT))

            def prepare2(b):
                for step in range(STEPS["prepare2"]):
                    if step == 5:
                        pe.wait_ge(h2_ready.sem, h2_ready.at(b, 1))
                        for i in range(NT):
                            ins = tr(ps[:, 5, i * P:(i + 1) * P], hn[:, i, :], ident)
                        ins.then_inc(h2T_psum.sem, 1)
                    if step == 6:
                        pe.wait_ge(h2T_ready.sem, h2T_ready.at(b, 1))
                        for i in range(NT):
                            o = (i % 2) * 3 * L2
                            ins = mm(ps[:, 6 + i // 2, o:o + 3 * L2], hT[:, i * P:(i + 1) * P], w_qkv2[:, :], start=True, stop=True)
                        ins.then_inc(qkv2_psum.sem, 1)
                    if 11 <= step < 15:
                        w, half = (step - 11) // 2, (step - 11) % 2
                        pe.wait_ge(parts2_ready.sem, parts2_ready.at(b, 1))
                        if w == 1 and half == 1:
                            pe.wait_ge(q2T_ready.sem, q2T_ready.at(b, 1))
                        bk = (5, 6, 7, 5)[2 * w + half]
                        for g in range(2 * half, 2 * half + 2):
                            for i in range(NT):
                                src = parts2[:, w, i * H2 + 4 * g:i * H2 + 4 * g + 4, :, :].rearrange("p h s d -> p (h s d)")
                                o = ((g % 2) * NT + i) * P // 2
                                ins = tr(ps[:, bk, o:o + P // 2].bitcast(BF16), src, ident_bf)
                        ins.then_inc((k2T_psum if w else q2T_psum).sem, 1)
                    yield
                pe.wait_ge(k2T_psum.sem, k2T_psum.at(b, 2))

            def maxima2(b):
                for n, (g, i, hh, nh) in enumerate(UNITS_MAX2):
                    if n == 0:
                        pe.wait_ge(q2T_ready.sem, q2T_ready.at(b, 2))
                        pe.wait_ge(k2Z_low.sem, k2Z_low.at(b, 2))
                        pe.wait_ge(k2Z_high.sem, k2Z_high.at(b, 2))
                    if n >= 3:
                        pe.wait_ge(max2_done.sem, max2_done.at(b, n - 2))
                    w = (i + 1) * P
                    dst = ps[:, 5 + n % 3, 0:nh * w].rearrange("p (h k) -> p h k", h=nh)
                    for m in range(nh):
                        mm(dst[:, m, :], q2T[:, g, i * P:w], k2Z[:, g, hh + m, 0:w], start=True, stop=False)
                        ins = mm(dst[:, m, w - P:], ident_bf, con_bf("causal_q"), start=False, stop=True)
                    ins.then_inc(s2_psum.sem, 1)
                    yield
                yield
                pe.wait_ge(nmax2_split.sem, nmax2_split.at(b, 1))
                tr(ps[:, 5, 0:P // 2].bitcast(BF16), nmax2_bf[:, :, :].rearrange("p n s -> p (n s)"), ident_bf).then_inc(shift2_psum.sem, 1)
                yield
                yield
                pe.wait_ge(shift2_psum.sem, shift2_psum.at(b, 1))

            pick2 = con_bf("shift2_pick").rearrange("p (n r) -> p n r", n=H2)

            def scores2(b, u):
                g, j, hh = u // (4 * NT), u // 4 % NT, u % 4
                if u >= 3:
                    pe.wait_ge(exp2_done.sem, exp2_done.at(b, u - 2))
                dst = ps[:, u % 3, 0:T - j * P]
                mm(dst, k2Z[:, g, hh, j * P:(j + 1) * P], q2T[:, g, j * P:], start=True, stop=False)
                mm(dst, pick2[:, 4 * g + hh, :], shift2T[:, j:, :].rearrange("p i n -> p (i n)"), start=False, stop=False)
                mm(dst[:, 0:P], ident_bf, con_bf("causal_k"), start=False, stop=True).then_inc(st2_psum.sem, 1)

            def natural2(b, g):
                pe.wait_ge(o2T_ready.sem, o2T_ready.at(b, g + 1))
                if g >= 1:
                    pe.wait_ge(o2n_ready.sem, o2n_ready.at(b, g))
                elif in_range(b + 2):
                    pe.wait_ge(hT_ready.sem, hT_ready.at(b + 2, 1))
                for i in range(NT):
                    ins = tr(ps[:, 4, i * P:(i + 1) * P], o2T[g % 2][:, i * P:(i + 1) * P], ident)
                ins.then_inc(o2n_psum.sem, 1)

            def attention2(b):
                for step in range(STEPS["attention2"]):
                    if step == 0:
                        scores2(b, 0)
                        scores2(b, 1)
                    if step + 2 < NU2:
                        scores2(b, step + 2)
                    if step >= 4 and step % 4 == 0 and step <= NU2:
                        k = step // 4 - 1
                        g, j = k // NT, k % NT
                        pe.wait_ge(exp2_done.sem, exp2_done.at(b, 4 * (k + 1)))
                        if j == 0 and g >= 1:
                            pe.wait_ge(o2T_ready.sem, o2T_ready.at(b, g))
                        for hh in range(4):
                            ins = mm(ps[RW * hh:RW * (hh + 1), 3, j * P:], va2[:, j, 4 * g + hh, :], probs2[(4 * k + hh) % 6][:, 0:T - j * P],
                                     start=j == 0, stop=True, skip_group_check=True)
                        ins.then_inc(pv2_done.sem, 1)
                    if step >= 4 * NT + 2 and (step - 2) % (4 * NT) == 0:
                        natural2(b, (step - 2) // (4 * NT) - 1)
                    yield
                pe.wait_ge(o2n_psum.sem, o2n_psum.at(b, 4))

            def after2(b):
                for step in range(STEPS["after2"]):
                    if step == 0:
                        pe.wait_ge(o2n_ready.sem, o2n_ready.at(b, 4))
                        for i in range(NT):
                            ins = tr(ps[:, 0, i * P:(i + 1) * P], o2n[:, i, :, :].rearrange("p h d -> p (h d)"), ident)
                        ins.then_inc(o2nT_psum.sem, 1)
                    if step == 1:
                        pe.wait_ge(o2nT_ready.sem, o2nT_ready.at(b, 1))
                        for i in range(NT):
                            ins = mm(ps[:, 1, i * P:(i + 1) * P], o2nT[:, i * P:(i + 1) * P], w_up_sb[:, :], start=True, stop=True)
                        ins.then_inc(up_psum.sem, 1)
                    if step == 5:
                        pe.wait_ge(t_ready.sem, t_ready.at(b, 1))
                        for i in range(NT):
                            ins = tr(ps[:, 2, i * P:(i + 1) * P], t_sb[:, i, :], ident)
                        ins.then_inc(tT_psum.sem, 1)
                    if step == 6:
                        pe.wait_ge(tT_ready.sem, tT_ready.at(b, 1))
                        for i in range(NT):
                            ins = mm(ps[:, 4, i * E:(i + 1) * E], tT[:, i * P:(i + 1) * P], router_sb[:, :], start=True, stop=True)
                        ins.then_inc(router_psum.sem, 1)
                    yield

            def experts(b):
                for step in range(STEPS["experts"]):
                    if step < 2 * NX and step % 2 == 0:
                        n = step // 2
                        e, c = n // FC, n % FC
                        pe.wait_ge(tT_ready.sem, tT_ready.at(b, 1))
                        if n >= FC:
                            pe.wait_ge(hid_ready.sem, hid_ready.at(b, n - FC + 1))
                        for k in range(2):
                            ins = mm(bank(2 * c + k), w13_sb[:, e, k, c * P:(c + 1) * P], tT[:, :], start=True, stop=True)
                        ins.then_inc(hid_psum.sem, 1)
                    if step >= 5 and step % 2 == 1 and step < 5 + 4 * E:
                        e, part = (step - 5) // 4, (step - 5) // 2 % 2
                        if part == 0:
                            pe.wait_ge(hid_ready.sem, hid_ready.at(b, FC * (e + 1)))
                            pe.wait_ge(router_psum.sem, router_psum.at(b, 1))
                        if part == 0 and e >= 1:
                            pe.wait_ge(yg_ready.sem, yg_ready.at(b, e))
                        for i in range(NT // 2 * part, NT // 2 * (part + 1)):
                            for c in range(FC):
                                ins = mm(ps[:, 4, i * P:(i + 1) * P], hid[e % 2][:, c, i * P:(i + 1) * P], w2_sb[:, e, c, :], start=c == 0, stop=c == FC - 1)
                        if part == 1:
                            ins.then_inc(y_psum.sem, 1)
                    yield
                pe.wait_ge(y_psum.sem, y_psum.at(b, E))

            def turn(b):
                if in_range(b) or in_range(b - 1):
                    stages = {}
                    if in_range(b):
                        stages["attention"] = attention(b)
                    if in_range(b - 1):
                        stages["prepare2"] = prepare2(b - 1)
                        stages["maxima2"] = maxima2(b - 1)
                    pe.wait_ge(slot_done, SLOTS_ENGINES * slots_before(b, 0))
                    take(0, **stages)
                    pe.sem_inc(slot_done, 1)
                stages = {}
                if in_range(b):
                    stages["mix"] = mix(b)
                if in_range(b + 1):
                    stages["prepare1"] = prepare1(b + 1)
                if in_range(b - 1):
                    stages["attention2"] = attention2(b - 1)
                if not is_first(b + 1):
                    pe.wait_ge(slot_done, SLOTS_ENGINES * slots_before(b, 1))
                take(1, **stages)
                pe.sem_inc(slot_done, 1)
                stages = {}
                if in_range(b + 1):
                    stages["maxima1"] = maxima1(b + 1)
                if in_range(b - 1):
                    stages["after2"] = after2(b - 1)
                    stages["experts"] = experts(b - 1)
                pe.wait_ge(slot_done, SLOTS_ENGINES * slots_before(b, 2))
                take(2, **stages)
                pe.sem_inc(slot_done, 1)

            turn(-1)
            turn(0)
            if n_batch > 2:
                with pe.Fori(1, n_batch - 1) as b:
                    turn(b)
            if n_batch > 1:
                turn(n_batch - 1)
            turn(n_batch)


N_LOADS = 26
VECTOR_LINKS = 100

_INS = ['L0_attn_h', 'L0_attn_w_qc', 'L0_attn_w_qup', 'L0_attn_w_k', 'L0_attn_w_v', 'L0_attn_g_qnorm', 'L0_attn_g_knorm',
        'L0_attn_w_gate', 'L0_attn_b_gate', 'L0_attn_sink_logit', 'L0_attn_w_out_group', 'L0_attn_w_out',
        'L0_ffn_g1', 'L0_ffn_g2', 'L0_ffn_w_down', 'L0_ffn_wq', 'L0_ffn_wk', 'L0_ffn_wv', 'L0_ffn_w_up',
        'L0_ffn_router_w', 'L0_ffn_w1', 'L0_ffn_w2', 'L0_ffn_w3']


def kernel(**inputs):
    import concourse.bacc as bacc
    from concourse.bass_utils import run_bass_kernel_spmd

    nc = bacc.Bacc("TRN2", target_bir_lowering=False, num_devices=1)
    arrays, args = {}, []
    for name in _INS:
        a = np.ascontiguousarray(inputs[name])
        arrays[f"in_{name}"] = a
        args.append(nc.dram_tensor(f"in_{name}", a.shape, mybir.dt.from_np(a.dtype), kind="ExternalInput").ap())
    arrays["shape_constants"] = CONSTS
    arrays["shape_constants_bf16"] = CONSTS_BF
    args.append(nc.dram_tensor("shape_constants", CONSTS.shape, F32, kind="ExternalInput").ap())
    args.append(nc.dram_tensor("shape_constants_bf16", CONSTS_BF.shape, BF16, kind="ExternalInput").ap())
    args.append(nc.dram_tensor("out", (B, T, HID), F32, kind="ExternalOutput").ap())
    sandwich(nc, *args)
    r = run_bass_kernel_spmd(nc, [arrays], core_ids=[0])
    return r.results[0]["out"]
```

```python
import concourse.bass as bass
from concourse import mybir
from contextlib import ExitStack
import numpy as np

F32 = mybir.dt.float32
F32R = mybir.dt.float32r
BF16 = mybir.dt.bfloat16
ALU = mybir.AluOpType
ACT = mybir.ActivationFunctionType
AX = mybir.AxisListType

B, T, HID = 8, 512, 128
P = 128
NT = T // P
H, D, ROPE = 8, 64, 32
CR, WINDOW = 32, 64
NBLK = T // CR
H2, D2, L2 = 16, 4, 64
E, F = 8, 256
FC = F // P
BANK = 512
NEG = -1.0e30
EPS5, EPS6 = 1e-5, 1e-6
SPLIT2 = 8
OW = D + 1
RW = 32

CONST_COLS = {}


def shape_constants():
    p = np.arange(P)
    cols, at = [], 0

    def add(name, a):
        nonlocal at
        a = np.asarray(a, np.float32).reshape(P, -1)
        CONST_COLS[name] = (at, a.shape[1])
        cols.append(a)
        at += a.shape[1]

    def rope(width, theta=10000.0):
        half = width // 2
        inv = (np.float32(1.0) / np.power(np.float32(theta), np.arange(half, dtype=np.float32) * np.float32(2.0) / np.float32(width))).astype(np.float32)
        ang = (np.arange(T, dtype=np.float32)[:, None] * inv[None, :]).astype(np.float32)
        ang = ang.reshape(NT, P, half).transpose(1, 0, 2)
        return np.cos(ang.astype(np.float64)), np.sin(ang.astype(np.float64))

    c, s = rope(ROPE)
    add("cos1", np.repeat(c[:, :, None, :], 2, axis=2))
    add("sin1", np.repeat(s[:, :, None, :], 2, axis=2))
    c, s = rope(D2)
    add("cos2", c)
    add("sin2", s)
    add("ident", np.eye(P))
    q, k = p[:, None], p[None, :]
    neg = lambda ok: np.where(ok, 0.0, NEG)
    back = np.concatenate([q + P - k, q - k], 1)
    add("near_q", neg((back >= 0) & (back < WINDOW)))
    add("causal_q", neg(q - k >= 0))
    kk, qq = p[:, None], p[None, :]
    add("near_own_k", neg((qq - kk >= 0) & (qq - kk < WINDOW)))
    add("near_prev_k", neg(qq + P - kk < WINDOW)[:, :P // 2])
    add("far_own_k", neg(qq - kk >= WINDOW))
    add("far_prev_k", neg(qq + P - kk >= WINDOW))
    add("causal_k", neg(qq - kk >= 0))
    tok = np.arange(NT)[None, :, None] * P + p[:, None, None]
    add("block_valid", neg((np.arange(NBLK)[None, None, :] + 1) * CR - 1 <= tok))
    blk = (np.arange(NT)[None, :, None] * P + p[:, None, None]) // CR
    add("mean_rows", (blk == (np.arange(P) % NBLK)[None, None, :]) / CR)
    add("head_rows", (p[:, None] // NBLK) == np.arange(H)[None, :])
    row = p
    quad, tile, kind, head = row // 64, row // 16 % 4, row // 8 % 2, row // 2 % 4
    add("shift_head", head[:, None] == np.arange(4)[None, :])
    add("shift_pick", np.repeat(((quad * 4 + tile) * 2 + kind)[:, None, None] == np.arange(16)[None, :, None], P, axis=2))
    add("iota8", np.tile(np.arange(E, dtype=np.float32), (P, 1)))
    narrow, wide = [], []
    for (name, (at, n)), a in zip(list(CONST_COLS.items()), cols):
        if name in BF_CONSTS:
            BF_COLS[name] = (sum(c.shape[1] for c in narrow), n)
            narrow.append(a)
        if name not in BF_CONSTS or name == "ident":
            CONST_COLS[name] = (sum(c.shape[1] for c in wide), n)
            wide.append(a)
    return np.concatenate(wide, 1), np.concatenate(narrow, 1).astype(mybir.dt.np(BF16))


BF_COLS = {}
BF_CONSTS = ["ident", "near_q", "causal_q", "near_own_k", "near_prev_k", "far_own_k",
             "far_prev_k", "causal_k", "shift_pick"]
CONSTS, CONSTS_BF = shape_constants()


class Signal:

    def __init__(self, sem, per):
        self.sem, self.per, self.given = sem, per, 0

    def at(self, b, n):
        assert 0 <= n <= self.per
        return b * self.per + n


def sandwich(nc, x, w_qc, w_qup, w_k, w_v, g_q, g_k, w_gate, b_gate, sink, w_og, w_out,
             g1, g2, w_down, wq2, wk2, wv2, w_up, router_w, w1, w2, w3, consts, consts_bf, out, n_batch=B):
    ctx = ExitStack()
    with ctx:
        def sb(name, shape, dt=F32):
            return ctx.enter_context(nc.sbuf_tensor(name, shape, dt))

        def sem(name):
            return ctx.enter_context(nc.semaphore(name))

        def signal(name, per):
            return Signal(sem(name), per)

        ncols = CONSTS.shape[1]
        cst = sb("cst", [P, ncols])
        cst_bf = sb("cst_bf", [P, CONSTS_BF.shape[1]], BF16)

        def con(name):
            a, n = CONST_COLS[name]
            return cst[:, a:a + n]

        def con_bf(name):
            a, n = BF_COLS[name]
            return cst_bf[:, a:a + n]

        ident, ident_bf = con("ident"), con_bf("ident")
        w_qc_sb = sb("w_qc_sb", [HID, 32])
        w_out_sb = sb("w_out_sb", [64, 2, HID])
        w_down_sb = sb("w_down_sb", [HID, L2])
        w_proj = sb("w_proj", [HID, H * D + 2 * D])
        w_fold = sb("w_fold", [P, 4, HID])
        w_qkv2 = sb("w_qkv2", [HID, 3 * L2])
        w_up_sb = sb("w_up_sb", [P, HID])
        router_sb = sb("router_sb", [HID, E])
        w13_sb = sb("w13_sb", [HID, E, 2, F])
        w2_sb = sb("w2_sb", [P, E, FC, HID])
        gain_key = sb("gain_key", [P, D])
        gain_col = sb("gain_col", [P, 1])
        gain_in = sb("gain_in", [P, 2, D])
        g1_sb = sb("g1_sb", [P, HID])
        g2_sb = sb("g2_sb", [P, HID])
        bgate_sb = sb("bgate_sb", [P, 3])
        sink_sb = sb("sink_sb", [P, H])
        minus_half = sb("minus_half", [P, NT * (H + 1)])

        xin = sb("xin", [P, NT, HID])
        hn = sb("hn", [P, NT, HID])
        hT = sb("hT", [HID, T])
        stats = sb("stats", [P, NT, 6])
        mv = sb("mv", [P, NT, 2])
        var_in = sb("var_in", [P, NT * (H + 1)])
        rstd = sb("rstd", [P, NT * (H + 1)])
        qkv = sb("qkv", [P, NT, H + 2, D])
        sq = sb("sq", [P, H + 1, D])
        sumsq = sb("sumsq", [P, NT, H + 1])
        ropeA = sb("ropeA", [P, H + 1, ROPE])
        ropeB = sb("ropeB", [P, H + 1, ROPE])
        qsplit = sb("qsplit", [P, NT, H, 2, D])
        kdup = sb("kdup", [P, NT, 2, D])
        qT = sb("qT", [P, H, NT, P], F32R)
        kT_hi = sb("kT_hi", [P, T], F32R)
        kT_lo = sb("kT_lo", [P, T], F32R)
        va = sb("va", [P, NT, OW])
        comp_gate = sb("comp_gate", [P, RW])
        kmean = sb("kmean", [P, NBLK])
        vmean = sb("vmean", [P, H, D])
        cgT = sb("cgT", [P, 2, T])
        cg = sb("cg", [P, NT, H, RW])
        cs = sb("cs", [P, NT, H, NBLK])
        cexp = cs
        cmax = sb("cmax", [P, NT, H])
        csum = sb("csum", [P, NT, H])
        csink = sb("csink", [P, NT, H])
        ccoef = sb("ccoef", [P, NT, H])
        gz = sb("gz", [P, NT * H, 3])
        gate = sb("gate", [P, NT * H, 3])
        gsum = sb("gsum", [P, NT * H])
        pcT = sb("pcT", [P, T])
        nmax = sb("nmax", [P, 2, NT, 2, 4])
        nmax_bf = sb("nmax_bf", [P, 64, 2], BF16)
        masked = sb("masked", [P, 4, 2 * P], BF16)
        shiftT = sb("shiftT", [P, 4, P], BF16)
        prob_pairs = [sb(f"prob_pair{i}", [P, 2, BANK]) for i in range(2)]
        oT = [sb(f"oT{i}", [P, 2, BANK]) for i in range(2)]
        probs = [prob_pairs[n // 2][:, n % 2, :] for n in range(4)]
        left_t = prob_pairs[0][0:64, :, :].rearrange("p a n -> p (a n)")[:, 0:6 * P].rearrange("p (c n) -> p c n", c=6)
        w_qup_sb = prob_pairs[1][0:32, 0, 0:H * D]
        w_og_sb = prob_pairs[1][:, 1, 0:4 * 64].rearrange("p (c n) -> p c n", c=4)
        w_qkv2_in = prob_pairs[1][0:L2, 1, 4 * 64:4 * 64 + 3 * L2].rearrange("p (w n) -> p w n", w=3)
        on = sb("on", [P, 2, NT, H, OW])
        cargs = sb("cargs", [P, 3, NT, H])
        cexps = sb("cexps", [P, 3, NT, H])
        nsink = sb("nsink", [P, NT, H])
        zfull = sb("zfull", [P, NT, H])
        zwin = sb("zwin", [P, NT, H])
        coef = sb("coef", [P, 2, NT, H])
        spare_s = qsplit[:, :, :, :, :].rearrange("p i h s d -> p (i h s d)")
        mixa, mixb = ([spare_s[:, (2 * m + n) * H * D:(2 * m + n + 1) * H * D].rearrange("p (h d) -> p h d", h=H)
                       for n in range(2)] for m in range(2))
        mixT = [spare_s[:, (4 + n) * H * D:(5 + n) * H * D].rearrange("p (c n) -> p c n", c=4) for n in range(2)]
        x1 = sb("x1", [P, NT, HID])
        x1_last = sb("x1_last", [P, NT, HID])
        ffn_in = sb("ffn_in", [P, NT, HID])
        ffn_in_last = sb("ffn_in_last", [P, NT, HID])
        var_end = sb("var_end", [P, NT])
        rstd_end = sb("rstd_end", [P, NT])
        ms_end = sb("ms_end", [P, NT])
        ms = sb("ms", [P, NT])
        scrap = sb("scrap", [P, 1])
        qkv2 = sb("qkv2", [P, NT, 3 * L2])
        n_parts = NT * H2 * SPLIT2 * D2
        parts2 = spare_s[:, 0:n_parts].bitcast(BF16).rearrange("p (w n s d) -> p w n s d", w=2, s=SPLIT2, d=D2)
        n_rot = NT * 2 * H2 * 2
        rot = [spare_s[:, n_parts + n * n_rot:n_parts + (n + 1) * n_rot].rearrange("p (i h r) -> p i h r", i=NT, r=2) for n in range(4)]
        at = n_parts + 4 * n_rot
        n_qk = 2 * NT * L2
        qk2 = spare_s[:, at:at + n_qk].rearrange("p (w n d) -> p w n d", w=2, d=D2)
        rem = spare_s[:, at + n_qk:at + 2 * n_qk].rearrange("p (w n d) -> p w n d", w=2, d=D2)
        q2T = sb("q2T", [P, 4, T], BF16)
        k2Z = sb("k2Z", [P, 4, 4, T], BF16)
        va2 = sb("va2", [P, NT, H2, RW])
        nmax2 = sb("nmax2", [P, H2, NT])
        nmax2_bf = sb("nmax2_bf", [P, 4, 2, 4, NT], BF16)
        shift2_sb = sb("shift2_sb", [P, P], BF16)
        probs2 = probs + [oT[n][:, 1, :] for n in range(2)]
        o2T = [oT[n][:, 0, :] for n in range(2)]
        rz2 = sb("rz2", [P, NT, 4])
        o2n = sb("o2n", [P, NT, 2 * H2, D2])
        res = sb("res", [P, NT, HID])
        tT = sb("tT", [HID, T])
        logit = sb("logit", [P, NT, E])
        top1 = sb("top1", [P, NT])
        top2 = sb("top2", [P, NT])
        pick = sb("pick", [P, NT, E])
        hot1 = sb("hot1", [P, NT, E])
        hot2 = sb("hot2", [P, NT, E])
        wtop = sb("wtop", [P, 2, NT])
        egate = sb("egate", [P, NT, E])
        spare = on[:, :, :, :, :].rearrange("p k i h d -> p (k i h d)")
        hid = [spare[:, n * FC * T:(n + 1) * FC * T].rearrange("p (c t) -> p c t", c=FC) for n in range(2)]
        th = [spare[:, (2 * FC + n) * T:(2 * FC + n + 1) * T] for n in range(2)]
        o2nT = spare[:, 3 * FC * T:(3 * FC + 1) * T]
        t_sb = spare[:, (3 * FC + 1) * T:(3 * FC + 2) * T].rearrange("p (i c) -> p i c", i=NT)
        spare_q = qkv[:, :, :, :].rearrange("p i h d -> p (i h d)")
        yg = [spare_q[:, n * T:(n + 1) * T].rearrange("p (i c) -> p i c", i=NT) for n in range(2)]
        acc = spare_q[:, 2 * T:3 * T].rearrange("p (i c) -> p i c", i=NT)
        yout = spare_q[:, 3 * T:4 * T].rearrange("p (i c) -> p i c", i=NT)

        ps = ctx.enter_context(nc.psum_tensor("ps", [P, 8, BANK], F32))

        def bank(n, k=1):
            return ps[:, n:n + k, :] if k > 1 else ps[:, n, :]

        loaded = sem("loaded")
        cast_done = sem("cast_done")
        folded = sem("folded")
        fold_psum = sem("fold_psum")
        padded = sem("padded")
        experts_loaded = sem("experts_loaded")
        slot_done = sem("slot_done")
        x_loaded = signal("x_loaded", 16)
        x_again = signal("x_again", 16)
        var1_ready = signal("var1_ready", 1 + NT)
        rstd1_ready = signal("rstd1_ready", 1 + NT)
        var2_ready = signal("var2_ready", 3)
        rstd2_ready = signal("rstd2_ready", 3)
        var3_ready = signal("var3_ready", 2)
        rstd3_ready = signal("rstd3_ready", 2)
        h_ready = signal("h_ready", 1)
        hT_psum = signal("hT_psum", 1)
        hT_ready = signal("hT_ready", 1)
        kv_psum = signal("kv_psum", 1)
        kv_ready = signal("kv_ready", 1)
        qkv_psum = signal("qkv_psum", NT)
        qkv_ready = signal("qkv_ready", NT)
        sq_ready = signal("sq_ready", NT)
        sq_used = signal("sq_used", NT)
        rope_done = signal("rope_done", NT)
        v_ready = signal("v_ready", 1)
        split_ready = signal("split_ready", NT)
        qT_psum = signal("qT_psum", 2 * NT)
        qT_ready = signal("qT_ready", 2 * NT)
        kT_psum = signal("kT_psum", 1)
        k_ready = signal("k_ready", 1)
        vmean_psum = signal("vmean_psum", 1)
        vmean_ready = signal("vmean_ready", 1)
        cgT_psum = signal("cgT_psum", 2)
        cgT_ready = signal("cgT_ready", 2)
        cg_psum = signal("cg_psum", 2)
        cg_ready = signal("cg_ready", 2)
        cexp_arg = signal("cexp_arg", 1)
        cexp_ready = signal("cexp_ready", 1)
        pc_ready = signal("pc_ready", 1)
        pcT_psum = signal("pcT_psum", 1)
        pcT_ready = signal("pcT_ready", 1)
        s_psum = signal("s_psum", NT * H)
        max_done = signal("max_done", NT * H)
        nmax_split = signal("nmax_split", 1)
        shift_psum = signal("shift_psum", 1)
        shift_ready = signal("shift_ready", 1)
        coef_arg = signal("coef_arg", 1)
        coef_exp = signal("coef_exp", 1)
        coef_done = signal("coef_done", 1)
        NU1 = 28
        st_psum = signal("st_psum", NU1)
        exp_done = signal("exp_done", NU1)
        pv_done = signal("pv_done", NU1)
        oT_ready = signal("oT_ready", 8)
        on_psum = signal("on_psum", 16)
        on_ready = signal("on_ready", 16)
        comp_psum = signal("comp_psum", NT)
        near_scaled = signal("near_scaled", NT)
        mix_ready = signal("mix_ready", NT)
        mixT_psum = signal("mixT_psum", NT)
        mixT_ready = signal("mixT_ready", NT)
        mixT_used = signal("mixT_used", NT)
        attn_ready = signal("attn_ready", 1)
        x1_ready = signal("x1_ready", 1)
        h2_ready = signal("h2_ready", 1)
        h2T_psum = signal("h2T_psum", 1)
        h2T_ready = signal("h2T_ready", 1)
        qkv2_psum = signal("qkv2_psum", 1)
        qkv2_ready = signal("qkv2_ready", 1)
        va2_ready = signal("va2_ready", 1)
        parts2_ready = signal("parts2_ready", 1)
        q2T_psum = signal("q2T_psum", 2)
        q2T_ready = signal("q2T_ready", 2)
        k2T_psum = signal("k2T_psum", 2)
        k2Z_low = signal("k2Z_low", 2)
        k2Z_high = signal("k2Z_high", 2)
        UNITS_MAX2 = [(g, i, hh, n) for g in range(4) for i in range(NT)
                      for n in [{0: 4, 1: 2}.get(i, 1)] for hh in range(0, 4, n)]
        s2_psum = signal("s2_psum", len(UNITS_MAX2))
        max2_done = signal("max2_done", len(UNITS_MAX2))
        nmax2_split = signal("nmax2_split", 1)
        shift2_psum = signal("shift2_psum", 1)
        shift2_ready = signal("shift2_ready", 1)
        shift2_placed = signal("shift2_placed", 16 * 8)
        slots_filled = signal("slots_filled", 1)
        NU2 = 4 * NT * 4
        st2_psum = signal("st2_psum", NU2)
        exp2_done = signal("exp2_done", NU2)
        pv2_done = signal("pv2_done", NU2 // 4)
        o2T_ready = signal("o2T_ready", 4)
        o2n_psum = signal("o2n_psum", 4)
        o2n_ready = signal("o2n_ready", 4)
        o2nT_psum = signal("o2nT_psum", 1)
        o2nT_ready = signal("o2nT_ready", 1)
        up_psum = signal("up_psum", 1)
        res_ready = signal("res_ready", 1)
        res_sq = signal("res_sq", 1)
        t_ready = signal("t_ready", 1)
        tT_psum = signal("tT_psum", 1)
        tT_ready = signal("tT_ready", 1)
        router_psum = signal("router_psum", 1)
        wtop_arg = signal("wtop_arg", 1)
        wtop_exp = signal("wtop_exp", 1)
        NX = E * FC
        hid_psum = signal("hid_psum", NX)
        th_ready = signal("th_ready", NX)
        hid_ready = signal("hid_ready", NX)
        y_psum = signal("y_psum", E)
        yg_ready = signal("yg_ready", E)
        acc_done = signal("acc_done", E)
        out_ready = signal("out_ready", 1)
        out_stored = signal("out_stored", 16)
        vector_chain = sem("vector_chain")

        def units1(i):
            near, far = 0, 1
            own = (near, i, 0, P, "near_own_k")
            if i == 0:
                return [[own], [(far, 0, 0, P, "far_own_k")]]
            return [[own],
                    [(near, i - 1, 0, P // 2, "near_prev_k"), (far, i, P // 2, P // 2, "far_own_k")],
                    [(far, i - 1, 0, P, "far_prev_k")]] + [[(far, j, 0, P, None)] for j in range(i - 1)]

        UNITS1 = [(quad, i, u, n) for quad in range(2) for i in range(NT) for n, u in enumerate(units1(i))]
        assert len(UNITS1) == NU1
        FIRST1 = [u for u in range(NU1) if UNITS1[u][3] == 0] + [NU1]

        def spread(*stages):
            marks = []
            for name, n, ends in stages:
                marks += [(float(np.interp((k + 0.5) / n, np.linspace(0, 1, len(ends)), ends)), name) for k in range(n)]
            return [name for _, name in sorted(marks, key=lambda m: m[0])]

        STEPS = {"attention": NU1 + 4, "prepare2": 2 * 15, "maxima2": len(UNITS_MAX2) + 3,
                 "mix": 2 * 8, "prepare1": 2 * 12, "compressed": 5, "attention2": NU2 + 4,
                 "maxima1": NT * H + 3, "after2": 11, "experts": 4 * E + 8}
        SLOTS = [
            spread(("attention", STEPS["attention"], (0, 0.167, 0.333, 0.5, 0.667, 0.833, 1)),
                   ("prepare2", STEPS["prepare2"], (0, 0.07, 0.15, 0.22, 0.3, 0.36, 0.42)),
                   ("maxima2", STEPS["maxima2"], (0.42, 0.5, 0.577, 0.65, 0.73, 0.807, 0.88))),
            spread(("prepare1", 4, (0, 0.01, 0.06)),
                   ("mix", STEPS["mix"], (0.02, 0.077, 0.133, 0.19, 0.247, 0.303, 0.36)),
                   ("prepare1", STEPS["prepare1"] - 4, (0.36, 0.467, 0.573, 0.68, 0.787, 0.893, 1)),
                   ("attention2", STEPS["attention2"], (0, 0.133, 0.267, 0.4, 0.533, 0.667, 0.8)),
                   ("after2", STEPS["after2"], (0.82, 0.858, 0.897, 0.935, 0.973, 1.012, 1.05))),
            spread(("compressed", 2, (0, 0.015, 0.03)),
                   ("compressed", 3, (0.05, 0.15, 0.25)),
                   ("experts", STEPS["experts"], (0, 0.167, 0.333, 0.5, 0.667, 0.833, 1)),
                   ("maxima1", STEPS["maxima1"], (0.1, 0.258, 0.417, 0.575, 0.733, 0.892, 1.05))),
            spread(("prepare2", STEPS["prepare2"], (0, 0.067, 0.133, 0.2, 0.267, 0.333, 0.4)),
                   ("maxima2", STEPS["maxima2"], (0.4, 0.483, 0.567, 0.65, 0.733, 0.817, 0.9)),
                   ("experts", STEPS["experts"], (0.05, 0.208, 0.367, 0.525, 0.683, 0.842, 1))),
        ]
        SLOTS_ENGINES = 4

        def take(slot, **stages):
            for name in SLOTS[slot]:
                if name in stages:
                    next(stages[name])
            for name, stage in stages.items():
                assert next(stage, "end") == "end", name

        def slots_before(b, slot):
            return 3 * (b + 1) + slot - (2 if is_end(b) else 1)

        def in_range(b):
            return not isinstance(b, int) or 0 <= b < n_batch

        def is_first(b):
            return isinstance(b, int) and b == 0

        def is_last(b):
            return isinstance(b, int) and b == n_batch - 1

        def is_end(b):
            return isinstance(b, int) and b == n_batch

        def x1_of(b):
            return x1_last if is_last(b) else x1

        def ffn_in_of(b):
            return ffn_in_last if is_last(b) else ffn_in

        block = ctx.enter_context(nc.Block())

        def row_bcast(v, n):
            return v.rearrange("(a n) -> a n", a=1).partition_broadcast(P)

        loads = [
            (cst[:, :], consts), (cst_bf[:, :], consts_bf), (w_qc_sb[:, :], w_qc), (w_qup_sb[:, :], w_qup),
            (w_og_sb[:, 0:2, :], w_og[0, :, :].rearrange("(c p) n -> p c n", p=P)),
            (w_og_sb[:, 2:4, :], w_og[1, :, :].rearrange("(c p) n -> p c n", p=P)),
            (w_out_sb[:, :, :], w_out.rearrange("(g p) n -> p g n", p=64)),
            (w_down_sb[:, :], w_down),
            (w_qkv2_in[:, 0, :], wq2), (w_qkv2_in[:, 1, :], wk2), (w_qkv2_in[:, 2, :], wv2),
            (w_proj[:, H * D:H * D + D], w_k), (w_proj[:, H * D + D:], w_v),
            (w_up_sb[0:L2, :], w_up), (router_sb[:, :], router_w),
            (gain_col[0:D, :], g_q.rearrange("(n a) -> n a", a=1)), (gain_col[D:P, :], g_q.rearrange("(n a) -> n a", a=1)),
            (gain_in[:, 0, :], row_bcast(g_q, D)), (gain_in[:, 1, :], row_bcast(g_k, D)),
            (g1_sb[:, :], row_bcast(g1, HID)), (g2_sb[:, :], row_bcast(g2, HID)),
            (bgate_sb[:, :], row_bcast(b_gate, 3)), (sink_sb[:, :], row_bcast(sink, H)),
            (comp_gate[0:D, NBLK:NBLK + 3], w_gate), (comp_gate[D:P, NBLK:NBLK + 3], w_gate),
        ]
        expert_loads = [
            (w13_sb[:, :, 0, :], w1.rearrange("e d f -> d e f")),
            (w13_sb[:, :, 1, :], w3.rearrange("e d f -> d e f")),
            (w2_sb[:, :, :, :].rearrange("p e c n -> p (e c) n"), w2.rearrange("e (c p) n -> p (e c) n", p=P)),
        ]

        @block.sync
        def _(sync):
            sync.dma_start(xin[:, :, :], x[0:1, :, :].rearrange("b (i p) c -> p (b i) c", p=P)).then_inc(x_loaded.sem, 16)
            sync.sem_inc(out_stored.sem, 1)
            sync.wait_ge(padded, 1)
            for dst, src in loads[:N_LOADS // 2]:
                sync.dma_start(dst, src).then_inc(loaded, 16)
            assert len(loads) == N_LOADS
            for dst, src in expert_loads:
                sync.dma_start(dst, src).then_inc(experts_loaded, 16)

            def rows(b):
                return bass.ds(b, 1) if not isinstance(b, int) else slice(b, b + 1)

            def load(b, sig):
                sync.dma_start(xin[:, :, :], x[rows(b), :, :].rearrange("b (i p) c -> p (b i) c", p=P)).then_inc(sig.sem, 16)

            def place_shifts(b):
                sync.wait_ge(shift2_ready.sem, shift2_ready.at(b, 1))
                for n in range(8):
                    hh, part = n // 2, n % 2
                    row = RW * hh + 6 * D2 + part
                    sync.dma_start(q2T[row:row + 1, :, :].rearrange("a g (i n) -> a (g i) n", i=NT),
                                   shift2_sb[16 * n:16 * (n + 1), :]).then_inc(shift2_placed.sem, 16)

            def turn(b):
                if in_range(b + 1) and not is_first(b + 1):
                    if is_first(b):
                        sync.wait_ge(h_ready.sem, h_ready.at(b, 1))
                    else:
                        sync.wait_ge(x1_ready.sem, x1_ready.at(b - 1, 1))
                    load(b + 1, x_loaded)
                if in_range(b - 1) and not is_end(b):
                    place_shifts(b - 1)
                if in_range(b):
                    if in_range(b + 1):
                        sync.wait_ge(h_ready.sem, h_ready.at(b + 1, 1))
                    elif is_first(b):
                        sync.wait_ge(h_ready.sem, h_ready.at(b, 1))
                    else:
                        sync.wait_ge(x1_ready.sem, x1_ready.at(b - 1, 1))
                    load(b, x_again)
                if is_last(b):
                    place_shifts(b)
                if in_range(b - 1):
                    sync.wait_ge(out_ready.sem, out_ready.at(b - 1, 1))
                    sync.dma_start(out[rows(b - 1), :, :].rearrange("b (i p) c -> p (b i) c", p=P), yout[:, :, :]).then_inc(out_stored.sem, 16)

            turn(0)
            if n_batch > 2:
                with sync.Fori(1, n_batch - 1) as b:
                    turn(b)
            if n_batch > 1:
                turn(n_batch - 1)
            turn(n_batch)
            sync.wait_ge(out_stored.sem, out_stored.at(n_batch - 1, 16) + 1)

        @block.gpsimd
        def _(pool):
            pool.memset(w_up_sb[:, :], 0.0)
            pool.memset(comp_gate[:, :], 0.0).then_inc(padded, 1)
            pool.memset(minus_half[:, :], -0.5)
            pool.memset(va[:, :, D:OW], 1.0)
            pool.memset(k2Z[:, :, :, :], 0.0)
            pool.memset(o2n[:, :, H2:, :], 0.0)
            pool.memset(va2[:, :, :, :], 0.0).then_inc(padded, 1)
            pool.wait_ge(padded, 2)
            pool.memset(va2[:, :, :, D2:D2 + 1], 1.0).then_inc(padded, 1)
            pool.wait_ge(cast_done, 1)

            def inverse_root(cols, dst=rstd, src=var_in):
                return pool.tensor_tensor(dst[:, 0:cols], src[:, 0:cols], minus_half[:, 0:cols], ALU.pow)

            def prepare1(b):
                for step in range(STEPS["prepare1"] // 2):
                    yield
                    if step == 0:
                        pool.wait_ge(var1_ready.sem, var1_ready.at(b, 1))
                        inverse_root(NT).then_inc(rstd1_ready.sem, 1)
                    if 4 <= step < 4 + NT:
                        i = step - 4
                        n = H + 1
                        pool.wait_ge(var1_ready.sem, var1_ready.at(b, i + 2))
                        pool.tensor_tensor(rstd[:, i * n:(i + 1) * n], var_in[:, i * n:(i + 1) * n], minus_half[:, 0:n],
                                           ALU.pow).then_inc(rstd1_ready.sem, 1)
                    if step == 8:
                        pool.tensor_copy(va[:, :, 0:D], qkv[:, :, H + 1, :]).then_inc(v_ready.sem, 1)
                    yield
                pool.wait_ge(v_ready.sem, v_ready.at(b, 1))

            def mix(b):
                for step in range(STEPS["mix"] // 2):
                    yield
                    if 1 <= step < 1 + NT:
                        i = step - 1
                        pool.wait_ge(coef_done.sem, coef_done.at(b, 1))
                        if i >= 2:
                            pool.wait_ge(mix_ready.sem, mix_ready.at(b, i - 1))
                        pool.tensor_tensor(mixb[i % 2][:, :, :], on[:, 0, i, :, 0:D],
                                           coef[:, 0, i, :].unsqueeze(2).to_broadcast([P, H, D]),
                                           ALU.mult).then_inc(near_scaled.sem, 1)
                    yield
                pool.wait_ge(near_scaled.sem, near_scaled.at(b, NT))

            def prepare2(b):
                for step in range(STEPS["prepare2"] // 2):
                    yield
                    if step in (0, 2, 4):
                        use = step // 2 + 1
                        pool.wait_ge(var2_ready.sem, var2_ready.at(b, use))
                        inverse_root(NT).then_inc(rstd2_ready.sem, 1)
                    if step == 0:
                        pool.memset(parts2[:, 0, :, 6:8, :], 0.0)
                        pool.memset(parts2[:, 1, :, 6:8, :], 1.0).then_inc(slots_filled.sem, 1)
                    yield
                pool.wait_ge(slots_filled.sem, slots_filled.at(b, 1))
                pool.wait_ge(rstd2_ready.sem, rstd2_ready.at(b, 3))

            def after2(b):
                for step in range(STEPS["after2"]):
                    if step == 3:
                        pool.wait_ge(var3_ready.sem, var3_ready.at(b, 1))
                        inverse_root(NT, rstd_end, var_end).then_inc(rstd3_ready.sem, 1)
                    yield

            def experts(b):
                for step in range(STEPS["experts"]):
                    if step >= 9 and (step - 9) % 4 == 0 and (step - 9) // 4 < E:
                        e = (step - 9) // 4
                        pool.wait_ge(yg_ready.sem, yg_ready.at(b, e + 1))
                        if e >= 1:
                            pool.wait_ge(acc_done.sem, acc_done.at(b, e))
                        so_far = acc if e >= 1 else res
                        pool.tensor_tensor(acc[:, :, :], so_far[:, :, :], yg[e % 2][:, :, :], ALU.add).then_inc(acc_done.sem, 1)
                    yield
                pool.wait_ge(acc_done.sem, acc_done.at(b, E))

            def finish(b):
                pool.wait_ge(var3_ready.sem, var3_ready.at(b, 2))
                inverse_root(NT, rstd_end, var_end).then_inc(rstd3_ready.sem, 1)

            def turn(b):
                if not is_end(b) and (in_range(b) or in_range(b - 1)):
                    pool.wait_ge(slot_done, SLOTS_ENGINES * slots_before(b, 0))
                    take(0, **({"prepare2": prepare2(b - 1)} if in_range(b - 1) else {}))
                    pool.sem_inc(slot_done, 1)
                stages = {}
                if in_range(b):
                    stages["mix"] = mix(b)
                if in_range(b + 1):
                    stages["prepare1"] = prepare1(b + 1)
                if in_range(b - 1):
                    stages["after2"] = after2(b - 1)
                if not is_first(b + 1):
                    pool.wait_ge(slot_done, SLOTS_ENGINES * slots_before(b, 1))
                take(1, **stages)
                pool.sem_inc(slot_done, 1)
                stages = {}
                if in_range(b - 1):
                    stages["experts"] = experts(b - 1)
                if is_last(b):
                    stages["prepare2"] = prepare2(b)
                pool.wait_ge(slot_done, SLOTS_ENGINES * slots_before(b, 2))
                take(3 if is_last(b) else 2, **stages)
                pool.sem_inc(slot_done, 1)
                if in_range(b - 1):
                    finish(b - 1)

            turn(-1)
            turn(0)
            if n_batch > 2:
                with pool.Fori(1, n_batch - 1) as b:
                    turn(b)
            if n_batch > 1:
                turn(n_batch - 1)
            turn(n_batch)

        @block.scalar
        def _(act):
            act.wait_ge(padded, 1)
            for dst, src in loads[N_LOADS // 2:]:
                act.dma_start(dst, src).then_inc(loaded, 16)
            act.wait_ge(fold_psum, 1)
            flat = ps[:, 0:2, :].rearrange("p a n -> p (a n)")
            nc.scalar.activation(left_t[:, 0:5, :].rearrange("p c n -> p (c n)"), flat[0:64, 0:5 * P], ACT.Copy)
            nc.scalar.activation(left_t[0:32, 5, :], flat[0:32, 5 * P:6 * P], ACT.Copy).then_inc(folded, 1)
            act.wait_ge(fold_psum, 2)
            nc.scalar.activation(w_proj[:, 0:H * D], bank(2), ACT.Copy).then_inc(folded, 1)
            nc.scalar.activation(w_fold[:, :, :], bank(3).rearrange("p (c n) -> p c n", c=4), ACT.Copy).then_inc(folded, 1)
            nc.scalar.activation(w_qkv2[:, :], ps[:, 4, 0:3 * L2], ACT.Copy).then_inc(folded, 1)

            def copy(dst, src):
                return nc.scalar.activation(dst, src, ACT.Copy)

            def prepare1(b):
                for step in range(STEPS["prepare1"] // 2):
                    yield
                    if step == 1:
                        act.wait_ge(hT_psum.sem, hT_psum.at(b, 1))
                        copy(hT[:, :], bank(4)).then_inc(hT_ready.sem, 1)
                    if step == 2:
                        if not (isinstance(b, int) and b < 3):
                            act.wait_ge(out_stored.sem, out_stored.at(b - 3, 16) + 1)
                        act.wait_ge(kv_psum.sem, kv_psum.at(b, 1))
                        copy(qkv[:, :, H:, :].rearrange("p i h d -> p i (h d)"), bank(7).rearrange("p (i n) -> p i n", i=NT)).then_inc(kv_ready.sem, 1)
                        act.wait_ge(kv_ready.sem, kv_ready.at(b, 1))
                    if 2 <= step < 2 + NT:
                        i = step - 2
                        act.wait_ge(qkv_psum.sem, qkv_psum.at(b, i + 1))
                        copy(qkv[:, i, 0:H, :].rearrange("p h d -> p (h d)"), bank(5 + i % 2)).then_inc(qkv_ready.sem, 1)
                    if 3 <= step < 3 + NT:
                        i = step - 3
                        if i >= 1:
                            act.wait_ge(sq_used.sem, sq_used.at(b, i))
                        act.wait_ge(qkv_ready.sem, qkv_ready.at(b, i + 1))
                        nc.scalar.activation(sq[:, :, :], qkv[:, i, 0:H + 1, :], ACT.Square).then_inc(sq_ready.sem, 1)
                    if 6 <= step < 6 + NT:
                        i = step - 6
                        for quad in range(2):
                            act.wait_ge(qT_psum.sem, qT_psum.at(b, 2 * i + quad + 1))
                            copy(qT[:, 4 * quad:4 * quad + 4, i, :], bank(5 + quad).rearrange("p (h n) -> p h n", n=P)).then_inc(qT_ready.sem, 1)
                    yield
                act.wait_ge(qT_ready.sem, qT_ready.at(b, 2 * NT))

            def compressed(b):
                for step in range(STEPS["compressed"]):
                    if step == 0:
                        for quad in range(2):
                            act.wait_ge(cgT_psum.sem, cgT_psum.at(b, quad + 1))
                            copy(cgT[:, quad, :], bank(6 - quad)).then_inc(cgT_ready.sem, 1)
                    if step == 1:
                        for quad in range(2):
                            act.wait_ge(cg_psum.sem, cg_psum.at(b, quad + 1))
                            copy(cg[:, :, 4 * quad:4 * quad + 4, :].rearrange("p i h r -> p i (h r)"),
                                 bank(7 - quad).rearrange("p (i r) -> p i r", i=NT)).then_inc(cg_ready.sem, 1)
                    if step == 3:
                        act.wait_ge(cexp_arg.sem, cexp_arg.at(b, 1))
                        nc.scalar.activation(cexp[:, :, :, :], cs[:, :, :, :], ACT.Exp)
                        nc.scalar.activation(csink[:, :, :], csink[:, :, :], ACT.Exp)
                        nc.scalar.activation(gz[:, :, :], gz[:, :, :], ACT.Exp, scale=-1.0).then_inc(cexp_ready.sem, 1)
                    yield
                act.wait_ge(cexp_ready.sem, cexp_ready.at(b, 1))

            def maxima1(b):
                for _ in range(NT * H):
                    yield
                act.wait_ge(pcT_psum.sem, pcT_psum.at(b, 1))
                copy(pcT[:, :], bank(7)).then_inc(pcT_ready.sem, 1)
                yield
                yield
                act.wait_ge(coef_arg.sem, coef_arg.at(b, 1))
                nc.scalar.activation(cexps[:, :, :, :], cargs[:, :, :, :], ACT.Exp).then_inc(coef_exp.sem, 1)
                yield
                act.wait_ge(coef_exp.sem, coef_exp.at(b, 1))

            def attention(b):
                for step in range(STEPS["attention"]):
                    for g in range(8):
                        if step == FIRST1[g + 1] + 1:
                            act.wait_ge(pv_done.sem, pv_done.at(b, FIRST1[g + 1]))
                            if g >= 2:
                                act.wait_ge(on_psum.sem, on_psum.at(b, 2 * (g - 1)))
                            copy(oT[g % 2][0:OW, :, :], ps[0:OW, 2:4, :]).then_inc(oT_ready.sem, 1)
                    if step < NU1:
                        u = step
                        act.wait_ge(st_psum.sem, st_psum.at(b, u + 1))
                        if u >= 4:
                            act.wait_ge(pv_done.sem, pv_done.at(b, u - 3))
                        nc.scalar.activation(probs[u % 4], bank(u % 2), ACT.Exp).then_inc(exp_done.sem, 1)
                    for g in range(8):
                        for kind in range(2):
                            if step == FIRST1[g + 1] + 2 + kind:
                                act.wait_ge(on_psum.sem, on_psum.at(b, 2 * g + kind + 1))
                                quad, i = g // NT, g % NT
                                copy(on[:, kind, i, 4 * quad:4 * quad + 4, :].rearrange("p h d -> p (h d)"),
                                     ps[:, 4, 0:4 * OW]).then_inc(on_ready.sem, 1)
                    yield
                act.wait_ge(on_ready.sem, on_ready.at(b, 16))

            def mix(b):
                for step in range(STEPS["mix"] // 2):
                    yield
                    if 2 <= step < 2 + NT:
                        i = step - 2
                        act.wait_ge(mixT_psum.sem, mixT_psum.at(b, i + 1))
                        if i >= 2:
                            act.wait_ge(mixT_used.sem, mixT_used.at(b, i - 1))
                        copy(mixT[i % 2][:, :, :], bank(6).rearrange("p (c n) -> p c n", c=4)).then_inc(mixT_ready.sem, 1)
                    if step == 3 + NT:
                        act.wait_ge(mixT_used.sem, mixT_used.at(b, NT))
                        if in_range(b + 1):
                            act.wait_ge(hT_psum.sem, hT_psum.at(b + 1, 1))
                        copy(hn[:, :, :], bank(7).rearrange("p (i c) -> p i c", i=NT)).then_inc(attn_ready.sem, 1)
                    yield
                act.wait_ge(attn_ready.sem, attn_ready.at(b, 1))

            def prepare2(b):
                for step in range(STEPS["prepare2"] // 2):
                    yield
                    if step == 5:
                        act.wait_ge(h2T_psum.sem, h2T_psum.at(b, 1))
                        copy(hT[:, :], bank(5)).then_inc(h2T_ready.sem, 1)
                    if step == 6:
                        act.wait_ge(qkv2_psum.sem, qkv2_psum.at(b, 1))
                        copy(qkv2[:, :, :].rearrange("p (a i) n -> p a (i n)", a=2), ps[:, 6:8, 0:2 * 3 * L2]).then_inc(qkv2_ready.sem, 1)
                    if step == 7:
                        act.wait_ge(qkv2_ready.sem, qkv2_ready.at(b, 1))
                        copy(va2[:, :, :, 0:D2], qkv2[:, :, 2 * L2:].rearrange("p i (h d) -> p i h d", d=D2)).then_inc(va2_ready.sem, 1)
                    if step in (11, 12):
                        half = step - 11
                        act.wait_ge(q2T_psum.sem, q2T_psum.at(b, half + 1))
                        copy(q2T[:, 2 * half:2 * half + 2, :].rearrange("p g n -> p (g n)"), bank(5 + half).bitcast(BF16)).then_inc(q2T_ready.sem, 1)
                    if step in (13, 14):
                        half = step - 13
                        act.wait_ge(k2T_psum.sem, k2T_psum.at(b, half + 1))
                        act.wait_ge(k2Z_low.sem, k2Z_low.at(b, half + 1))
                        kp = bank(7 - 2 * half).bitcast(BF16).rearrange("p (g n) -> p g n", g=2)
                        for hh in range(2, 4):
                            rows = slice(RW * hh, RW * (hh + 1))
                            ins = copy(k2Z[rows, 2 * half:2 * half + 2, hh, :], kp[rows, :, :])
                        ins.then_inc(k2Z_high.sem, 1)
                    yield
                act.wait_ge(k2Z_high.sem, k2Z_high.at(b, 2))

            def attention2(b):
                for step in range(STEPS["attention2"]):
                    if step < NU2:
                        u = step
                        j = u // 4 % NT
                        act.wait_ge(st2_psum.sem, st2_psum.at(b, u + 1))
                        if u >= 6:
                            act.wait_ge(pv2_done.sem, pv2_done.at(b, (u - 6) // 4 + 1))
                        nc.scalar.activation(probs2[u % 6][:, 0:T - j * P], ps[:, u % 3, 0:T - j * P],
                                             ACT.Exp, scale=0.5).then_inc(exp2_done.sem, 1)
                    if step >= 4 * NT + 1 and (step - 1) % (4 * NT) == 0:
                        g = (step - 1) // (4 * NT) - 1
                        act.wait_ge(pv2_done.sem, pv2_done.at(b, NT * (g + 1)))
                        if g >= 2:
                            act.wait_ge(o2n_psum.sem, o2n_psum.at(b, g - 1))
                        copy(o2T[g % 2], bank(3)).then_inc(o2T_ready.sem, 1)
                    yield
                act.wait_ge(o2T_ready.sem, o2T_ready.at(b, 4))

            def after2(b):
                for step in range(STEPS["after2"]):
                    if step == 0:
                        act.wait_ge(o2nT_psum.sem, o2nT_psum.at(b, 1))
                        if in_range(b + 1):
                            act.wait_ge(mix_ready.sem, mix_ready.at(b + 1, NT))
                        copy(o2nT, bank(0)).then_inc(o2nT_ready.sem, 1)
                    if step == 2:
                        act.wait_ge(res_ready.sem, res_ready.at(b, 1))
                        for i in range(NT):
                            ins = nc.scalar.activation(t_sb[:, i, :], res[:, i, :], ACT.Square, accum_out=ms_end[:, i:i + 1])
                        ins.then_inc(res_sq.sem, 1)
                    if step == 5:
                        act.wait_ge(tT_psum.sem, tT_psum.at(b, 1))
                        copy(tT[:, :], bank(2)).then_inc(tT_ready.sem, 1)
                    if step == 9:
                        act.wait_ge(wtop_arg.sem, wtop_arg.at(b, 1))
                        nc.scalar.activation(wtop[:, 1, :], wtop[:, 0, :], ACT.Exp).then_inc(wtop_exp.sem, 1)
                    yield

            def experts(b):
                for step in range(STEPS["experts"]):
                    if step < 2 * NX and step % 2 == 0:
                        n = step // 2
                        act.wait_ge(hid_psum.sem, hid_psum.at(b, n + 1))
                        if n >= 2:
                            act.wait_ge(hid_ready.sem, hid_ready.at(b, n - 1))
                        nc.scalar.activation(th[n % 2][:, :], bank(2 * (n % FC)), ACT.Tanh, scale=0.5).then_inc(th_ready.sem, 1)
                    yield
                act.wait_ge(th_ready.sem, th_ready.at(b, NX))

            def turn(b):
                if not is_end(b) and (in_range(b) or in_range(b - 1)):
                    stages = {}
                    if in_range(b):
                        stages["attention"] = attention(b)
                    if in_range(b - 1):
                        stages["prepare2"] = prepare2(b - 1)
                    act.wait_ge(slot_done, SLOTS_ENGINES * slots_before(b, 0))
                    take(0, **stages)
                    act.sem_inc(slot_done, 1)
                stages = {}
                if in_range(b):
                    stages["mix"] = mix(b)
                if in_range(b + 1):
                    stages["prepare1"] = prepare1(b + 1)
                if in_range(b - 1):
                    stages["attention2"] = attention2(b - 1)
                    stages["after2"] = after2(b - 1)
                if not is_first(b + 1):
                    act.wait_ge(slot_done, SLOTS_ENGINES * slots_before(b, 1))
                take(1, **stages)
                act.sem_inc(slot_done, 1)
                stages = {}
                if in_range(b + 1):
                    stages["compressed"] = compressed(b + 1)
                    stages["maxima1"] = maxima1(b + 1)
                if in_range(b - 1):
                    stages["experts"] = experts(b - 1)
                if is_last(b):
                    stages["prepare2"] = prepare2(b)
                act.wait_ge(slot_done, SLOTS_ENGINES * slots_before(b, 2))
                take(3 if is_last(b) else 2, **stages)
                act.sem_inc(slot_done, 1)

            turn(-1)
            turn(0)
            if n_batch > 2:
                with act.Fori(1, n_batch - 1) as b:
                    turn(b)
            if n_batch > 1:
                turn(n_batch - 1)
            turn(n_batch)

        @block.vector
        def _(dve):
            v = nc.vector
            dve.wait_ge(loaded, 16 * N_LOADS)
            v.tensor_scalar(comp_gate[:, NBLK:NBLK + 3], comp_gate[:, NBLK:NBLK + 3], gain_col[:, :], None, ALU.mult)
            v.scalar_tensor_tensor(gain_key[:, :], gain_in[:, 0, :], D ** -0.5, gain_in[:, 1, :], ALU.mult, ALU.mult).then_inc(cast_done, 1)
            dve.wait_ge(padded, 3)

            chain = {"before": 0, "given": 0}

            def link(ins):
                chain["given"] += 1
                ins.then_inc(vector_chain, 1)
                dve.wait_ge(vector_chain, chain["before"] + chain["given"])

            def over(a, shape, axis):
                return a.unsqueeze(axis).to_broadcast(shape)

            def mean_var(src, var=var_in):
                for i in range(NT):
                    ins = v.bn_stats(stats[:, i, :], src(i))
                link(ins)
                v.memset(scrap[:, :], 0.0)
                for i in range(NT):
                    ins = v.bn_aggr(mv[:, i, :], stats[:, i, :])
                link(ins)
                return v.tensor_scalar(var[:, 0:NT], mv[:, :, 1], EPS5, None, ALU.add)

            def centred(dst, src, inverse=rstd):
                for i in range(NT):
                    ins = v.tensor_scalar(dst[:, i, :], src(i), mv[:, i, 0:1], inverse[:, i:i + 1], ALU.subtract, ALU.mult)
                return ins

            gates = gate[:, :, :].rearrange("p (i h) c -> p i h c", i=NT)
            sink_b = over(sink_sb[:, :], [P, NT, H], 1)

            def prepare1(b):
                cos1 = con("cos1").rearrange("p (i r) -> p i r", i=NT)
                sin1 = con("sin1").rearrange("p (i r) -> p i r", i=NT)
                half = ROPE // 2
                n = H + 1
                for step in range(STEPS["prepare1"] // 2):
                    yield
                    if step == 0:
                        dve.wait_ge(x_loaded.sem, x_loaded.at(b, 16))
                        mean_var(lambda i: xin[:, i, :]).then_inc(var1_ready.sem, 1)
                        dve.wait_ge(rstd1_ready.sem, rstd1_ready.at(b, 1))
                        centred(hn, lambda i: xin[:, i, :]).then_inc(h_ready.sem, 1)
                    if 3 <= step < 3 + NT:
                        i = step - 3
                        dve.wait_ge(sq_ready.sem, sq_ready.at(b, i + 1))
                        link(v.tensor_reduce(sumsq[:, i, :], sq[:, :, :], AX.X, ALU.add))
                        v.sem_inc(sq_used.sem, 1)
                        v.tensor_scalar(var_in[:, i * n:(i + 1) * n], sumsq[:, i, :], 1.0 / D, EPS6, ALU.mult, ALU.add).then_inc(var1_ready.sem, 1)
                        if i >= 1:
                            dve.wait_ge(rope_done.sem, rope_done.at(b, i))
                        part = qkv[:, i, 0:n, 0:ROPE]
                        v.tensor_tensor(ropeA[:, :, :], part, over(cos1[:, i, :], [P, n, ROPE], 1), ALU.mult)
                        link(v.tensor_tensor(ropeB[:, :, :], part, over(sin1[:, i, :], [P, n, ROPE], 1), ALU.mult))
                        v.tensor_tensor(qkv[:, i, 0:n, 0:half], ropeA[:, :, 0:half], ropeB[:, :, half:], ALU.subtract)
                        v.tensor_tensor(qkv[:, i, 0:n, half:ROPE], ropeB[:, :, 0:half], ropeA[:, :, half:], ALU.add).then_inc(rope_done.sem, 1)
                    if 5 <= step < 5 + NT:
                        i = step - 5
                        dve.wait_ge(rstd1_ready.sem, rstd1_ready.at(b, i + 2))
                        dve.wait_ge(rope_done.sem, rope_done.at(b, i + 1))
                        if i == 0 and not is_first(b):
                            dve.wait_ge(mixT_used.sem, mixT_used.at(b - 1, NT))
                        r = rstd[:, i * n:(i + 1) * n]
                        qk = qkv[:, i, 0:n, :]
                        link(v.tensor_tensor(qk, qk, over(r, [P, n, D], 2), ALU.mult))
                        v.tensor_tensor(kdup[:, i, :, :], over(qkv[:, i, H, :], [P, 2, D], 1), over(gain_key[:, :], [P, 2, D], 1), ALU.mult)
                        link(v.tensor_copy(qsplit[:, i, :, 0, :].bitcast(F32R), qkv[:, i, 0:H, :]))
                        v.tensor_tensor(qsplit[:, i, :, 1, :], qkv[:, i, 0:H, :], qsplit[:, i, :, 0, :], ALU.subtract).then_inc(split_ready.sem, 1)
                    if step == 10:
                        dve.wait_ge(kT_psum.sem, kT_psum.at(b, 1))
                        v.tensor_reduce(kmean[:, :], bank(7).rearrange("p (n r) -> p n r", r=CR), AX.X, ALU.add)
                        link(v.tensor_copy(kT_hi[:, :], bank(7)))
                        v.tensor_scalar(comp_gate[:, 0:NBLK], kmean[:, :], 1.0 / CR, None, ALU.mult)
                        v.tensor_tensor(kT_lo[:, :], bank(7), kT_hi[:, :], ALU.subtract).then_inc(k_ready.sem, 1)
                    if step == 11:
                        dve.wait_ge(vmean_psum.sem, vmean_psum.at(b, 1))
                        v.tensor_tensor(vmean[:, :, :], over(ps[:, 5, 0:D], [P, H, D], 1), over(con("head_rows"), [P, H, D], 2), ALU.mult).then_inc(vmean_ready.sem, 1)
                    yield
                dve.wait_ge(vmean_ready.sem, vmean_ready.at(b, 1))

            def compressed(b):
                yield
                yield
                dve.wait_ge(cg_ready.sem, cg_ready.at(b, 2))
                valid = con("block_valid").rearrange("p (i n) -> p i n", i=NT)
                for i in range(NT):
                    ins = v.tensor_tensor(cs[:, i, :, :], cg[:, i, :, 0:NBLK], over(valid[:, i, :], [P, H, NBLK], 1), ALU.add)
                gf = cg[:, :, :, NBLK:NBLK + 3].rearrange("p i h c -> p (i h) c")
                v.tensor_tensor(gz[:, :, :], gf, over(bgate_sb[:, :], [P, NT * H, 3], 1), ALU.add)
                link(ins)
                link(v.tensor_reduce(cmax[:, :, :], cs[:, :, :, :], AX.X, ALU.max))
                link(v.tensor_tensor(cmax[:, :, :], cmax[:, :, :], sink_b, ALU.max))
                csf = cs[:, :, :, :].rearrange("p i h n -> p (i h) n")
                cmf = cmax[:, :, :].rearrange("p i h -> p (i h)")
                v.tensor_tensor(csf, csf, over(cmf, [P, NT * H, NBLK], 2), ALU.subtract)
                v.tensor_tensor(csink[:, :, :], sink_b, cmax[:, :, :], ALU.subtract).then_inc(cexp_arg.sem, 1)
                yield
                yield
                dve.wait_ge(cexp_ready.sem, cexp_ready.at(b, 1))
                link(v.tensor_scalar(gz[:, :, :], gz[:, :, :], 1.0, None, ALU.add))
                link(v.reciprocal(gate[:, :, :], gz[:, :, :]))
                link(v.tensor_reduce(gsum[:, :], gate[:, :, :], AX.X, ALU.add))
                link(v.tensor_scalar(gsum[:, :], gsum[:, :], 1e-6, None, ALU.max))
                v.tensor_reduce(csum[:, :, :], cexp[:, :, :, :], AX.X, ALU.add)
                link(v.reciprocal(gsum[:, :], gsum[:, :]))
                link(v.tensor_tensor(gate[:, :, :], gate[:, :, :], over(gsum[:, :], [P, NT * H, 3], 2), ALU.mult))
                link(v.tensor_tensor(csum[:, :, :], csum[:, :, :], csink[:, :, :], ALU.add))
                link(v.reciprocal(ccoef[:, :, :], csum[:, :, :]))
                link(v.tensor_tensor(ccoef[:, :, :], ccoef[:, :, :], gates[:, :, :, 0], ALU.mult))
                cef = cexp[:, :, :, :].rearrange("p i h n -> p (i h) n")
                v.tensor_tensor(cef, cef, over(ccoef[:, :, :].rearrange("p i h -> p (i h)"), [P, NT * H, NBLK], 2), ALU.mult).then_inc(pc_ready.sem, 1)
                yield
                dve.wait_ge(pc_ready.sem, pc_ready.at(b, 1))

            def maxima1(b):
                for n in range(NT * H):
                    h, i = n // NT, n % NT
                    quad, hh = h // 4, h % 4
                    dve.wait_ge(s_psum.sem, s_psum.at(b, n + 1))
                    w = (i + 1) * P
                    lo = P if i == 0 else P // 2
                    v.tensor_reduce(nmax[:, quad, i, 1, hh:hh + 1], ps[:, 5 + n % 3, 0:w], AX.X, ALU.max, negate=True)
                    v.tensor_tensor_reduce(masked[:, n % 4, lo:], ps[:, 5 + n % 3, w + lo - 2 * P:w], con_bf("near_q")[:, lo:], -1.0, 3.0e38,
                                           ALU.add, ALU.min, nmax[:, quad, i, 0, hh:hh + 1]).then_inc(max_done.sem, 1)
                    yield
                dve.wait_ge(max_done.sem, max_done.at(b, NT * H))
                nm = nmax[:, :, :, :, :].rearrange("p a i k h -> p (a i k h)")
                link(v.tensor_copy(nmax_bf[:, :, 0], nm))
                link(v.tensor_tensor(nmax_bf[:, :, 1], nm, nmax_bf[:, :, 0], ALU.subtract))
                v.tensor_tensor(nm, nmax_bf[:, :, 0], nmax_bf[:, :, 1], ALU.add).then_inc(nmax_split.sem, 1)
                yield
                dve.wait_ge(shift_psum.sem, shift_psum.at(b, 1))
                v.tensor_tensor(shiftT[:, :, :], over(ps[:, 5, 0:P // 2].bitcast(BF16), [P, 4, P], 1),
                                over(con("shift_head"), [P, 4, P], 2), ALU.mult).then_inc(shift_ready.sem, 1)
                yield
                dve.wait_ge(nmax_split.sem, nmax_split.at(b, 1))

                def nk(kind, quad):
                    return nmax[:, quad, :, kind, :]
                for quad in range(2):
                    hs = slice(4 * quad, 4 * quad + 4)
                    v.tensor_tensor(cargs[:, 0, :, hs], nk(1, quad), nk(0, quad), ALU.subtract)
                    ins = v.scalar_tensor_tensor(nsink[:, :, hs], over(sink_sb[:, hs], [P, NT, 4], 1), -1.0, nk(0, quad), ALU.mult, ALU.min)
                link(ins)
                for quad in range(2):
                    hs = slice(4 * quad, 4 * quad + 4)
                    v.tensor_tensor(cargs[:, 1, :, hs], nsink[:, :, hs], nk(0, quad), ALU.subtract)
                v.tensor_tensor(cargs[:, 2, :, :], nsink[:, :, :], sink_b, ALU.add).then_inc(coef_arg.sem, 1)
                yield
                dve.wait_ge(coef_arg.sem, coef_arg.at(b, 1))

            def mix(b):
                yield
                dve.wait_ge(on_ready.sem, on_ready.at(b, 16))
                dve.wait_ge(coef_exp.sem, coef_exp.at(b, 1))
                zn, zf = on[:, 0, :, :, D], on[:, 1, :, :, D]
                v.tensor_tensor(zfull[:, :, :], cexps[:, 0, :, :], zn, ALU.mult)
                link(v.tensor_tensor(zwin[:, :, :], cexps[:, 1, :, :], zn, ALU.mult))
                v.tensor_tensor(zfull[:, :, :], zfull[:, :, :], zf, ALU.add)
                link(v.tensor_tensor(zwin[:, :, :], zwin[:, :, :], cexps[:, 2, :, :], ALU.add))
                v.reciprocal(zfull[:, :, :], zfull[:, :, :])
                link(v.reciprocal(zwin[:, :, :], zwin[:, :, :]))
                v.tensor_tensor(coef[:, 1, :, :], zfull[:, :, :], gates[:, :, :, 1], ALU.mult)
                link(v.tensor_tensor(zwin[:, :, :], zwin[:, :, :], gates[:, :, :, 2], ALU.mult))
                v.tensor_tensor(coef[:, 0, :, :], cexps[:, 0, :, :], coef[:, 1, :, :], ALU.mult)
                link(v.tensor_tensor(zwin[:, :, :], cexps[:, 1, :, :], zwin[:, :, :], ALU.mult))
                v.tensor_tensor(coef[:, 0, :, :], coef[:, 0, :, :], zwin[:, :, :], ALU.add).then_inc(coef_done.sem, 1)
                yield
                yield
                for i in range(NT):
                    dve.wait_ge(coef_done.sem, coef_done.at(b, 1))
                    if i >= 2:
                        dve.wait_ge(mixT_psum.sem, mixT_psum.at(b, i - 1))
                    m = mixa[i % 2]
                    link(v.tensor_tensor(m[:, :, :], on[:, 1, i, :, 0:D], over(coef[:, 1, i, :], [P, H, D], 2), ALU.mult))
                    dve.wait_ge(comp_psum.sem, comp_psum.at(b, i + 1))
                    link(v.tensor_tensor(m[:, :, :], m[:, :, :], bank(5).rearrange("p (h d) -> p h d", h=H), ALU.add))
                    dve.wait_ge(near_scaled.sem, near_scaled.at(b, i + 1))
                    v.tensor_tensor(m[:, :, :], m[:, :, :], mixb[i % 2][:, :, :], ALU.add).then_inc(mix_ready.sem, 1)
                    yield
                    yield
                for _ in range(5):
                    yield
                dve.wait_ge(mix_ready.sem, mix_ready.at(b, NT))

            def prepare2(b):
                yield
                ao = lambda i: hn[:, i, :]
                dve.wait_ge(attn_ready.sem, attn_ready.at(b, 1))
                mean_var(ao).then_inc(var2_ready.sem, 1)
                yield
                yield
                dve.wait_ge(rstd2_ready.sem, rstd2_ready.at(b, 1))
                link(centred(x1_of(b), ao))
                dve.wait_ge(x_again.sem, x_again.at(b, 16))
                v.tensor_tensor(x1_of(b)[:, :, :], x1_of(b)[:, :, :], xin[:, :, :], ALU.add).then_inc(x1_ready.sem, 1)
                dve.wait_ge(x1_ready.sem, x1_ready.at(b, 1))
                yield
                yield
                mean_var(lambda i: x1_of(b)[:, i, :]).then_inc(var2_ready.sem, 1)
                yield
                yield
                dve.wait_ge(rstd2_ready.sem, rstd2_ready.at(b, 2))
                link(centred(ffn_in_of(b), lambda i: x1_of(b)[:, i, :]))
                link(v.tensor_tensor(ms[:, :], rstd[:, 0:NT], rstd[:, 0:NT], ALU.mult))
                link(v.tensor_tensor(ms[:, :], ms[:, :], mv[:, :, 1], ALU.mult))
                v.tensor_scalar(var_in[:, 0:NT], ms[:, :], EPS5, None, ALU.add).then_inc(var2_ready.sem, 1)
                yield
                yield
                dve.wait_ge(rstd2_ready.sem, rstd2_ready.at(b, 3))
                for i in range(NT):
                    ins = v.scalar_tensor_tensor(hn[:, i, :], ffn_in_of(b)[:, i, :], rstd[:, i:i + 1], g1_sb[:, :], ALU.mult, ALU.mult)
                ins.then_inc(h2_ready.sem, 1)
                for _ in range(3):
                    yield
                    yield
                dve.wait_ge(qkv2_ready.sem, qkv2_ready.at(b, 1))
                cos2 = con("cos2").rearrange("p (i r) -> p i r", i=NT)
                sin2 = con("sin2").rearrange("p (i r) -> p i r", i=NT)
                pairs = qkv2[:, :, 0:2 * L2].rearrange("p i (h r c) -> p i h r c", r=2, c=2)
                for i in range(NT):
                    even, odd = pairs[:, i, :, :, 0], pairs[:, i, :, :, 1]
                    cb, sbb = over(cos2[:, i, :], [P, 2 * H2, 2], 1), over(sin2[:, i, :], [P, 2 * H2, 2], 1)
                    v.tensor_tensor(rot[0][:, i, :, :], even, cb, ALU.mult)
                    v.tensor_tensor(rot[1][:, i, :, :], odd, sbb, ALU.mult)
                    v.tensor_tensor(rot[2][:, i, :, :], even, sbb, ALU.mult)
                    ins = v.tensor_tensor(rot[3][:, i, :, :], odd, cb, ALU.mult)
                link(ins)
                yield
                yield
                for w in range(2):
                    hs = slice(w * H2, (w + 1) * H2)
                    dst = qk2[:, w, :, :].rearrange("p (i h) (r c) -> p i h r c", i=NT, r=2)
                    for i in range(NT):
                        v.tensor_tensor(dst[:, i, :, :, 0], rot[0][:, i, hs, :], rot[1][:, i, hs, :], ALU.subtract)
                        ins = v.tensor_tensor(dst[:, i, :, :, 1], rot[2][:, i, hs, :], rot[3][:, i, hs, :], ALU.add)
                link(ins)
                yield
                yield
                sl = ((0, 3, 5), (0, 1, 2))
                for lvl in range(3):
                    for w in range(2):
                        src = (qk2 if lvl == 0 else rem)[:, w, :, :]
                        ins = v.tensor_copy(parts2[:, w, :, sl[w][lvl], :], src)
                    link(ins)
                    if lvl < 2:
                        for w in range(2):
                            src = (qk2 if lvl == 0 else rem)[:, w, :, :]
                            ins = v.tensor_tensor(rem[:, w, :, :], src, parts2[:, w, :, sl[w][lvl], :], ALU.subtract)
                        link(ins)
                yield
                yield
                pq, pk = parts2[:, 0, :, :, :], parts2[:, 1, :, :, :]
                v.tensor_copy(pq[:, :, 1:3, :], over(pq[:, :, 0, :], [P, NT * H2, 2, D2], 2))
                v.tensor_copy(pq[:, :, 4, :], pq[:, :, 3, :])
                v.tensor_copy(pk[:, :, 3:5, :], pk[:, :, 0:2, :])
                v.tensor_copy(pk[:, :, 5, :], pk[:, :, 0, :]).then_inc(parts2_ready.sem, 1)
                for _ in range(3):
                    yield
                    yield
                for half in range(2):
                    if half == 1:
                        yield
                    dve.wait_ge(k2T_psum.sem, k2T_psum.at(b, half + 1))
                    kp = bank(7 - 2 * half).bitcast(BF16).rearrange("p (g n) -> p g n", g=2)
                    for hh in range(2):
                        rows = slice(RW * hh, RW * (hh + 1))
                        ins = v.tensor_copy(k2Z[rows, 2 * half:2 * half + 2, hh, :], kp[rows, :, :])
                    ins.then_inc(k2Z_low.sem, 1)
                    yield
                dve.wait_ge(k2Z_low.sem, k2Z_low.at(b, 2))

            def maxima2(b):
                for n, (g, i, hh, nh) in enumerate(UNITS_MAX2):
                    dve.wait_ge(s2_psum.sem, s2_psum.at(b, n + 1))
                    w = (i + 1) * P
                    v.tensor_reduce(nmax2[:, 4 * g + hh:4 * g + hh + nh, i], ps[:, 5 + n % 3, 0:nh * w].rearrange("p (h k) -> p h k", h=nh),
                                    AX.X, ALU.max, negate=True).then_inc(max2_done.sem, 1)
                    yield
                dve.wait_ge(max2_done.sem, max2_done.at(b, len(UNITS_MAX2)))
                nm2 = nmax2[:, :, :].rearrange("p (g m) i -> p m g i", m=4)
                link(v.tensor_copy(nmax2_bf[:, :, 0, :, :], nm2))
                v.tensor_tensor(nmax2_bf[:, :, 1, :, :], nm2, nmax2_bf[:, :, 0, :, :], ALU.subtract).then_inc(nmax2_split.sem, 1)
                yield
                yield
                dve.wait_ge(shift2_psum.sem, shift2_psum.at(b, 1))
                v.tensor_copy(shift2_sb[:, :], ps[:, 5, 0:P // 2].bitcast(BF16)).then_inc(shift2_ready.sem, 1)
                yield
                dve.wait_ge(shift2_ready.sem, shift2_ready.at(b, 1))

            def attention2(b):
                for step in range(STEPS["attention2"]):
                    if step >= 4 * NT + 3 and (step - 3) % (4 * NT) == 0:
                        g = (step - 3) // (4 * NT) - 1
                        dve.wait_ge(o2n_psum.sem, o2n_psum.at(b, g + 1))
                        nat = bank(4).rearrange("p (i h r) -> p i h r", i=NT, h=4)
                        link(v.reciprocal(rz2[:, :, :], nat[:, :, :, D2]))
                        for i in range(NT):
                            ins = v.tensor_tensor(o2n[:, i, 4 * g:4 * g + 4, :], nat[:, i, :, 0:D2], over(rz2[:, i, :], [P, 4, D2], 2), ALU.mult)
                        ins.then_inc(o2n_ready.sem, 1)
                        dve.wait_ge(o2n_ready.sem, o2n_ready.at(b, g + 1))
                    yield

            def after2(b):
                yield
                yield
                dve.wait_ge(up_psum.sem, up_psum.at(b, 1))
                v.tensor_tensor(res[:, :, :], ffn_in_of(b)[:, :, :], bank(1).rearrange("p (i c) -> p i c", i=NT), ALU.add).then_inc(res_ready.sem, 1)
                yield
                dve.wait_ge(res_sq.sem, res_sq.at(b, 1))
                v.tensor_scalar(var_end[:, :], ms_end[:, :], 1.0 / HID, EPS5, ALU.mult, ALU.add).then_inc(var3_ready.sem, 1)
                yield
                dve.wait_ge(rstd3_ready.sem, rstd3_ready.at(b, 1))
                for i in range(NT):
                    ins = v.scalar_tensor_tensor(t_sb[:, i, :], res[:, i, :], rstd_end[:, i:i + 1], g2_sb[:, :], ALU.mult, ALU.mult)
                ins.then_inc(t_ready.sem, 1)
                for _ in range(3):
                    yield
                dve.wait_ge(router_psum.sem, router_psum.at(b, 1))
                link(v.tensor_copy(logit[:, :, :], ps[:, 4, 0:NT * E].rearrange("p (i e) -> p i e", i=NT)))
                yield
                shape = [P, NT, E]
                iota = over(con("iota8"), shape, 1)
                for top, hot in ((top1, hot1), (top2, hot2)):
                    if hot is hot2:
                        yield
                    link(v.tensor_reduce(top[:, :], logit[:, :, :], AX.X, ALU.max))
                    link(v.tensor_tensor(pick[:, :, :], logit[:, :, :], over(top[:, :], shape, 2), ALU.is_lt))
                    link(v.scalar_tensor_tensor(pick[:, :, :], pick[:, :, :], float(E), iota, ALU.mult, ALU.add))
                    link(v.tensor_reduce(ms_end[:, :], pick[:, :, :], AX.X, ALU.min))
                    link(v.tensor_tensor(hot[:, :, :], iota, over(ms_end[:, :], shape, 2), ALU.is_equal))
                    if hot is hot1:
                        link(v.scalar_tensor_tensor(logit[:, :, :], hot[:, :, :], -3.0e38, logit[:, :, :], ALU.mult, ALU.add))
                v.tensor_tensor(wtop[:, 0, :], top2[:, :], top1[:, :], ALU.subtract).then_inc(wtop_arg.sem, 1)
                yield
                dve.wait_ge(wtop_exp.sem, wtop_exp.at(b, 1))
                link(v.tensor_scalar(top1[:, :], wtop[:, 1, :], 1.0, 2.0, ALU.add, ALU.mult))
                link(v.reciprocal(top1[:, :], top1[:, :]))
                link(v.tensor_tensor(top2[:, :], top1[:, :], wtop[:, 1, :], ALU.mult))
                v.tensor_tensor(hot1[:, :, :], hot1[:, :, :], over(top1[:, :], shape, 2), ALU.mult)
                link(v.tensor_tensor(hot2[:, :, :], hot2[:, :, :], over(top2[:, :], shape, 2), ALU.mult))
                link(v.tensor_tensor(egate[:, :, :], hot1[:, :, :], hot2[:, :, :], ALU.add))
                yield

            def experts(b):
                for step in range(STEPS["experts"]):
                    if step < 2 * NX and step % 2 == 1:
                        n = step // 2
                        e, c = n // FC, n % FC
                        dve.wait_ge(th_ready.sem, th_ready.at(b, n + 1))
                        if c == 0 and e >= 2:
                            dve.wait_ge(y_psum.sem, y_psum.at(b, e - 1))
                        link(v.scalar_tensor_tensor(th[n % 2], th[n % 2], 1.0, bank(2 * c), ALU.add, ALU.mult))
                        v.tensor_tensor(hid[e % 2][:, c, :], th[n % 2][:, :], bank(2 * c + 1), ALU.mult).then_inc(hid_ready.sem, 1)
                    if step >= 8 and step % 4 == 0 and step // 4 - 2 < E:
                        e = step // 4 - 2
                        dve.wait_ge(y_psum.sem, y_psum.at(b, e + 1))
                        if e == 0 and not is_first(b):
                            dve.wait_ge(out_stored.sem, out_stored.at(b - 1, 16) + 1)
                        if e >= 2:
                            dve.wait_ge(acc_done.sem, acc_done.at(b, e - 1))
                        v.tensor_tensor(yg[e % 2][:, :, :], bank(4).rearrange("p (i c) -> p i c", i=NT),
                                        over(egate[:, :, e], [P, NT, HID], 2), ALU.mult).then_inc(yg_ready.sem, 1)
                    yield
                dve.wait_ge(yg_ready.sem, yg_ready.at(b, E))

            def finish(b):
                dve.wait_ge(acc_done.sem, acc_done.at(b, E))
                mean_var(lambda i: acc[:, i, :], var_end).then_inc(var3_ready.sem, 1)
                dve.wait_ge(rstd3_ready.sem, rstd3_ready.at(b, 2))
                link(centred(acc, lambda i: acc[:, i, :], rstd_end))
                v.tensor_tensor(yout[:, :, :], acc[:, :, :], x1_of(b)[:, :, :], ALU.add).then_inc(out_ready.sem, 1)
                dve.wait_ge(out_ready.sem, out_ready.at(b, 1))

            def turn(b):
                if in_range(b - 1) and not is_end(b):
                    dve.wait_ge(slot_done, SLOTS_ENGINES * slots_before(b, 0))
                    take(0, prepare2=prepare2(b - 1), maxima2=maxima2(b - 1))
                    dve.sem_inc(slot_done, 1)
                elif in_range(b):
                    dve.wait_ge(slot_done, SLOTS_ENGINES * slots_before(b, 0))
                    dve.sem_inc(slot_done, 1)
                stages = {}
                if in_range(b):
                    stages["mix"] = mix(b)
                if in_range(b + 1):
                    stages["prepare1"] = prepare1(b + 1)
                if in_range(b - 1):
                    stages["attention2"] = attention2(b - 1)
                    stages["after2"] = after2(b - 1)
                if not is_first(b + 1):
                    dve.wait_ge(slot_done, SLOTS_ENGINES * slots_before(b, 1))
                take(1, **stages)
                dve.sem_inc(slot_done, 1)
                stages = {}
                if in_range(b + 1):
                    stages["compressed"] = compressed(b + 1)
                    stages["maxima1"] = maxima1(b + 1)
                if in_range(b - 1):
                    stages["experts"] = experts(b - 1)
                if is_last(b):
                    stages["prepare2"] = prepare2(b)
                    stages["maxima2"] = maxima2(b)
                dve.wait_ge(slot_done, SLOTS_ENGINES * slots_before(b, 2))
                take(3 if is_last(b) else 2, **stages)
                dve.sem_inc(slot_done, 1)
                if in_range(b - 1):
                    finish(b - 1)

            turn(-1)
            turn(0)
            if n_batch > 2:
                before = chain["given"]
                with dve.Fori(1, n_batch - 1) as b:
                    chain["before"], chain["given"] = before + (b - 1) * VECTOR_LINKS, 0
                    turn(b)
                    assert chain["given"] == VECTOR_LINKS, chain["given"]
                chain["before"], chain["given"] = before + (n_batch - 2) * VECTOR_LINKS, 0
            if n_batch > 1:
                turn(n_batch - 1)
            turn(n_batch)

        @block.tensor
        def _(pe):
            mm, tr = nc.tensor.matmul, nc.tensor.transpose
            pe.wait_ge(loaded, 16 * N_LOADS)
            flat = ps[:, 0:2, :].rearrange("p a n -> p (a n)")
            for c in range(4):
                tr(flat[0:64, c * P:(c + 1) * P], w_og_sb[:, c, :], ident)
            tr(flat[0:L2, 4 * P:5 * P], w_down_sb[:, :], ident)
            tr(flat[0:32, 5 * P:6 * P], w_qc_sb[:, :], ident).then_inc(fold_psum, 1)
            pe.wait_ge(folded, 1)
            mm(bank(2), left_t[0:32, 5, :], w_qup_sb[:, :], start=True, stop=True)
            for c in range(4):
                mm(ps[:, 3, c * P:(c + 1) * P], left_t[:, c, :], w_out_sb[:, c // 2, :], start=True, stop=True)
            mm(ps[:, 4, 0:3 * L2], left_t[:, 4, :], w_qkv2_in[:, :, :].rearrange("p w n -> p (w n)"), start=True, stop=True).then_inc(fold_psum, 1)
            pe.wait_ge(folded, 4)
            pe.wait_ge(cast_done, 1)
            pe.wait_ge(padded, 3)

            def prepare1(b):
                for step in range(STEPS["prepare1"] // 2):
                    if step == 1:
                        pe.wait_ge(h_ready.sem, h_ready.at(b, 1))
                        for i in range(NT):
                            ins = tr(ps[:, 4, i * P:(i + 1) * P], hn[:, i, :], ident)
                        ins.then_inc(hT_psum.sem, 1)
                    if step == 2:
                        pe.wait_ge(hT_ready.sem, hT_ready.at(b, 1))
                        if not is_first(b):
                            pe.wait_ge(attn_ready.sem, attn_ready.at(b - 1, 1))
                        for i in range(NT):
                            ins = mm(ps[:, 7, i * 2 * D:(i + 1) * 2 * D], hT[:, i * P:(i + 1) * P], w_proj[:, H * D:], start=True, stop=True)
                        ins.then_inc(kv_psum.sem, 1)
                    if 2 <= step < 2 + NT:
                        i = step - 2
                        if i >= 2:
                            pe.wait_ge(qkv_ready.sem, qkv_ready.at(b, i - 1))
                        mm(bank(5 + i % 2), hT[:, i * P:(i + 1) * P], w_proj[:, 0:H * D], start=True, stop=True).then_inc(qkv_psum.sem, 1)
                    if 6 <= step < 6 + NT:
                        i = step - 6
                        pe.wait_ge(split_ready.sem, split_ready.at(b, i + 1))
                        for quad in range(2):
                            if i >= 1:
                                pe.wait_ge(qT_ready.sem, qT_ready.at(b, 2 * (i - 1) + quad + 1))
                            else:
                                pe.wait_ge(qkv_ready.sem, qkv_ready.at(b, NT))
                            for h in range(4 * quad, 4 * quad + 4):
                                ins = tr(ps[:, 5 + quad, (h % 4) * P:(h % 4 + 1) * P],
                                         qsplit[:, i, h, :, :].rearrange("p s d -> p (s d)"), ident)
                            ins.then_inc(qT_psum.sem, 1)
                        if i == NT - 1:
                            for n in range(NT):
                                ins = tr(ps[:, 7, n * P:(n + 1) * P], kdup[:, n, :, :].rearrange("p s d -> p (s d)"), ident)
                            ins.then_inc(kT_psum.sem, 1)
                    if step == 10:
                        pe.wait_ge(v_ready.sem, v_ready.at(b, 1))
                        pe.wait_ge(qT_ready.sem, qT_ready.at(b, 2 * NT))
                        rows = con("mean_rows").rearrange("p (i r) -> p i r", i=NT)
                        for i in range(NT):
                            ins = mm(ps[:, 5, 0:D], rows[:, i, :], va[:, i, 0:D], start=i == 0, stop=i == NT - 1)
                        ins.then_inc(vmean_psum.sem, 1)
                    yield
                    yield
                pe.wait_ge(vmean_psum.sem, vmean_psum.at(b, 1))

            def compressed(b):
                for step in range(STEPS["compressed"]):
                    if step == 0:
                        pe.wait_ge(k_ready.sem, k_ready.at(b, 1))
                        for h in range(H):
                            r0 = RW * (h % 4)
                            ins = mm(ps[r0:r0 + RW, 6 - h // 4, :], comp_gate[:, :], qT[:, h, :, :].rearrange("p i n -> p (i n)").bitcast(F32), start=True, stop=True)
                            if h % 4 == 3:
                                ins.then_inc(cgT_psum.sem, 1)
                    if step == 1:
                        for quad in range(2):
                            pe.wait_ge(cgT_ready.sem, cgT_ready.at(b, quad + 1))
                            for i in range(NT):
                                ins = tr(ps[:, 7 - quad, i * P:(i + 1) * P], cgT[:, quad, i * P:(i + 1) * P], ident)
                            ins.then_inc(cg_psum.sem, 1)
                    yield
                pe.wait_ge(cg_psum.sem, cg_psum.at(b, 2))

            def maxima1(b):
                for n in range(NT * H):
                    h, i = n // NT, n % NT
                    if n == 0:
                        pe.wait_ge(cg_ready.sem, cg_ready.at(b, 2))
                    if n >= 3:
                        pe.wait_ge(max_done.sem, max_done.at(b, n - 2))
                    w = (i + 1) * P
                    dst = ps[:, 5 + n % 3, 0:w]
                    mm(dst, qT[:, h, i, :], kT_hi[:, 0:w], start=True, stop=False)
                    mm(dst[:, w - P:], ident_bf, con_bf("causal_q"), start=False, stop=True).then_inc(s_psum.sem, 1)
                    yield
                pe.wait_ge(pc_ready.sem, pc_ready.at(b, 1))
                pe.wait_ge(max_done.sem, max_done.at(b, NT * H - 1))
                for i in range(NT):
                    ins = tr(ps[:, 7, i * P:(i + 1) * P], cexp[:, i, :, :].rearrange("p h n -> p (h n)"), ident)
                ins.then_inc(pcT_psum.sem, 1)
                yield
                pe.wait_ge(nmax_split.sem, nmax_split.at(b, 1))
                tr(ps[:, 5, 0:P // 2].bitcast(BF16), nmax_bf[:, :, :].rearrange("p n s -> p (n s)"), ident_bf).then_inc(shift_psum.sem, 1)
                yield
                yield
                pe.wait_ge(shift_psum.sem, shift_psum.at(b, 1))

            pick1 = con_bf("shift_pick").rearrange("p (n r) -> p n r", n=16)

            def scores(b, u):
                quad, i, blocks, _ = UNITS1[u]
                if u >= 2:
                    pe.wait_ge(exp_done.sem, exp_done.at(b, u - 1))
                at = 0
                for kind, j, q0, nq, mask in blocks:
                    dst = ps[:, u % 2, at:at + 4 * nq].rearrange("p (h n) -> p h n", h=4)
                    q = qT[:, 4 * quad:4 * quad + 4, i, q0:q0 + nq]
                    keys = slice(j * P, (j + 1) * P)
                    mm(dst, kT_hi[:, keys], q, start=True, stop=False)
                    mm(dst, kT_lo[:, keys], q, start=False, stop=False)
                    if mask:
                        m = con_bf(mask)
                        if m.shape[1] > nq:
                            m = m[:, q0:q0 + nq]
                        mm(dst, ident_bf, m.unsqueeze(1).to_broadcast([P, 4, nq]), start=False, stop=False)
                    ins = mm(dst, pick1[:, (quad * 4 + i) * 2 + kind, :], shiftT[:, :, q0:q0 + nq], start=False, stop=True)
                    at += 4 * nq
                ins.then_inc(st_psum.sem, 1)

            def natural(b, g, kind):
                pe.wait_ge(oT_ready.sem, oT_ready.at(b, g + 1))
                if g or kind:
                    pe.wait_ge(on_ready.sem, on_ready.at(b, 2 * g + kind))
                for hh in range(4):
                    ins = tr(ps[:, 4, hh * OW:(hh + 1) * OW], oT[g % 2][0:OW, kind, hh * P:(hh + 1) * P], ident[0:OW, 0:OW])
                ins.then_inc(on_psum.sem, 1)

            def attention(b):
                for step in range(STEPS["attention"]):
                    if step == 0:
                        scores(b, 0)
                    if step + 1 < NU1:
                        scores(b, step + 1)
                    if 1 <= step <= NU1:
                        u = step - 1
                        quad, i, blocks, place = UNITS1[u]
                        g = quad * NT + i
                        pe.wait_ge(exp_done.sem, exp_done.at(b, u + 1))
                        if place == 0 and g >= 1:
                            pe.wait_ge(oT_ready.sem, oT_ready.at(b, g))
                        at = 0
                        for kind, j, q0, nq, mask in blocks:
                            pr = probs[u % 4][:, at:at + 4 * nq].rearrange("p (h n) -> p h n", h=4)
                            at += 4 * nq
                            dst = ps[0:OW, 2 + kind, :].rearrange("p (h n) -> p h n", h=4)[:, :, q0:q0 + nq]
                            ins = mm(dst, va[:, j, :], pr, start=j == i, stop=True, skip_group_check=True)
                        ins.then_inc(pv_done.sem, 1)
                    for g in range(8):
                        for kind in range(2):
                            if step == FIRST1[g + 1] + 2 + kind:
                                natural(b, g, kind)
                    yield
                pe.wait_ge(on_psum.sem, on_psum.at(b, 16))

            def mix(b):
                for step in range(STEPS["mix"] // 2):
                    i = step - 1
                    if 0 <= i < NT:
                        if i >= 1:
                            pe.wait_ge(mix_ready.sem, mix_ready.at(b, i))
                        mm(bank(5), pcT[:, i * P:(i + 1) * P], vmean[:, :, :].rearrange("p h d -> p (h d)"), start=True, stop=True).then_inc(comp_psum.sem, 1)
                    i = step - 2
                    if 0 <= i < NT:
                        pe.wait_ge(mix_ready.sem, mix_ready.at(b, i + 1))
                        if i >= 1:
                            pe.wait_ge(mixT_ready.sem, mixT_ready.at(b, i))
                        for c in range(4):
                            ins = tr(ps[:, 6, c * P:(c + 1) * P], mixa[i % 2][:, 2 * c:2 * c + 2, :].rearrange("p h d -> p (h d)"), ident)
                        ins.then_inc(mixT_psum.sem, 1)
                    i = step - 3
                    if 0 <= i < NT:
                        pe.wait_ge(mixT_ready.sem, mixT_ready.at(b, i + 1))
                        for c in range(4):
                            ins = mm(ps[:, 7, i * P:(i + 1) * P], mixT[i % 2][:, c, :], w_fold[:, c, :], start=c == 0, stop=c == 3)
                        ins.then_inc(mixT_used.sem, 1)
                    yield
                    yield
                pe.wait_ge(mixT_used.sem, mixT_used.at(b, NT))

            def prepare2(b):
                for step in range(STEPS["prepare2"] // 2):
                    if step == 5:
                        pe.wait_ge(h2_ready.sem, h2_ready.at(b, 1))
                        for i in range(NT):
                            ins = tr(ps[:, 5, i * P:(i + 1) * P], hn[:, i, :], ident)
                        ins.then_inc(h2T_psum.sem, 1)
                    if step == 6:
                        pe.wait_ge(h2T_ready.sem, h2T_ready.at(b, 1))
                        for i in range(NT):
                            o = (i % 2) * 3 * L2
                            ins = mm(ps[:, 6 + i // 2, o:o + 3 * L2], hT[:, i * P:(i + 1) * P], w_qkv2[:, :], start=True, stop=True)
                        ins.then_inc(qkv2_psum.sem, 1)
                    if 11 <= step < 15:
                        w, half = (step - 11) // 2, (step - 11) % 2
                        pe.wait_ge(parts2_ready.sem, parts2_ready.at(b, 1))
                        pe.wait_ge(slots_filled.sem, slots_filled.at(b, 1))
                        if w == 1 and half == 1:
                            pe.wait_ge(q2T_ready.sem, q2T_ready.at(b, 1))
                        bk = (5, 6, 7, 5)[2 * w + half]
                        for g in range(2 * half, 2 * half + 2):
                            for i in range(NT):
                                src = parts2[:, w, i * H2 + 4 * g:i * H2 + 4 * g + 4, :, :].rearrange("p h s d -> p (h s d)")
                                o = ((g % 2) * NT + i) * P // 2
                                ins = tr(ps[:, bk, o:o + P // 2].bitcast(BF16), src, ident_bf)
                        ins.then_inc((k2T_psum if w else q2T_psum).sem, 1)
                    yield
                    yield
                pe.wait_ge(k2T_psum.sem, k2T_psum.at(b, 2))

            def maxima2(b):
                for n, (g, i, hh, nh) in enumerate(UNITS_MAX2):
                    if n == 0:
                        pe.wait_ge(q2T_ready.sem, q2T_ready.at(b, 2))
                        pe.wait_ge(k2Z_low.sem, k2Z_low.at(b, 2))
                        pe.wait_ge(k2Z_high.sem, k2Z_high.at(b, 2))
                    if n >= 3:
                        pe.wait_ge(max2_done.sem, max2_done.at(b, n - 2))
                    w = (i + 1) * P
                    dst = ps[:, 5 + n % 3, 0:nh * w].rearrange("p (h k) -> p h k", h=nh)
                    for m in range(nh):
                        mm(dst[:, m, :], q2T[:, g, i * P:w], k2Z[:, g, hh + m, 0:w], start=True, stop=False)
                        ins = mm(dst[:, m, w - P:], ident_bf, con_bf("causal_q"), start=False, stop=True)
                    ins.then_inc(s2_psum.sem, 1)
                    yield
                yield
                pe.wait_ge(nmax2_split.sem, nmax2_split.at(b, 1))
                tr(ps[:, 5, 0:P // 2].bitcast(BF16), nmax2_bf[:, :, :, :, :].rearrange("p m s g i -> p (m s g i)"), ident_bf).then_inc(shift2_psum.sem, 1)
                yield
                yield
                pe.wait_ge(shift2_psum.sem, shift2_psum.at(b, 1))

            def scores2(b, u):
                g, j, hh = u // (4 * NT), u // 4 % NT, u % 4
                if u >= 3:
                    pe.wait_ge(exp2_done.sem, exp2_done.at(b, u - 2))
                dst = ps[:, u % 3, 0:T - j * P]
                mm(dst, k2Z[:, g, hh, j * P:(j + 1) * P], q2T[:, g, j * P:], start=True, stop=False)
                mm(dst[:, 0:P], ident_bf, con_bf("causal_k"), start=False, stop=True).then_inc(st2_psum.sem, 1)

            def natural2(b, g):
                pe.wait_ge(o2T_ready.sem, o2T_ready.at(b, g + 1))
                if g >= 1:
                    pe.wait_ge(o2n_ready.sem, o2n_ready.at(b, g))
                elif in_range(b + 2):
                    pe.wait_ge(hT_ready.sem, hT_ready.at(b + 2, 1))
                for i in range(NT):
                    ins = tr(ps[:, 4, i * P:(i + 1) * P], o2T[g % 2][:, i * P:(i + 1) * P], ident)
                ins.then_inc(o2n_psum.sem, 1)

            def attention2(b):
                for step in range(STEPS["attention2"]):
                    if step == 0:
                        pe.wait_ge(shift2_placed.sem, shift2_placed.at(b, 16 * 8))
                        scores2(b, 0)
                        scores2(b, 1)
                    if step + 2 < NU2:
                        scores2(b, step + 2)
                    if step >= 4 and step % 4 == 0 and step <= NU2:
                        k = step // 4 - 1
                        g, j = k // NT, k % NT
                        pe.wait_ge(exp2_done.sem, exp2_done.at(b, 4 * (k + 1)))
                        if j == 0 and g >= 1:
                            pe.wait_ge(o2T_ready.sem, o2T_ready.at(b, g))
                        for hh in range(4):
                            ins = mm(ps[RW * hh:RW * (hh + 1), 3, j * P:], va2[:, j, 4 * g + hh, :], probs2[(4 * k + hh) % 6][:, 0:T - j * P],
                                     start=j == 0, stop=True, skip_group_check=True)
                        ins.then_inc(pv2_done.sem, 1)
                    if step >= 4 * NT + 2 and (step - 2) % (4 * NT) == 0:
                        natural2(b, (step - 2) // (4 * NT) - 1)
                    yield
                pe.wait_ge(o2n_psum.sem, o2n_psum.at(b, 4))

            def after2(b):
                for step in range(STEPS["after2"]):
                    if step == 0:
                        pe.wait_ge(o2n_ready.sem, o2n_ready.at(b, 4))
                        for i in range(NT):
                            ins = tr(ps[:, 0, i * P:(i + 1) * P], o2n[:, i, :, :].rearrange("p h d -> p (h d)"), ident)
                        ins.then_inc(o2nT_psum.sem, 1)
                    if step == 1:
                        pe.wait_ge(o2nT_ready.sem, o2nT_ready.at(b, 1))
                        for i in range(NT):
                            ins = mm(ps[:, 1, i * P:(i + 1) * P], o2nT[:, i * P:(i + 1) * P], w_up_sb[:, :], start=True, stop=True)
                        ins.then_inc(up_psum.sem, 1)
                    if step == 5:
                        pe.wait_ge(t_ready.sem, t_ready.at(b, 1))
                        for i in range(NT):
                            ins = tr(ps[:, 2, i * P:(i + 1) * P], t_sb[:, i, :], ident)
                        ins.then_inc(tT_psum.sem, 1)
                    if step == 6:
                        pe.wait_ge(tT_ready.sem, tT_ready.at(b, 1))
                        for i in range(NT):
                            ins = mm(ps[:, 4, i * E:(i + 1) * E], tT[:, i * P:(i + 1) * P], router_sb[:, :], start=True, stop=True)
                        ins.then_inc(router_psum.sem, 1)
                    yield

            def experts(b):
                for step in range(STEPS["experts"]):
                    if step < 2 * NX and step % 2 == 0:
                        n = step // 2
                        e, c = n // FC, n % FC
                        pe.wait_ge(tT_ready.sem, tT_ready.at(b, 1))
                        if is_first(b) and n == 0:
                            pe.wait_ge(experts_loaded, 16 * 3)
                        if n >= FC:
                            pe.wait_ge(hid_ready.sem, hid_ready.at(b, n - FC + 1))
                        for k in range(2):
                            ins = mm(bank(2 * c + k), w13_sb[:, e, k, c * P:(c + 1) * P], tT[:, :], start=True, stop=True)
                        ins.then_inc(hid_psum.sem, 1)
                    if step >= 5 and step % 2 == 1 and step < 5 + 4 * E:
                        e, part = (step - 5) // 4, (step - 5) // 2 % 2
                        if part == 0:
                            pe.wait_ge(hid_ready.sem, hid_ready.at(b, FC * (e + 1)))
                            pe.wait_ge(router_psum.sem, router_psum.at(b, 1))
                        if part == 0 and e >= 1:
                            pe.wait_ge(yg_ready.sem, yg_ready.at(b, e))
                        for i in range(NT // 2 * part, NT // 2 * (part + 1)):
                            for c in range(FC):
                                ins = mm(ps[:, 4, i * P:(i + 1) * P], hid[e % 2][:, c, i * P:(i + 1) * P], w2_sb[:, e, c, :], start=c == 0, stop=c == FC - 1)
                        if part == 1:
                            ins.then_inc(y_psum.sem, 1)
                    yield
                pe.wait_ge(y_psum.sem, y_psum.at(b, E))

            def turn(b):
                if not is_end(b) and (in_range(b) or in_range(b - 1)):
                    stages = {}
                    if in_range(b):
                        stages["attention"] = attention(b)
                    if in_range(b - 1):
                        stages["prepare2"] = prepare2(b - 1)
                        stages["maxima2"] = maxima2(b - 1)
                    pe.wait_ge(slot_done, SLOTS_ENGINES * slots_before(b, 0))
                    take(0, **stages)
                    pe.sem_inc(slot_done, 1)
                stages = {}
                if in_range(b):
                    stages["mix"] = mix(b)
                if in_range(b + 1):
                    stages["prepare1"] = prepare1(b + 1)
                if in_range(b - 1):
                    stages["attention2"] = attention2(b - 1)
                    stages["after2"] = after2(b - 1)
                if not is_first(b + 1):
                    pe.wait_ge(slot_done, SLOTS_ENGINES * slots_before(b, 1))
                take(1, **stages)
                pe.sem_inc(slot_done, 1)
                stages = {}
                if in_range(b + 1):
                    stages["compressed"] = compressed(b + 1)
                    stages["maxima1"] = maxima1(b + 1)
                if in_range(b - 1):
                    stages["experts"] = experts(b - 1)
                if is_last(b):
                    stages["prepare2"] = prepare2(b)
                    stages["maxima2"] = maxima2(b)
                pe.wait_ge(slot_done, SLOTS_ENGINES * slots_before(b, 2))
                take(3 if is_last(b) else 2, **stages)
                pe.sem_inc(slot_done, 1)

            turn(-1)
            turn(0)
            if n_batch > 2:
                with pe.Fori(1, n_batch - 1) as b:
                    turn(b)
            if n_batch > 1:
                turn(n_batch - 1)
            turn(n_batch)


N_LOADS = 25
VECTOR_LINKS = 103

_INS = ['L0_attn_h', 'L0_attn_w_qc', 'L0_attn_w_qup', 'L0_attn_w_k', 'L0_attn_w_v', 'L0_attn_g_qnorm', 'L0_attn_g_knorm',
        'L0_attn_w_gate', 'L0_attn_b_gate', 'L0_attn_sink_logit', 'L0_attn_w_out_group', 'L0_attn_w_out',
        'L0_ffn_g1', 'L0_ffn_g2', 'L0_ffn_w_down', 'L0_ffn_wq', 'L0_ffn_wk', 'L0_ffn_wv', 'L0_ffn_w_up',
        'L0_ffn_router_w', 'L0_ffn_w1', 'L0_ffn_w2', 'L0_ffn_w3']


def kernel(**inputs):
    import concourse.bacc as bacc
    from concourse.bass_utils import run_bass_kernel_spmd

    nc = bacc.Bacc("TRN2", target_bir_lowering=False, num_devices=1)
    arrays, args = {}, []
    for name in _INS:
        a = np.ascontiguousarray(inputs[name])
        arrays[f"in_{name}"] = a
        args.append(nc.dram_tensor(f"in_{name}", a.shape, mybir.dt.from_np(a.dtype), kind="ExternalInput").ap())
    arrays["shape_constants"] = CONSTS
    arrays["shape_constants_bf16"] = CONSTS_BF
    args.append(nc.dram_tensor("shape_constants", CONSTS.shape, F32, kind="ExternalInput").ap())
    args.append(nc.dram_tensor("shape_constants_bf16", CONSTS_BF.shape, BF16, kind="ExternalInput").ap())
    args.append(nc.dram_tensor("out", (B, T, HID), F32, kind="ExternalOutput").ap())
    sandwich(nc, *args)
    r = run_bass_kernel_spmd(nc, [arrays], core_ids=[0])
    return r.results[0]["out"]
```
